# Optimizing a Trainium2 kernel written in Bass

```python
import numpy as np
import jax
import jax.numpy as jnp

def _softmax(x, axis=-1):
    return jax.nn.softmax(x, axis=axis)

def _gelu(x):
    return jax.nn.gelu(x, approximate=True)

def _silu(x):
    return jax.nn.silu(x)

def _sigmoid(x):
    return jax.nn.sigmoid(x)

def _layernorm(x, axis=-1, eps=1e-05):
    m = jnp.mean(x, axis=axis, keepdims=True)
    v = jnp.var(x, axis=axis, keepdims=True)
    return (x - m) / jnp.sqrt(v + eps)

def _scatter_add(tgt, idx, src, axis=0):
    return tgt.at[idx].add(src)

def _segment_sum(src, seg, n):
    return jax.ops.segment_sum(src, seg, n)
kernel_name = 'mk_decoder_preln_d1_seqx_r4_eb4815'

def setup_inputs(seed: int=0):
    np.random.seed(seed)
    _w = jnp.asarray

    def _rec_inputs():
        import jax
        import jax.numpy as jnp
        _rk = jax.random.key(seed)
        x = 7.22e-05 + 1 * jax.random.normal(jax.random.fold_in(_rk, 1), (8, 512, 256), jnp.float32)
        _lenS = 512 - jax.random.randint(jax.random.fold_in(_rk, 7), (8,), 0, max(1, 512 // 4) + 1, jnp.int32)
        _lenS2 = 1601 - jax.random.randint(jax.random.fold_in(_rk, 8), (8,), 0, max(1, 1601 // 4) + 1, jnp.int32)
        _ctx_1024P = jax.random.normal(jax.random.fold_in(_rk, 11), (8, 16, 256), jnp.float32)
        _ctx_1024c = jax.random.dirichlet(jax.random.fold_in(_rk, 511), 0.3 * jnp.ones((16,), jnp.float32), (8, 1601))
        _ctx_1024t = jnp.einsum('bsk,bkd->bsd', _ctx_1024c, _ctx_1024P)
        _ctx_1024t = _ctx_1024t * jax.lax.rsqrt(jnp.mean(jnp.square(_ctx_1024t)) + 1e-12) * 0.953939
        ctx_1024 = 4.13588e-05 + 0.999923 * (_ctx_1024t + 0.3 * jax.random.normal(jax.random.fold_in(_rk, 611), (8, 1601, 256), jnp.float32))
        return (x, ctx_1024)
    x, ctx_1024 = _rec_inputs()

    def _L0_attn_setup():
        import jax, jax.numpy as jnp
        import numpy as np
        E = 256
        H = 16
        HD = E // H
        MAX_REL = 20
        key = jax.random.key(seed)
        ks = jax.random.split(key, 12)
        B, S = (4, 256)

        def lin_w(k):
            return jax.random.normal(k, (E, E), dtype=jnp.float32) * (1.0 / np.sqrt(E))
        return {'hidden_states': jax.random.normal(ks[0], (B, S, E), dtype=jnp.float32), 'Wq': lin_w(ks[1]), 'bq': jnp.zeros((E,), jnp.float32), 'Wk': lin_w(ks[2]), 'bk': jnp.zeros((E,), jnp.float32), 'Wv': lin_w(ks[3]), 'bv': jnp.zeros((E,), jnp.float32), 'Wo': lin_w(ks[4]), 'bo': jnp.zeros((E,), jnp.float32), 'rel_k': jax.random.uniform(ks[5], (2 * MAX_REL + 1, HD), jnp.float32, -0.24, 0.24), 'rel_v': jax.random.uniform(ks[6], (2 * MAX_REL + 1, HD), jnp.float32, -0.24, 0.24)}
    _L0_attn_all = _L0_attn_setup()
    _L0_attn_in = {k: v for k, v in _L0_attn_all.items() if k in ('Wq', 'bq', 'Wk', 'bk', 'Wv', 'bv', 'Wo', 'bo', 'rel_k', 'rel_v')}
    del _L0_attn_all

    def _L0_xattn_setup():
        import jax, jax.numpy as jnp
        import numpy as np
        DIM = 256
        HEADS = 16
        DIM_HEAD = 64
        INNER = HEADS * DIM_HEAD
        MLP = 1024
        EPS = 1e-05

        def _layernorm(x, g, b):
            mu = jnp.mean(x, axis=-1, keepdims=True)
            var = jnp.mean(jnp.square(x - mu), axis=-1, keepdims=True)
            return (x - mu) * jax.lax.rsqrt(var + EPS) * g + b

        def _l2norm(x):
            n = jnp.sqrt(jnp.sum(jnp.square(x), axis=-1, keepdims=True))
            return x / jnp.maximum(n, 1e-12)

        def _split_heads(x, B, N):
            return x.reshape(B, N, HEADS, DIM_HEAD).transpose(0, 2, 1, 3)
        key = jax.random.key(seed)
        ks = jax.random.split(key, 16)
        B, N = (4, 512)
        s = 0.02
        return {'Q': jax.random.normal(ks[0], (B, N, DIM), jnp.float32), 'K': jax.random.normal(ks[1], (B, N, DIM), jnp.float32), 'V': jax.random.normal(ks[2], (B, N, DIM), jnp.float32), 'wq': jax.random.normal(ks[3], (DIM, INNER), jnp.float32) * s, 'wk': jax.random.normal(ks[4], (DIM, INNER), jnp.float32) * s, 'wv': jax.random.normal(ks[5], (DIM, INNER), jnp.float32) * s, 'wo': jax.random.normal(ks[6], (INNER, DIM), jnp.float32) * s, 'bo': jnp.zeros((DIM,), jnp.float32), 'w1': jax.random.normal(ks[7], (DIM, MLP), jnp.float32) * s, 'b1': jnp.zeros((MLP,), jnp.float32), 'w2': jax.random.normal(ks[8], (MLP, DIM), jnp.float32) * s, 'b2': jnp.zeros((DIM,), jnp.float32), 'ln1_g': jnp.ones((DIM,), jnp.float32), 'ln1_b': jnp.zeros((DIM,), jnp.float32), 'ln2_g': jnp.ones((DIM,), jnp.float32), 'ln2_b': jnp.zeros((DIM,), jnp.float32)}
    _L0_xattn_all = _L0_xattn_setup()
    _L0_xattn_in = {k: v for k, v in _L0_xattn_all.items() if k in ('wq', 'wk', 'wv', 'wo', 'bo', 'w1', 'b1', 'w2', 'b2', 'ln1_g', 'ln1_b', 'ln2_g', 'ln2_b')}
    del _L0_xattn_all

    def _L0_ffn_setup():
        import jax, jax.numpy as jnp
        import numpy as np
        BLOCK = 16
        _GRID = jnp.array([0.0, 0.5, 1.0, 1.5, 2.0, 3.0, 4.0, 6.0], dtype=jnp.float32)
        _MID = jnp.array([0.25, 0.75, 1.25, 1.75, 2.5, 3.5, 5.0], dtype=jnp.float32)

        def fp4_quant_dequant(x):
            shape = x.shape
            xb = x.reshape(shape[:-1] + (shape[-1] // BLOCK, BLOCK))
            scale = jnp.max(jnp.abs(xb), axis=-1, keepdims=True) / 6.0
            scale = jnp.maximum(scale, jnp.float32(1e-12))
            xn = xb / scale
            idx = jnp.searchsorted(_MID, jnp.abs(xn))
            q = _GRID[idx] * jnp.sign(xn) * scale
            return q.reshape(shape)

        def fp4_linear(x, w):
            xq = fp4_quant_dequant(x)
            wq = fp4_quant_dequant(w)
            return jnp.einsum('bsk,nk->bsn', xq, wq)
        key = jax.random.key(seed)
        k1, k2, k3, k4 = jax.random.split(key, 4)
        H, I = (256, 704)
        x = jax.random.normal(k1, (4, 1024, H), dtype=jnp.float32)
        w_gate = jax.random.normal(k2, (I, H), dtype=jnp.float32) * 0.02
        w_up = jax.random.normal(k3, (I, H), dtype=jnp.float32) * 0.02
        w_down = jax.random.normal(k4, (H, I), dtype=jnp.float32) * 0.02
        return {'x': x, 'w_gate': w_gate, 'w_up': w_up, 'w_down': w_down}
    _L0_ffn_all = _L0_ffn_setup()
    _L0_ffn_in = {k: v for k, v in _L0_ffn_all.items() if k in ('w_gate', 'w_up', 'w_down')}
    del _L0_ffn_all
    return {'x': x, 'ctx_1024': ctx_1024, 'L0_attn_Wq': _L0_attn_in['Wq'], 'L0_attn_bq': _L0_attn_in['bq'], 'L0_attn_Wk': _L0_attn_in['Wk'], 'L0_attn_bk': _L0_attn_in['bk'], 'L0_attn_Wv': _L0_attn_in['Wv'], 'L0_attn_bv': _L0_attn_in['bv'], 'L0_attn_Wo': _L0_attn_in['Wo'], 'L0_attn_bo': _L0_attn_in['bo'], 'L0_attn_rel_k': _L0_attn_in['rel_k'], 'L0_attn_rel_v': _L0_attn_in['rel_v'], 'L0_xattn_wq': _L0_xattn_in['wq'], 'L0_xattn_wk': _L0_xattn_in['wk'], 'L0_xattn_wv': _L0_xattn_in['wv'], 'L0_xattn_wo': _L0_xattn_in['wo'], 'L0_xattn_bo': _L0_xattn_in['bo'], 'L0_xattn_w1': _L0_xattn_in['w1'], 'L0_xattn_b1': _L0_xattn_in['b1'], 'L0_xattn_w2': _L0_xattn_in['w2'], 'L0_xattn_b2': _L0_xattn_in['b2'], 'L0_xattn_ln1_g': _L0_xattn_in['ln1_g'], 'L0_xattn_ln1_b': _L0_xattn_in['ln1_b'], 'L0_xattn_ln2_g': _L0_xattn_in['ln2_g'], 'L0_xattn_ln2_b': _L0_xattn_in['ln2_b'], 'L0_ffn_w_gate': _L0_ffn_in['w_gate'], 'L0_ffn_w_up': _L0_ffn_in['w_up'], 'L0_ffn_w_down': _L0_ffn_in['w_down']}

def reference(x, ctx_1024, L0_attn_Wq, L0_attn_bq, L0_attn_Wk, L0_attn_bk, L0_attn_Wv, L0_attn_bv, L0_attn_Wo, L0_attn_bo, L0_attn_rel_k, L0_attn_rel_v, L0_xattn_wq, L0_xattn_wk, L0_xattn_wv, L0_xattn_wo, L0_xattn_bo, L0_xattn_w1, L0_xattn_b1, L0_xattn_w2, L0_xattn_b2, L0_xattn_ln1_g, L0_xattn_ln1_b, L0_xattn_ln2_g, L0_xattn_ln2_b, L0_ffn_w_gate, L0_ffn_w_up, L0_ffn_w_down):
    import jax
    import jax.numpy as jnp

    def _L0_attn_ref(hidden_states, Wq, bq, Wk, bk, Wv, bv, Wo, bo, rel_k, rel_v):
        import jax, jax.numpy as jnp
        import numpy as np
        E = 256
        H = 16
        HD = E // H
        MAX_REL = 20
        B, S, _ = hidden_states.shape
        scale = jnp.sqrt(jnp.float32(HD))

        def proj(W, b):
            return (hidden_states @ W.T + b).reshape(B, S, H, HD).transpose(0, 2, 1, 3)
        q = proj(Wq, bq)
        k = proj(Wk, bk)
        v = proj(Wv, bv)
        pos = jnp.arange(S)
        idx = jnp.clip(pos[None, :] - pos[:, None], -MAX_REL, MAX_REL) + MAX_REL
        rk2 = rel_k[idx]
        rv2 = rel_v[idx]
        attn1 = jnp.einsum('bhqd,bhkd->bhqk', q, k)
        attn2 = jnp.einsum('bhqd,qkd->bhqk', q, rk2)
        attn = jax.nn.softmax((attn1 + attn2) / scale, axis=-1)
        w1 = jnp.einsum('bhqk,bhkd->bhqd', attn, v)
        w2 = jnp.einsum('bhqk,qkd->bhqd', attn, rv2)
        x = (w1 + w2).transpose(0, 2, 1, 3).reshape(B, S, E)
        out = x @ Wo.T + bo
        return out

    def _L0_xattn_ref(Q, K, V, wq, wk, wv, wo, bo, w1, b1, w2, b2, ln1_g, ln1_b, ln2_g, ln2_b):
        import jax, jax.numpy as jnp
        import numpy as np
        DIM = 256
        HEADS = 16
        DIM_HEAD = 64
        INNER = HEADS * DIM_HEAD
        MLP = 1024
        EPS = 1e-05

        def _layernorm(x, g, b):
            mu = jnp.mean(x, axis=-1, keepdims=True)
            var = jnp.mean(jnp.square(x - mu), axis=-1, keepdims=True)
            return (x - mu) * jax.lax.rsqrt(var + EPS) * g + b

        def _l2norm(x):
            n = jnp.sqrt(jnp.sum(jnp.square(x), axis=-1, keepdims=True))
            return x / jnp.maximum(n, 1e-12)

        def _split_heads(x, B, N):
            return x.reshape(B, N, HEADS, DIM_HEAD).transpose(0, 2, 1, 3)
        B, Nq, _ = Q.shape
        Nk = K.shape[1]
        Qn = _layernorm(Q, ln1_g, ln1_b)
        Kn = _layernorm(K, ln1_g, ln1_b)
        Vn = _layernorm(V, ln1_g, ln1_b)
        q = _split_heads(Qn @ wq, B, Nq)
        k = _split_heads(Kn @ wk, B, Nk)
        v = _split_heads(Vn @ wv, B, Nk)
        qn = _l2norm(q)
        kn = _l2norm(k)
        attn = jnp.einsum('bhqd,bhkd->bhqk', qn, kn)
        out = jnp.einsum('bhqk,bhkd->bhqd', attn, v)
        out = out.transpose(0, 2, 1, 3).reshape(B, Nq, INNER)
        x = Q + out @ wo + bo
        xn = _layernorm(x, ln2_g, ln2_b)
        h = jax.nn.gelu(xn @ w1 + b1, approximate=False)
        return x + h @ w2 + b2

    def _L0_ffn_ref(x, w_gate, w_up, w_down):
        import jax, jax.numpy as jnp
        import numpy as np
        BLOCK = 16
        _GRID = jnp.array([0.0, 0.5, 1.0, 1.5, 2.0, 3.0, 4.0, 6.0], dtype=jnp.float32)
        _MID = jnp.array([0.25, 0.75, 1.25, 1.75, 2.5, 3.5, 5.0], dtype=jnp.float32)

        def fp4_quant_dequant(x):
            shape = x.shape
            xb = x.reshape(shape[:-1] + (shape[-1] // BLOCK, BLOCK))
            scale = jnp.max(jnp.abs(xb), axis=-1, keepdims=True) / 6.0
            scale = jnp.maximum(scale, jnp.float32(1e-12))
            xn = xb / scale
            idx = jnp.searchsorted(_MID, jnp.abs(xn))
            q = _GRID[idx] * jnp.sign(xn) * scale
            return q.reshape(shape)

        def fp4_linear(x, w):
            xq = fp4_quant_dequant(x)
            wq = fp4_quant_dequant(w)
            return jnp.einsum('bsk,nk->bsn', xq, wq)
        gate = fp4_linear(x, w_gate)
        y = fp4_linear(x, w_up)
        h = jax.nn.silu(gate) * y
        return fp4_linear(h, w_down)
    x = x + _L0_attn_ref(_layernorm(x, axis=-1), L0_attn_Wq, L0_attn_bq, L0_attn_Wk, L0_attn_bk, L0_attn_Wv, L0_attn_bv, L0_attn_Wo, L0_attn_bo, L0_attn_rel_k, L0_attn_rel_v)
    x = x + _L0_xattn_ref(_layernorm(x, axis=-1), ctx_1024, ctx_1024, L0_xattn_wq, L0_xattn_wk, L0_xattn_wv, L0_xattn_wo, L0_xattn_bo, L0_xattn_w1, L0_xattn_b1, L0_xattn_w2, L0_xattn_b2, L0_xattn_ln1_g, L0_xattn_ln1_b, L0_xattn_ln2_g, L0_xattn_ln2_b)
    x = x + _L0_ffn_ref(_layernorm(x, axis=-1), L0_ffn_w_gate, L0_ffn_w_up, L0_ffn_w_down)
    return x

_drawn_inputs = setup_inputs


def setup_inputs(seed=0):
    import zlib

    import numpy as np

    out = dict(_drawn_inputs(seed))
    spreads = {'L0_attn_bq': (0.0, 0.8),
     'L0_attn_bk': (0.0, 0.8),
     'L0_attn_bv': (0.0, 0.1),
     'L0_attn_bo': (0.0, 0.1),
     'L0_xattn_bo': (0.0, 0.8),
     'L0_xattn_b1': (0.0, 0.8),
     'L0_xattn_b2': (0.0, 0.8),
     'L0_xattn_ln1_g': (1.0, 0.2),
     'L0_xattn_ln1_b': (0.0, 0.1),
     'L0_xattn_ln2_g': (1.0, 0.6),
     'L0_xattn_ln2_b': (0.0, 0.8)}
    factors = {'L0_attn_rel_k': 5.003,
     'L0_xattn_w1': 7.086,
     'L0_xattn_w2': 6.595,
     'L0_ffn_w_gate': 8.0,
     'L0_ffn_w_up': 8.0,
     'L0_ffn_w_down': 8.0}
    for name, (base, spread) in spreads.items():
        noise = np.random.default_rng([zlib.crc32(name.encode()), seed]).standard_normal(out[name].shape)
        drawn = base * np.exp(spread * noise) if base else spread * noise
        out[name] = jnp.asarray(drawn.astype(out[name].dtype))
    for name, factor in factors.items():
        out[name] = (out[name] * factor).astype(out[name].dtype)
    return out
```

```python
import numpy as np

NB, S, E, H, HD = 8, 512, 256, 16, 16
T = S // 128
MAX_REL = 20
BAND = 2 * MAX_REL
NREL = BAND + 1
PAD = MAX_REL
ROW = PAD + S + PAD
WIN = 128 + BAND
SKEW = WIN + 1
REGION = 128 * SKEW
CTX = 1601
CT = (CTX + 127) // 128
CLAST = CTX - (CT - 1) * 128
XH, XD = 16, 64
INNER = XH * XD
NM = INNER // 128
MLP = 1024
NF = MLP // 128
FF = 704
NFF = (FF + 127) // 128
FLAST = FF - (NFF - 1) * 128
QB = 16
EPS = 1e-5
HG = 4
NG = H // HG
GR = 88
NGR = FF // GR
BIG = 3.0e38
ARENA = 25200
TAB0 = HG * NREL + 5 * 64 + 3 * E
START_MEMSETS = 3
OWN = {"dve_start": 110, "dve_prep": 8, "dve_norm": 2, "dve_scale": 1, "dve_attn": 9, "dve_tail": 124,
       "pool_start": 10, "pool_affine": 1, "pool_fill": 1, "pool_tail": 20}


def build(nc, bass, mybir, d, out):
    from contextlib import ExitStack
    f32, bf16 = mybir.dt.float32, mybir.dt.bfloat16
    ALU, ACT, AX = mybir.AluOpType, mybir.ActivationFunctionType, mybir.AxisListType
    ds = bass.ds
    ctx = ExitStack()
    with ctx:
        def sb(name, shape, dt=f32):
            return ctx.enter_context(nc.sbuf_tensor(name, shape, dt))

        starts = []

        def sem(name, start=1):
            made = ctx.enter_context(nc.semaphore(name))
            starts.append((made, start))
            return made

        wq_s, wk_s = sb("wq_s", [128, 2, 512]), sb("wk_s", [128, 2, 512])
        wv_s, wo_s = sb("wv_s", [128, 2, E]), sb("wo_s", [128, 2, E])
        cwq, cwk, cwv = sb("cwq", [128, 2, INNER]), sb("cwk", [128, 2, INNER]), sb("cwv", [128, 2, INNER])
        cwo, w1, w2 = sb("cwo", [128, NM, E]), sb("w1", [128, 2, MLP]), sb("w2", [128, NF, E])
        rows = sb("rows", [128, 9, E])
        V_BV, V_BO, V_G1, V_B1, V_XBO, V_G2, V_B2, V_XB2, V_EDGE = range(9)
        cols = sb("cols", [128, 16])
        ident = sb("ident", [128, 128])
        right_mask = sb("right_mask", [128, 384 + S], bf16)
        mass_mask = sb("mass_mask", [128, 128])
        pair_mask = sb("pair_mask", [128, 128])
        bdk, bdv, bdr = sb("bdk", [128, HG * NREL]), sb("bdv", [128, 5, 64]), sb("bdr", [16, E])
        wgT, wuT, wdT = sb("wgT", [128, 2, FF]), sb("wuT", [128, 2, FF]), sb("wdT", [128, NFF, E])
        zeros = sb("zeros", [128, 512], bf16)
        xin = sb("xin", [128, T, E])
        M = sb("M", [128, NM, E])
        edge = sb("edge", [128, T, H])
        lsum, rl, mass = sb("lsum", [128, T, H]), sb("rl", [128, T, H]), sb("mass", [128, T, H])
        bnst, mv, rstd = sb("bnst", [128, T, 6]), sb("mv", [128, T, 2]), sb("rstd", [128, T])
        mhalf = sb("mhalf", [128, 16])
        ss, rn = sb("ss", [128, 2, 16]), sb("rn", [128, 2, 16])
        am, qsc, qrc, qhs = (sb(n, [128, 2, FF // QB]) for n in ("am", "qsc", "qrc", "qhs"))
        nmax = sb("nmax", [128, HG])
        arena = sb("arena", [128, ARENA])
        used = [0]

        def carve(n, shape, at=None):
            lo = used[0] if at is None else at
            used[0] = lo + n
            assert used[0] <= ARENA, used[0]
            v = arena[:, lo:lo + n]
            if len(shape) == 2:
                return v.rearrange("p (a b) -> p a b", a=shape[0])
            if len(shape) == 3:
                return v.rearrange("p (a b c) -> p a b c", a=shape[0], b=shape[1])
            return v

        KT, QT = carve(2048, (4, 512), 0), carve(2048, (4, 512))
        QS = carve(512, (4, 128))
        Vsel = carve(4096, (T, T, E))
        Rb = carve(T * H * NREL, (T, H, NREL), used[0])
        Pband = carve(T * H * BAND, (T, H, BAND), used[0] - T * H * NREL)
        used[0] += T * H
        xn = carve(1024, (T, E))
        Oraw = xn
        only_attn = used[0]
        Bt = carve(2 * HG * ROW, (2 * HG, ROW))
        Wn = carve(2 * HG * WIN, (2 * HG, WIN))
        P = carve(2 * HG * ROW, (2 * HG, ROW))
        Sb = carve(2 * S, (2, S))
        PTs = carve(2 * 512, (2, 512))
        prod = carve(HG * 128, (HG, 128))
        AT = carve(2 * 640, (2, 5, 128), only_attn)
        massT = carve(2 * 128, (2, 128))
        aT = carve(2 * 256, (2, 2, 128))
        xnT = carve(1024, (2, 512), only_attn)
        cin, Kn = carve(512, (2, E)), carve(1024, (4, E))
        cnT = carve(512, (2, 2, 128))
        csq = carve(1024, (1024,))
        kns_at = used[0]
        kns = carve(4096, (4, INNER))
        Gs = carve(2048, (NM, E))
        GT = carve(2048, (2, NM, 128), kns_at)
        KVT = carve(1024, (NM, 128))
        Qx, Qn, QnT = carve(1024, (T, E), 0), carve(1024, (T, E)), carve(1024, (2, 512))
        sq = carve(1024, (1024,))
        qn, qnT = carve(2048, (2, INNER)), carve(1024, (NM, 128))
        y, yr = carve(1024, (T, E)), carve(1024, (T, E))
        yn, ynT = Qn, QnT
        hT = carve(4096, (NF, 512))
        x2 = carve(1024, (T, E))
        zf = Qx
        qv, qa, qs, qc, qh = (carve(2 * FF, (2, FF)) for _ in range(5))
        xq, xqT = carve(1024, (T, E)), carve(1024, (2, 512))
        hqT = carve(2 * NFF * 128, (2, NFF, 128), 4096)
        yout = hT[:, 0:2, :].rearrange("p a (b c) -> p (a b) c", b=2)
        gs, hq = carve(2 * FF, (2, FF), 9216 + 1024), carve(2 * FF, (2, FF))

        raw_wg = carve(NGR * E, (NGR, E), H * SKEW)
        raw_wu = carve(NGR * E, (NGR, E))
        raw_wd = carve(2 * FF, (2, FF))
        qw = carve(2 * FF, (2, FF))
        rel0 = carve(TAB0, (TAB0,))
        mask32 = carve(384 + S, (384 + S,))

        PS = ctx.enter_context(nc.psum_tensor("PS", [128, 8 * 512], f32))

        def bank(i, lo=0, hi=512, parts=128):
            return PS[0:parts, i * 512 + lo:i * 512 + hi]

        bias_scr, prob_scr = d["bias_scr"], d["prob_scr"]

        waits_alone = sem("waits_alone")
        consts_loaded = sem("consts_loaded")
        attn_w_loaded = sem("attn_w_loaded")
        ctx_w_loaded = sem("ctx_w_loaded")
        ffn_w_loaded = sem("ffn_w_loaded")
        zeros_stored = sem("zeros_stored")
        setup_pool = sem("setup_pool")
        tables_ready = sem("tables_ready")
        dve_start = sem("dve_start")
        dve_prep = sem("dve_prep")
        dve_norm = sem("dve_norm")
        dve_scale = sem("dve_scale")
        dve_attn = sem("dve_attn")
        dve_tail = sem("dve_tail")
        pool_start = sem("pool_start")
        pool_affine = sem("pool_affine")
        pool_fill = sem("pool_fill")
        pool_tail = sem("pool_tail")
        x_var = sem("x_var")
        x_rstd = sem("x_rstd")
        c_var = sem("c_var")
        c_rstd = sem("c_rstd")
        c_norm = sem("c_norm")
        c_rnorm = sem("c_rnorm")
        t_var = sem("t_var")
        t_rstd = sem("t_rstd")
        q_norm = sem("q_norm")
        q_rnorm = sem("q_rnorm")
        x_loaded = sem("x_loaded")
        xn_ready = sem("xn_ready")
        xnT_psum = sem("xnT_psum")
        xnT_ready = sem("xnT_ready")
        k_psum = sem("k_psum")
        kT_ready = sem("kT_ready")
        q_psum = sem("q_psum")
        qT_ready = sem("qT_ready")
        v_psum = sem("v_psum")
        v_ready = sem("v_ready")
        vsel_ready = sem("vsel_ready")
        r_psum = sem("r_psum")
        r_act = sem("r_act")
        r_dve = sem("r_dve")
        e_ready = sem("e_ready")
        xb_ready = sem("xb_ready")
        bias_stored = sem("bias_stored")
        ctx_loaded = [sem("ctx_loaded0"), sem("ctx_loaded1")]
        cz_ready = sem("cz_ready", 5)
        caff_ready = sem("caff_ready", 5)
        ct_psum = sem("ct_psum", 5)
        ct_ready = sem("ct_ready", 5)
        ck_psum = sem("ck_psum", 5)
        kc_ready = sem("kc_ready", 5)
        csq_ready = sem("csq_ready", 5)
        cs_ready = sem("cs_ready", 5)
        cg_done = sem("cg_done", 5)
        g_act = sem("g_act")
        g_dve = sem("g_dve")
        gt_psum = sem("gt_psum")
        gt_act = sem("gt_act")
        gt_dve = sem("gt_dve")
        kvt_psum = sem("kvt_psum")
        kvt_ready = sem("kvt_ready")
        m_psum = sem("m_psum")
        m_act = sem("m_act")
        m_dve = sem("m_dve")
        qs_ready = sem("qs_ready")
        scores_ready = sem("scores_ready")
        scores_biased = sem("scores_biased", 5)
        bias_filled = sem("bias_filled", 3)
        win_loaded = [sem("win_loaded0"), sem("win_loaded1")]
        probs_ready = sem("probs_ready", 5)
        p_stored = [sem("p_stored0"), sem("p_stored1")]
        transposed = sem("transposed", 5)
        pt_copied = [sem("pt_act"), sem("pt_dve")]
        pv_done = sem("pv_done", 3)
        o_evac = sem("o_evac")
        mass_mul = sem("mass_mul", 3)
        mass_red = sem("mass_red")
        band_loaded = sem("band_loaded")
        fa_psum = sem("fa_psum")
        fa_act = sem("fa_act")
        fa_dve = sem("fa_dve")
        f_psum = sem("f_psum")
        attn_ready = sem("attn_ready")
        at_psum = sem("at_psum")
        aT_ready = sem("aT_ready")
        wo_psum = sem("wo_psum")
        x1_ready = sem("x1_ready")
        rl_ready = sem("rl_ready")
        qx_ready = sem("qx_ready")
        qz_ready = sem("qz_ready")
        qaff_ready = sem("qaff_ready")
        qnT_psum = sem("qnT_psum")
        qnT_ready = sem("qnT_ready")
        xq_psum = sem("xq_psum")
        sq_ready = sem("sq_ready")
        qn_ready = sem("qn_ready")
        qt_psum = sem("qt_psum")
        qt_act = sem("qt_act")
        qt_dve = sem("qt_dve")
        o_psum = sem("o_psum")
        y_res = sem("y_res")
        y_ready = sem("y_ready")
        yz_ready = sem("yz_ready")
        yaff_ready = sem("yaff_ready")
        ynT_psum = sem("ynT_psum")
        ynT_ready = sem("ynT_ready")
        h_psum = sem("h_psum")
        h_ready = sem("h_ready")
        y2_res = sem("y2_res")
        m2_psum = sem("m2_psum")
        x2_ready = sem("x2_ready")
        zf_ready = sem("zf_ready")
        quant_scaled = sem("quant_scaled")
        quant_v = sem("quant_v")
        quant_a = sem("quant_a")
        quant_c = sem("quant_c")
        quant_out = sem("quant_out", 3)
        qwT_psum = sem("qwT_psum")
        qwT_ready = sem("qwT_ready")
        xqT_psum = sem("xqT_psum")
        xqT_ready = sem("xqT_ready")
        gu_psum = sem("gu_psum")
        silu_ready = sem("silu_ready")
        hh_ready = sem("hh_ready")
        ht_psum = sem("ht_psum")
        ht_act = sem("ht_act")
        ht_dve = sem("ht_dve")
        dn_psum = sem("dn_psum")
        out_ready = sem("out_ready")
        out_stored = sem("out_stored")

        class Steps:
            def __init__(self, which, name, turn=0):
                self.sem, self.name, self.n, self.base = which, name, 0, turn * OWN[name]

            def __call__(self, ins):
                self.n += 1
                return ins.then_inc(self.sem, 1)

            def all(self):
                return self.base + self.n + 1

            def close(self):
                assert self.n == OWN[self.name], (self.name, self.n)

        def bcast(v, n):
            return v.unsqueeze(2).broadcast_to([v.shape[0], v.shape[1], n])

        def root(pool, x, start, done, n):
            pool.wait_ge(start, n + 1)
            pool.sem_inc(waits_alone, 1)
            pool.tensor_tensor(x, x, mhalf[0:x.shape[0], 0:x.shape[1]], ALU.pow).then_inc(done, 1)

        def layernorm(eng, st, srcs, outs, done, var, inv, turn, parts=128):
            n = len(srcs)
            for i, x in enumerate(srcs):
                st(eng.bn_stats(bnst[0:parts, i, :], x))
            eng.wait_ge(st.sem, st.all())
            eng.sem_inc(waits_alone, 1)
            for i in range(n):
                st(eng.bn_aggr(mv[0:parts, i, :], bnst[0:parts, i, :]))
            eng.wait_ge(st.sem, st.all())
            eng.tensor_scalar(rstd[0:parts, 0:n], mv[0:parts, 0:n, 1], EPS, None, ALU.add).then_inc(var, 1)
            eng.wait_ge(inv, turn + 1)
            for i, x in enumerate(srcs):
                eng.tensor_scalar(outs[i], x, mv[0:parts, i, 0:1], rstd[0:parts, i:i + 1],
                                  ALU.subtract, ALU.mult).then_inc(done, 1)

        def quant_scale(eng, st, X, p, parts, n, k):
            nb = n // QB
            eng.wait_ge(quant_out, k + 2)
            st(eng.tensor_reduce(am[0:parts, p, 0:nb], X.rearrange("p (b c) -> p b c", c=QB), AX.X, ALU.max,
                                 apply_absolute_value=True))
            eng.wait_ge(st.sem, st.all())
            st(eng.tensor_scalar(qsc[0:parts, p, 0:nb], am[0:parts, p, 0:nb], 1.0 / 6.0, 1e-12, ALU.mult, ALU.max))
            eng.wait_ge(st.sem, st.all())
            st(eng.tensor_scalar(qhs[0:parts, p, 0:nb], qsc[0:parts, p, 0:nb], 0.5, None, ALU.mult))
            st(eng.reciprocal(qrc[0:parts, p, 0:nb], qsc[0:parts, p, 0:nb]))
            eng.wait_ge(st.sem, st.all())
            eng.tensor_tensor(qv[0:parts, p, 0:n].rearrange("p (b c) -> p b c", c=QB),
                              X.rearrange("p (b c) -> p b c", c=QB), bcast(qrc[0:parts, p, 0:nb], QB),
                              ALU.mult).then_inc(quant_v, 1)

        def quant_abs(eng, p, parts, n, k):
            eng.wait_ge(quant_v, k + 2)
            eng.activation(qa[0:parts, p, 0:n], qv[0:parts, p, 0:n], ACT.Abs).then_inc(quant_a, 1)
            eng.activation(qs[0:parts, p, 0:n], qv[0:parts, p, 0:n], ACT.Sign).then_inc(quant_a, 1)

        def quant_count(eng, st, p, parts, n, k):
            a, c, t = qa[0:parts, p, 0:n], qc[0:parts, p, 0:n], qv[0:parts, p, 0:n]
            eng.wait_ge(quant_a, 2 * k + 3)
            st(eng.tensor_scalar(c, a, 5.0, 2.0, ALU.is_gt, ALU.mult))
            st(eng.tensor_scalar(t, a, 0.25, None, ALU.is_gt))
            eng.wait_ge(st.sem, st.all())
            for m in (3.5, 2.5):
                st(eng.scalar_tensor_tensor(c, a, m, c, ALU.is_gt, ALU.add))
                eng.wait_ge(st.sem, st.all())
            st(eng.scalar_tensor_tensor(c, c, 2.0, t, ALU.mult, ALU.add))
            eng.wait_ge(st.sem, st.all())
            for m in (1.75, 1.25):
                st(eng.scalar_tensor_tensor(c, a, m, c, ALU.is_gt, ALU.add))
                eng.wait_ge(st.sem, st.all())
            eng.scalar_tensor_tensor(c, a, 0.75, c, ALU.is_gt, ALU.add).then_inc(quant_c, 1)

        def quant_finish(eng, st, X, p, parts, n, k):
            nb = n // QB
            eng.wait_ge(quant_a, 2 * k + 3)
            st(eng.tensor_tensor(qh[0:parts, p, 0:n].rearrange("p (b c) -> p b c", c=QB),
                                 qs[0:parts, p, 0:n].rearrange("p (b c) -> p b c", c=QB),
                                 bcast(qhs[0:parts, p, 0:nb], QB), ALU.mult))
            eng.wait_ge(quant_c, k + 2)
            eng.wait_ge(st.sem, st.all())
            eng.tensor_tensor(X, qc[0:parts, p, 0:n], qh[0:parts, p, 0:n], ALU.mult).then_inc(quant_out, 1)

        wjobs = [("g", GR, 2 * E, i) for i in range(NGR // 2)] + [("u", GR, 2 * E, i) for i in range(NGR // 2)] \
            + [("d", 128, FF, i) for i in range(2)]
        NQ0 = len(wjobs)
        QPB = 2 * T

        def wsrc(kind, i):
            if kind == "d":
                return raw_wd[:, i, :]
            return (raw_wg if kind == "g" else raw_wu)[0:GR, 2 * i:2 * i + 2, :].rearrange("p a b -> p (a b)")

        def ctx_tiles(eng, body):
            with eng.Fori(0, CMAIN // 4) as it:
                for q in range(4):
                    body(4 * it + q, q)
            for i in range(CMAIN, CT):
                body(i, i % 4)

        CMAIN = (CT - 2) // 4 * 4

        CSTEP = CT + 3

        def cdone(b, i):
            return b * CSTEP + i + 5

        def is_last(i):
            return isinstance(i, int) and i == CT - 1

        def crows(i):
            return CLAST if is_last(i) else 128

        def cinc(i):
            return 4 if is_last(i) else 1

        def exists(i):
            return not isinstance(i, int) or i < CT

        with nc.Block() as first:
            @first.sync
            def _(sp):
                for which, value in starts:
                    sp.sem_inc(which, value)

        block = ctx.enter_context(nc.Block())

        @block.sync
        def _(sp):
            n_attn = 0
            for dst, src in ((ident, "ident"), (mass_mask, "mass_mask"), (pair_mask, "pair_mask"),
                             (rows, "rows"), (cols, "cols"), (bdk, "bdk"), (bdv, "bdv"), (bdr, "bdr")):
                sp.dma_start(dst[:], d[src]).then_inc(consts_loaded, 16)
            sp.dma_start(rel0, d["rel0"]).then_inc(consts_loaded, 16)
            sp.dma_start(mask32, d["right_mask"]).then_inc(consts_loaded, 16)
            for dst, src in ((raw_wg[0:GR], "w_gate"), (raw_wu[0:GR], "w_up"), (raw_wd[:], "w_down")):
                sp.dma_start(dst, d[src]).then_inc(ffn_w_loaded, 16)
            for dst, src in ((wq_s, "wq"), (wk_s, "wk"), (wv_s, "wv"), (wo_s, "wo")):
                sp.dma_start(dst[:], d[src]).then_inc(attn_w_loaded, 16)
            for dst, src in ((cwk, "cwk"), (cwv, "cwv"), (cwo, "cwo"), (cwq, "cwq"), (w1, "w1"), (w2, "w2")):
                sp.dma_start(dst[:], d[src]).then_inc(ctx_w_loaded, 16)
            sp.wait_ge(setup_pool, START_MEMSETS + 1)
            for t in range(T):
                sp.dma_start(bias_scr[t].rearrange("h (p r) -> p h r", r=SKEW),
                             arena[:, 0:H * SKEW].rearrange("p (h r) -> p h r", r=SKEW)).then_inc(zeros_stored, 16)
            sp.wait_ge(zeros_stored, 16 * T + 1)
            with sp.Fori(0, NB) as b:
                sp.wait_ge(y2_res, T * b + 1)
                sp.sem_inc(waits_alone, 1)
                sp.dma_start(xin[:], d["x"][ds(b, 1)].rearrange("o (t p) e -> p (o t) e", p=128)).then_inc(x_loaded, 16)
                for t in range(T):
                    sp.wait_ge(r_act, T * b + t + 2)
                    sp.sem_inc(waits_alone, 1)
                    sp.wait_ge(r_dve, T * b + t + 2)
                    sp.sem_inc(waits_alone, 1)
                    sp.dma_start(bias_scr[t].rearrange("h (p r) -> p h r", r=SKEW)[:, :, 0:BAND],
                                 Rb[:, t, :, 0:BAND]).then_inc(bias_stored, 16)
                def load_ctx(i, q):
                    n, p = crows(i), q % 2
                    sp.wait_ge(caff_ready, cdone(b, i - 2) + 1)
                    sp.sem_inc(waits_alone, 1)
                    sp.dma_start(cin[0:n, p, :], d["ctx"][ds(b, 1), ds(i * 128, n), :].rearrange("o p e -> (o p) e"))\
                        .then_inc(ctx_loaded[p], 16)
                ctx_tiles(sp, load_ctx)
                sp.wait_ge(bias_stored, 16 * T * (b + 1) + 1)
                sp.sem_inc(waits_alone, 1)
                sp.wait_ge(e_ready, b + 2)
                sp.sem_inc(waits_alone, 1)
                sp.wait_ge(m_dve, 4 * (b + 1) + 1)
                sp.sem_inc(waits_alone, 1)
                sp.wait_ge(m_act, 4 * (b + 1) + 1)
                sp.sem_inc(waits_alone, 1)
                with sp.Fori(0, T) as t:
                    tile = b * T + t

                    def load_window(g):
                        m = tile * NG + g
                        sp.wait_ge(bias_filled, m + 2)
                        sp.sem_inc(waits_alone, 1)
                        sp.dma_start(Wn[:, (g % 2) * HG:(g % 2 + 1) * HG, :],
                                     bias_scr[ds(t, 1), g * HG:(g + 1) * HG, 0:128 * WIN]
                                     .rearrange("o h (p r) -> p (o h) r", r=WIN)).then_inc(win_loaded[g % 2], 16)

                    def store_probs(g):
                        sp.wait_ge(probs_ready, 4 + tile * H + (g + 1) * HG + 1)
                        sp.sem_inc(waits_alone, 1)
                        sp.dma_start(prob_scr[ds(t, 1), g * HG:(g + 1) * HG, 0:128 * WIN]
                                     .rearrange("o h (p r) -> p (o h) r", r=WIN),
                                     P[:, (g % 2) * HG:(g % 2 + 1) * HG, ds(t * 128, WIN)]).then_inc(p_stored[g % 2], 16)

                    def load_band(g):
                        sp.wait_ge(p_stored[g % 2], 16 * (tile * 2 + g // 2 + 1) + 1)
                        sp.sem_inc(waits_alone, 1)
                        sp.dma_start(Pband[:, ds(t, 1), g * HG:(g + 1) * HG, :].rearrange("p o h r -> p (o h) r"),
                                     prob_scr[ds(t, 1), g * HG:(g + 1) * HG, :]
                                     .rearrange("o h (p r) -> p (o h) r", r=SKEW)[:, :, 0:BAND]).then_inc(band_loaded, 16)

                    load_window(0)
                    load_window(1)
                    for g in range(NG):
                        if g + 2 < NG:
                            load_window(g + 2)
                        store_probs(g)
                        if g:
                            load_band(g - 1)
                    load_band(NG - 1)
                sp.wait_ge(band_loaded, 16 * T * NG * (b + 1) + 1)
                sp.sem_inc(waits_alone, 1)
                for t in range(T):
                    sp.wait_ge(out_ready, T * b + t + 2)
                    sp.sem_inc(waits_alone, 1)
                    sp.dma_start(out[ds(b, 1), t * 128:(t + 1) * 128, :].rearrange("o p e -> (o p) e"),
                                 yout[:, t, :]).then_inc(out_stored, 16)
                sp.wait_ge(out_stored, 16 * T * (b + 1) + 1)
                sp.sem_inc(waits_alone, 1)

        @block.gpsimd
        def _(pool):
            st = Steps(pool_start, "pool_start")
            pool.memset(mhalf[:], -0.5).then_inc(setup_pool, 1)
            pool.memset(zeros[:], 0.0).then_inc(setup_pool, 1)
            pool.memset(arena[:, 0:H * SKEW], 0.0).then_inc(setup_pool, 1)
            pool.wait_ge(consts_loaded, 16 * 10 + 1)
            for k, (kind, parts, n, i) in enumerate(wjobs):
                if k >= 2:
                    pool.wait_ge(qwT_psum, k)
                    pool.sem_inc(waits_alone, 1)
                quant_finish(pool, st, qw[0:parts, k % 2, 0:n], k % 2, parts, n, k)
            st.close()
            pool.wait_ge(tables_ready, 7)
            with pool.Fori(0, NB) as b:
                root(pool, rstd[:, 0:T], x_var, x_rstd, b + 1)
                pool.wait_ge(xn_ready, T * (b + 1) + 1)
                pool.sem_inc(waits_alone, 1)
                pool.tensor_tensor(xin[:], xin[:], rows[:, V_BO:V_BO + 1, :].broadcast_to([128, T, E]), ALU.add)\
                    .then_inc(xb_ready, 1)
                pool.wait_ge(v_ready, 2 * (b + 1) + 1)
                pool.sem_inc(waits_alone, 1)
                for t in range(T - 1):
                    pool.tensor_copy(Vsel[:, t, 0:t + 1, :], Vsel[:, T - 1, 0:t + 1, :]).then_inc(vsel_ready, 1)
                    pool.tensor_tensor(Vsel[:, t, t + 1:T, :], Vsel[:, T - 1, t + 1:T, :],
                                       rows[:, V_EDGE:V_EDGE + 1, :].broadcast_to([128, T - 1 - t, E]), ALU.add)\
                        .then_inc(vsel_ready, 1)
                pool.wait_ge(r_act, T * (b + 1) + 1)
                pool.sem_inc(waits_alone, 1)
                pool.wait_ge(r_dve, T * (b + 1) + 1)
                pool.sem_inc(waits_alone, 1)
                pool.tensor_copy(edge[:], Rb[:, :, :, BAND]).then_inc(e_ready, 1)
                def affine(i, q):
                    n, p = crows(i), q % 2
                    st = Steps(pool_affine, "pool_affine", b * CT + i)
                    root(pool, rstd[0:n, p:p + 1], c_var, c_rstd, b * CT + i + 1)
                    pool.wait_ge(cz_ready, cdone(b, i) + 1)
                    pool.sem_inc(waits_alone, 1)
                    pool.wait_ge(cg_done, cdone(b, i - 4) + 1)
                    pool.sem_inc(waits_alone, 1)
                    st(pool.tensor_tensor(Kn[0:n, q, :], cin[0:n, p, :], rows[0:n, V_G1, :], ALU.mult))
                    pool.wait_ge(st.sem, st.all())
                    pool.sem_inc(waits_alone, 1)
                    pool.tensor_tensor(Kn[0:n, q, :], Kn[0:n, q, :], rows[0:n, V_B1, :], ALU.add)\
                        .then_inc(caff_ready, cinc(i))
                    st.close()

                def norm_root(i, q):
                    root(pool, rn[0:crows(i), q % 2, :], c_norm, c_rnorm, b * CT + i + 1)

                affine(0, 0)
                affine(1, 1)
                affine(2, 2)
                norm_root(0, 0)

                def ctx_pool(i, q):
                    if exists(i + 1):
                        norm_root(i + 1, q + 1)
                    if exists(i + 3):
                        affine(i + 3, (q + 3) % 4)
                ctx_tiles(pool, ctx_pool)

                pool.wait_ge(m_dve, 4 * (b + 1) + 1)
                pool.sem_inc(waits_alone, 1)
                pool.wait_ge(m_act, 4 * (b + 1) + 1)
                pool.sem_inc(waits_alone, 1)
                pool.memset(P[:, :, 0:PAD], 0.0).then_inc(setup_pool, 1)
                pool.memset(P[:, :, PAD + S:ROW], 0.0).then_inc(setup_pool, 1)
                pool.memset(Bt[:, :, 0:PAD], 0.0).then_inc(setup_pool, 1)
                pool.memset(Bt[:, :, PAD + S:ROW], 0.0).then_inc(setup_pool, 1)
                pool.wait_ge(setup_pool, START_MEMSETS + 4 * (b + 1) + 1)
                pool.sem_inc(waits_alone, 1)
                with pool.Fori(0, T) as t:
                    tile = b * T + t
                    pool.wait_ge(scores_ready, tile * H + 1)
                    pool.sem_inc(waits_alone, 1)
                    pool.tensor_copy(QS[:], QT[:, :, ds(t * 128, 128)]).then_inc(qs_ready, 1)

                    def fill(g):
                        m = tile * NG + g
                        lo = (g % 2) * HG
                        stt = Steps(pool_fill, "pool_fill", m)
                        pool.wait_ge(scores_biased, m * HG + 1)
                        pool.sem_inc(waits_alone, 1)
                        stt(pool.tensor_tensor(
                            Bt[:, lo:lo + HG, PAD:PAD + S],
                            right_mask[:, ds(384 - t * 128, S)].unsqueeze(1).broadcast_to([128, HG, S]),
                            bcast(edge[:, ds(t, 1), g * HG:(g + 1) * HG].rearrange("p o h -> p (o h)"), S), ALU.mult))
                        pool.wait_ge(stt.sem, stt.all())
                        pool.sem_inc(waits_alone, 1)
                        pool.wait_ge(win_loaded[g % 2], 16 * (tile * 2 + g // 2 + 1) + 1)
                        pool.sem_inc(waits_alone, 1)
                        pool.tensor_tensor(Bt[:, lo:lo + HG, ds(t * 128, WIN)], Bt[:, lo:lo + HG, ds(t * 128, WIN)],
                                           Wn[:, lo:lo + HG, :], ALU.add).then_inc(bias_filled, 1)

                    def edge_mass(g):
                        m = tile * NG + g
                        pool.wait_ge(probs_ready, 4 + (m + 1) * HG + 1)
                        pool.sem_inc(waits_alone, 1)
                        pool.wait_ge(mass_red, m + 1)
                        pool.sem_inc(waits_alone, 1)
                        pool.tensor_tensor(prod[:], P[:, (g % 2) * HG:(g % 2 + 1) * HG, ds(t * 128 + BAND, 128)],
                                           mass_mask[:].unsqueeze(1).broadcast_to([128, HG, 128]), ALU.mult)\
                            .then_inc(mass_mul, 1)

                    fill(0)
                    fill(1)
                    for g in range(NG):
                        edge_mass(g)
                        if g + 2 < NG:
                            fill(g + 2)
                st = Steps(pool_tail, "pool_tail", b)
                root(pool, rstd[:, 0:T], t_var, t_rstd, 4 * b + 1)
                root(pool, rstd[:, 0:T], t_var, t_rstd, 4 * b + 2)
                for t in range(T):
                    pool.wait_ge(qz_ready, T * b + t + 2)
                    pool.sem_inc(waits_alone, 1)
                    st(pool.tensor_tensor(Qn[:, t, :], Qn[:, t, :], rows[:, V_G1, :], ALU.mult))
                    pool.wait_ge(st.sem, st.all())
                    pool.sem_inc(waits_alone, 1)
                    pool.tensor_tensor(Qn[:, t, :], Qn[:, t, :], rows[:, V_B1, :], ALU.add).then_inc(qaff_ready, 1)
                for t in range(T):
                    pool.tensor_tensor(yr[:, t, :], Qx[:, t, :], rows[:, V_XBO, :], ALU.add).then_inc(y_res, 1)
                for t in range(T):
                    root(pool, rn[:, t % 2, :], q_norm, q_rnorm, T * b + t + 1)
                root(pool, rstd[:, 0:T], t_var, t_rstd, 4 * b + 3)
                for t in range(T):
                    pool.wait_ge(yz_ready, T * b + t + 2)
                    pool.sem_inc(waits_alone, 1)
                    st(pool.tensor_tensor(yn[:, t, :], yn[:, t, :], rows[:, V_G2, :], ALU.mult))
                    pool.wait_ge(st.sem, st.all())
                    pool.sem_inc(waits_alone, 1)
                    pool.tensor_tensor(yn[:, t, :], yn[:, t, :], rows[:, V_B2, :], ALU.add).then_inc(yaff_ready, 1)
                for t in range(T):
                    st(pool.tensor_tensor(yr[:, t, :], y[:, t, :], rows[:, V_XB2, :], ALU.add))
                    pool.wait_ge(st.sem, st.all())
                    pool.sem_inc(waits_alone, 1)
                    pool.tensor_tensor(yr[:, t, :], yr[:, t, :], xin[:, t, :], ALU.add).then_inc(y2_res, 1)
                root(pool, rstd[:, 0:T], t_var, t_rstd, 4 * b + 4)
                for t in range(T):
                    k = NQ0 + b * QPB + t
                    quant_finish(pool, st, xq[:, t, :], t % 2, 128, E, k)
                for t in range(T):
                    k = NQ0 + b * QPB + T + t
                    if t >= 2:
                        pool.wait_ge(ht_psum, T * b + t)
                        pool.sem_inc(waits_alone, 1)
                    quant_finish(pool, st, hq[:, t % 2, :], t % 2, 128, FF, k)
                st.close()

        @block.scalar
        def _(act):
            for k, (kind, parts, n, i) in enumerate(wjobs):
                quant_abs(act, k % 2, parts, n, k)
            with act.Fori(0, NB) as b:
                act.wait_ge(xnT_psum, 2 * b + 2)
                act.sem_inc(waits_alone, 1)
                act.activation(xnT[:, 0, :], bank(0), ACT.Copy).then_inc(xnT_ready, 1)
                for c in range(4):
                    act.wait_ge(k_psum, 4 * b + c + 2)
                    act.activation(KT[:, c, :], bank(2 + c), ACT.Identity, bias=cols[:, 4 + c:5 + c]).then_inc(kT_ready, 1)
                for j in range(2):
                    act.wait_ge(v_psum, 2 * b + j + 2)
                    act.activation(Vsel[:, T - 1, 2 * j:2 * j + 2, :].rearrange("p a b -> p (a b)"), bank(2 + j), ACT.Copy)\
                        .then_inc(v_ready, 1)
                act.wait_ge(out_stored, 16 * T * b + 1)
                for t in range(T):
                    act.wait_ge(r_psum, 8 * b + 2 * t + 2)
                    act.activation(Rb[:, t, 0:8, :].rearrange("p h r -> p (h r)"), bank(4 + 2 * t % 4, 0, 8 * NREL), ACT.Copy)\
                        .then_inc(r_act, 1)

                def copy_ct(i, p):
                    n = crows(i)
                    act.wait_ge(ct_psum, cdone(b, i) + 1)
                    act.wait_ge(ck_psum, cdone(b, i - 2) + 1)
                    act.activation(cnT[:, p, :, 0:n],
                                   bank(6 + p, 0, 256).rearrange("p (c t) -> p c t", c=2)[:, :, 0:n], ACT.Copy)\
                        .then_inc(ct_ready, cinc(i))

                def copy_k(i, q):
                    n = crows(i)
                    act.wait_ge(ck_psum, cdone(b, i) + 1)
                    act.wait_ge(cg_done, cdone(b, i - 4) + 1)
                    act.activation(kns[0:n, q, :], PS[0:n, 4 * 512:6 * 512], ACT.Copy).then_inc(kc_ready, cinc(i))

                def square(i, q):
                    n = crows(i)
                    act.wait_ge(kc_ready, cdone(b, i) + 1)
                    act.wait_ge(c_norm, b * CT + i + 1)
                    act.activation(csq[0:n], kns[0:n, q, :], ACT.Square).then_inc(csq_ready, cinc(i))

                copy_ct(0, 0)
                copy_ct(1, 1)
                copy_k(0, 0)
                square(0, 0)
                copy_ct(2, 0)
                copy_k(1, 1)
                square(1, 1)

                def ctx_act(i, q):
                    if exists(i + 2):
                        copy_k(i + 2, (q + 2) % 4)
                    if exists(i + 3):
                        copy_ct(i + 3, (q + 3) % 2)
                    if exists(i + 2):
                        square(i + 2, (q + 2) % 4)
                ctx_tiles(act, ctx_act)
                act.wait_ge(cg_done, cdone(b, CT - 1) + 1)
                for j in (0, 2):
                    act.activation(Gs[:, 2 * j:2 * j + 2, :].rearrange("p a b -> p (a b)"), bank(j), ACT.Copy).then_inc(g_act, 1)
                for c in range(2):
                    act.wait_ge(gt_psum, 4 * b + 2 * c + 2)
                    act.activation(GT[:, c, 0:4, :].rearrange("p a b -> p (a b)"), bank(4 + 2 * c), ACT.Copy).then_inc(gt_act, 1)
                for j in (0, 2):
                    act.wait_ge(m_psum, 4 * b + j + 2)
                    act.activation(M[:, 2 * j:2 * j + 2, :].rearrange("p a b -> p (a b)"), bank(2 + j), ACT.Copy)\
                        .then_inc(m_act, 2)
                act.wait_ge(m_dve, 4 * (b + 1) + 1)
                act.wait_ge(setup_pool, START_MEMSETS + 4 * (b + 1) + 1)
                with act.Fori(0, T) as t:
                    tile = b * T + t

                    def exps(h):
                        g, j = divmod(h, HG)
                        u = tile * H + h
                        m = tile * NG + g
                        if j == 0:
                            act.wait_ge(transposed, m * HG + 1)
                            act.wait_ge(mass_mul, m + 2)
                            act.wait_ge(p_stored[g % 2], 16 * (tile * 2 + g // 2) + 1)
                        act.wait_ge(scores_biased, 4 + u + 2)
                        act.activation(P[:, (g % 2) * HG + j, PAD:PAD + S], Sb[:, h % 2, :], ACT.Exp, bias=nmax[:, j:j + 1],
                                       scale=-1.0, accum_out=lsum[:, ds(t, 1), h]).then_inc(probs_ready, 1)

                    def evac(h):
                        i = tile * (H // 2) + h // 2
                        act.wait_ge(transposed, 4 + tile * H + h + 2)
                        act.wait_ge(pv_done, tile * H + h + 2)
                        act.activation(PTs[:, 0, :], bank(4), ACT.Copy).then_inc(pt_copied[0], 1)

                    LAG = 4
                    for h in range(H + LAG):
                        if h < H:
                            exps(h)
                        if h >= LAG and h % 2 == 0:
                            evac(h - LAG)
                    act.wait_ge(pv_done, 2 + (tile + 1) * H + 1)
                    act.activation(Oraw[:, ds(t, 1), :].rearrange("p o e -> p (o e)"), bank(6, 0, E), ACT.Copy).then_inc(o_evac, 1)
                for t in range(T):
                    act.wait_ge(fa_psum, 2 * (T * b + t) + 2)
                    if t >= 2:
                        act.wait_ge(f_psum, T * b + t)
                    act.activation(AT[:, t % 2, 0:4, :].rearrange("p a b -> p (a b)"), bank(2 * (t % 2)), ACT.Copy)\
                        .then_inc(fa_act, 1)
                for t in range(T):
                    act.wait_ge(at_psum, T * b + t + 2)
                    if t >= 2:
                        act.wait_ge(wo_psum, T * b + t)
                    act.activation(aT[:, t % 2, :, :].rearrange("p a b -> p (a b)"), bank(6 + t % 2, 0, 256), ACT.Copy)\
                        .then_inc(aT_ready, 1)
                act.wait_ge(qnT_psum, 2 * b + 2)
                act.activation(QnT[:, 0, :], bank(0), ACT.Copy).then_inc(qnT_ready, 1)
                for t in range(T + 1):
                    if t < T:
                        act.wait_ge(xq_psum, T * b + t + 2)
                        if t:
                            act.wait_ge(qn_ready, T * b + t + 1)
                        act.activation(sq, PS[:, (2 + 2 * (t % 2)) * 512:(4 + 2 * (t % 2)) * 512], ACT.Square).then_inc(sq_ready, 1)
                    if t:
                        act.wait_ge(qt_psum, 2 * (T * b + t - 1) + 2)
                        if t >= 2:
                            act.wait_ge(o_psum, T * b + t)
                        act.activation(qnT[:, 0:4, :].rearrange("p a b -> p (a b)"), bank(6), ACT.Copy).then_inc(qt_act, 1)
                act.wait_ge(ynT_psum, 2 * b + 2)
                act.activation(ynT[:, 0, :], bank(2), ACT.Copy).then_inc(ynT_ready, 1)
                for f in range(NF):
                    act.wait_ge(h_psum, NF * b + f + 2)
                    act.activation(hT[:, f, :], bank(4 + f % 4), ACT.Gelu, bias=cols[:, 8 + f:9 + f]).then_inc(h_ready, 1)
                for t in range(T):
                    quant_abs(act, t % 2, 128, E, NQ0 + b * QPB + t)
                act.wait_ge(xqT_psum, 2 * b + 2)
                act.activation(xqT[:, 0, :], bank(2), ACT.Copy).then_inc(xqT_ready, 1)
                for t in range(T + 2):
                    if t < T:
                        act.wait_ge(gu_psum, T * b + t + 2)
                        if t >= 2:
                            act.wait_ge(quant_v, NQ0 + b * QPB + T + t)
                        g0 = (t % 2) * 3 * 512
                        act.activation(gs[:, t % 2, :], PS[:, g0:g0 + FF], ACT.Silu).then_inc(silu_ready, 1)
                    if 1 <= t <= T:
                        quant_abs(act, (t - 1) % 2, 128, FF, NQ0 + b * QPB + T + t - 1)
                    if t >= 2:
                        act.wait_ge(ht_psum, T * b + t)
                        if t >= 4:
                            act.wait_ge(dn_psum, T * b + t - 3 + 1)
                        act.activation(hqT[:, t % 2, 0:4, :].rearrange("p a b -> p (a b)"), bank(6), ACT.Copy)\
                            .then_inc(ht_act, 1)

        @block.vector
        def _(dve):
            st = Steps(dve_start, "dve_start")
            dve.wait_ge(consts_loaded, 16 * 10 + 1)
            dve.sem_inc(waits_alone, 1)
            dve.tensor_copy(right_mask[:], mask32).then_inc(tables_ready, 1)
            o = HG * NREL
            dve.tensor_tensor(bdk[:], bdk[:], rel0[:, 0:o], ALU.subtract).then_inc(tables_ready, 1)
            dve.tensor_tensor(bdv[:].rearrange("p a b -> p (a b)"), bdv[:].rearrange("p a b -> p (a b)"),
                              rel0[:, o:o + 320], ALU.subtract).then_inc(tables_ready, 1)
            o += 320
            dve.tensor_tensor(bdr[:], bdr[:], rel0[0:16, o:o + E], ALU.subtract).then_inc(tables_ready, 1)
            dve.tensor_tensor(rows[:, V_EDGE, :], rows[:, V_EDGE, :], rel0[:, o + E:o + 2 * E], ALU.subtract)\
                .then_inc(tables_ready, 1)
            dve.tensor_tensor(rows[:, V_BV, :], rows[:, V_BV, :], rel0[:, o + E:o + 2 * E], ALU.add).then_inc(tables_ready, 1)
            dve.wait_ge(ffn_w_loaded, 16 * 3 + 1)
            def wcopy(k):
                kind, parts, n, i = wjobs[k]
                dve.wait_ge(qwT_psum, k + 2)
                if kind == "d":
                    src = PS[:, 0:1024].rearrange("p (c r) -> p c r", r=128)
                    dve.tensor_copy(wdT[:, 0:5, i * 128:(i + 1) * 128], src[:, 0:5, :]).then_inc(qwT_ready, 1)
                    dve.tensor_copy(wdT[0:FLAST, 5, i * 128:(i + 1) * 128], src[0:FLAST, 5, :]).then_inc(qwT_ready, 1)
                else:
                    dst = wgT if kind == "g" else wuT
                    src = PS[:, 0:1024].rearrange("p (a c r) -> p a c r", a=2, c=4)
                    for a in range(2):
                        dve.tensor_copy(dst[:, :, (2 * i + a) * GR:(2 * i + a + 1) * GR], src[:, a, 0:2, 0:GR]).then_inc(qwT_ready, 1)
            for k, (kind, parts, n, i) in enumerate(wjobs):
                quant_scale(dve, st, wsrc(kind, i), k % 2, parts, n, k)
                if k:
                    _, pp, nn, _ = wjobs[k - 1]
                    quant_count(dve, st, (k - 1) % 2, pp, nn, k - 1)
                if k >= 2:
                    wcopy(k - 2)
            k = len(wjobs)
            quant_count(dve, st, (k - 1) % 2, wjobs[-1][1], wjobs[-1][2], k - 1)
            wcopy(k - 2)
            wcopy(k - 1)
            st.close()
            dve.wait_ge(tables_ready, 7)
            dve.wait_ge(zeros_stored, 16 * T + 1)
            with dve.Fori(0, NB) as b:
                st = Steps(dve_prep, "dve_prep", b)
                dve.wait_ge(x_loaded, 16 * (b + 1) + 1)
                dve.sem_inc(waits_alone, 1)
                layernorm(dve, st, [xin[:, t, :] for t in range(T)], [xn[:, t, :] for t in range(T)], xn_ready,
                          x_var, x_rstd, b + 1)
                dve.wait_ge(xnT_psum, 2 * b + 3)
                dve.tensor_copy(xnT[:, 1, :], bank(1)).then_inc(xnT_ready, 1)
                for c in range(4):
                    dve.wait_ge(q_psum, 4 * b + c + 2)
                    dve.tensor_scalar(QT[:, c, :], bank((6 + c) % 8), cols[:, c:c + 1], None, ALU.add).then_inc(qT_ready, 1)
                dve.wait_ge(out_stored, 16 * T * b + 1)
                for t in range(T):
                    dve.wait_ge(r_psum, 8 * b + 2 * t + 3)
                    dve.tensor_copy(Rb[:, t, 8:16, :].rearrange("p h r -> p (h r)"), bank(5 + 2 * t % 4, 0, 8 * NREL))\
                        .then_inc(r_dve, 1)
                st.close()

                def norm_stats(i, p):
                    n = crows(i)
                    st = Steps(dve_norm, "dve_norm", b * CT + i)
                    per = (CT + 1) // 2 if p == 0 else CT // 2
                    dve.wait_ge(ctx_loaded[p], 16 * per * b + 8 * (i - p) + 17)
                    st(dve.bn_stats(bnst[0:n, p, :], cin[0:n, p, :]))
                    dve.wait_ge(st.sem, st.all())
                    dve.sem_inc(waits_alone, 1)
                    st(dve.bn_aggr(mv[0:n, p, :], bnst[0:n, p, :]))
                    dve.wait_ge(st.sem, st.all())
                    dve.tensor_scalar(rstd[0:n, p:p + 1], mv[0:n, p, 1:2], EPS, None, ALU.add).then_inc(c_var, 1)
                    st.close()

                def norm_apply(i, p):
                    n = crows(i)
                    x = cin[0:n, p, :]
                    dve.wait_ge(c_rstd, b * CT + i + 2)
                    dve.tensor_scalar(x, x, mv[0:n, p, 0:1], rstd[0:n, p:p + 1], ALU.subtract, ALU.mult)\
                        .then_inc(cz_ready, cinc(i))

                def sum_squares(i, p):
                    n = crows(i)
                    st = Steps(dve_scale, "dve_scale", b * CT + i)
                    dve.wait_ge(csq_ready, cdone(b, i) + 1)
                    st(dve.tensor_reduce(ss[0:n, p, :], csq[0:n].rearrange("p (h c) -> p h c", c=XD), AX.X, ALU.add))
                    dve.wait_ge(st.sem, st.all())
                    dve.tensor_scalar(rn[0:n, p, :], ss[0:n, p, :], 1e-24, None, ALU.max).then_inc(c_norm, 1)
                    st.close()

                def scale_k(i, q):
                    n = crows(i)
                    dve.wait_ge(c_rnorm, b * CT + i + 2)
                    k = kns[0:n, q, :].rearrange("p (h c) -> p h c", c=XD)
                    dve.tensor_tensor(k, k, bcast(rn[0:n, q % 2, :], XD), ALU.mult).then_inc(cs_ready, cinc(i))

                for i in range(3):
                    norm_stats(i, i % 2)
                    norm_apply(i, i % 2)
                sum_squares(0, 0)

                def ctx_dve(i, q):
                    if exists(i + 1):
                        sum_squares(i + 1, (q + 1) % 2)
                    if exists(i + 3):
                        norm_stats(i + 3, (q + 3) % 2)
                    scale_k(i, q)
                    if exists(i + 3):
                        norm_apply(i + 3, (q + 3) % 2)
                ctx_tiles(dve, ctx_dve)
                dve.wait_ge(cg_done, cdone(b, CT - 1) + 1)
                for j in (1, 3):
                    dve.tensor_copy(Gs[:, 2 * j:2 * j + 2, :].rearrange("p a b -> p (a b)"), bank(j)).then_inc(g_dve, 1)
                for c in range(2):
                    dve.wait_ge(gt_psum, 4 * b + 2 * c + 3)
                    dve.tensor_copy(GT[:, c, 4:8, :].rearrange("p a b -> p (a b)"), bank(5 + 2 * c)).then_inc(gt_dve, 1)
                for j in range(2):
                    dve.wait_ge(kvt_psum, 2 * b + j + 2)
                    dve.tensor_tensor(KVT[:, 4 * j:4 * j + 4, :], bank(j).rearrange("p (a b) -> p a b", a=4),
                                      pair_mask[:].unsqueeze(1).broadcast_to([128, 4, 128]), ALU.mult).then_inc(kvt_ready, 1)
                for j in (1, 3):
                    dve.wait_ge(m_psum, 4 * b + j + 2)
                    dve.tensor_copy(M[:, 2 * j:2 * j + 2, :].rearrange("p a b -> p (a b)"), bank(2 + j)).then_inc(m_dve, 2)
                dve.wait_ge(m_act, 4 * (b + 1) + 1)
                dve.sem_inc(waits_alone, 1)
                with dve.Fori(0, T) as t:
                    tile = b * T + t

                    def bias(h):
                        g, j = divmod(h, HG)
                        u = tile * H + h
                        if j == 0:
                            dve.wait_ge(bias_filled, 2 + tile * NG + g + 2)
                        dve.wait_ge(scores_ready, u + 2)
                        dve.wait_ge(probs_ready, u + 4)
                        dve.sem_inc(waits_alone, 1)
                        dve.tensor_tensor_reduce(out=Sb[:, h % 2, :], in0=bank(j), in1=Bt[:, (g % 2) * HG + j, PAD:PAD + S],
                                                 scale=-0.25, scalar=BIG, op0=ALU.add, op1=ALU.min,
                                                 accum_out=nmax[:, j:j + 1]).then_inc(scores_biased, 1)

                    def evac(h):
                        dve.wait_ge(transposed, 4 + tile * H + h + 2)
                        dve.wait_ge(pv_done, tile * H + h + 2)
                        dve.tensor_copy(PTs[:, 1, :], bank(5)).then_inc(pt_copied[1], 1)

                    def sum_mass(g):
                        dve.wait_ge(mass_mul, 2 + tile * NG + g + 2)
                        dve.tensor_reduce(mass[:, ds(t, 1), g * HG:(g + 1) * HG].rearrange("p o h -> p (o h)"), prod, AX.X, ALU.add)\
                            .then_inc(mass_red, 1)

                    LAG = 4
                    for h in range(H + LAG):
                        if h < H:
                            bias(h)
                        if h >= LAG and h % 2 == 1:
                            evac(h - LAG)
                        if h % HG == HG - 1 and h >= 2 * HG - 1:
                            sum_mass(h // HG - 1)
                st = Steps(dve_attn, "dve_attn", b)
                dve.wait_ge(probs_ready, 4 + T * H * (b + 1) + 1)
                st(dve.reciprocal(rl[:], lsum[:]))

                def copy_band(t):
                    dve.wait_ge(fa_psum, 2 * (T * b + t) + 3)
                    if t >= 2:
                        dve.wait_ge(f_psum, T * b + t)
                    dve.tensor_copy(AT[:, t % 2, 4, :], bank(2 * (t % 2) + 1, 0, 128)).then_inc(fa_dve, 1)
                    dve.tensor_copy(massT[0:H, t % 2, :], bank(2 * (t % 2) + 1, 128, 256, H)).then_inc(fa_dve, 1)

                def combine(t):
                    dve.wait_ge(f_psum, T * b + t + 2)
                    dve.wait_ge(o_evac, T * b + t + 2)
                    st(dve.tensor_tensor(Oraw[:, t, :], Oraw[:, t, :], bank(4 + t % 2, 0, E), ALU.add))
                    dve.wait_ge(st.sem, st.all())
                    o = Oraw[:, t, :].rearrange("p (h c) -> p h c", c=HD)
                    st(dve.tensor_tensor(o, o, bcast(rl[:, t, :], HD), ALU.mult))
                    dve.wait_ge(st.sem, st.all())
                    dve.tensor_tensor(Oraw[:, t, :], Oraw[:, t, :], rows[:, V_BV, :], ALU.add).then_inc(attn_ready, 1)

                copy_band(0)
                for t in range(T):
                    if t + 1 < T:
                        copy_band(t + 1)
                    combine(t)
                for t in range(T):
                    dve.wait_ge(wo_psum, T * b + t + 2)
                    dve.wait_ge(xb_ready, b + 2)
                    dve.tensor_tensor(xin[:, t, :], xin[:, t, :], bank(4 + t % 2, 0, E), ALU.add).then_inc(x1_ready, 1)
                st.close()
                st = Steps(dve_tail, "dve_tail", b)
                dve.wait_ge(x1_ready, T * (b + 1) + 1)
                tiles = range(T)
                layernorm(dve, st, [xin[:, t, :] for t in tiles], [Qx[:, t, :] for t in tiles], qx_ready,
                          t_var, t_rstd, 4 * b + 1)
                dve.wait_ge(qx_ready, T * (b + 1) + 1)
                layernorm(dve, st, [Qx[:, t, :] for t in tiles], [Qn[:, t, :] for t in tiles], qz_ready,
                          t_var, t_rstd, 4 * b + 2)
                dve.wait_ge(qnT_psum, 2 * b + 3)
                dve.tensor_copy(QnT[:, 1, :], bank(1)).then_inc(qnT_ready, 1)

                def scale_q(t):
                    p = t % 2
                    dve.wait_ge(sq_ready, T * b + t + 2)
                    st(dve.tensor_reduce(ss[:, p, :], sq.rearrange("p (h c) -> p h c", c=XD), AX.X, ALU.add))
                    dve.wait_ge(st.sem, st.all())
                    dve.tensor_scalar(rn[:, p, :], ss[:, p, :], 1e-24, None, ALU.max).then_inc(q_norm, 1)
                    dve.wait_ge(q_rnorm, T * b + t + 2)
                    if t >= 2:
                        dve.wait_ge(qt_psum, 2 * (T * b + t - 1) + 1)
                    dve.tensor_tensor(qn[:, p, :].rearrange("p (h c) -> p h c", c=XD),
                                      PS[:, (2 + 2 * p) * 512:(4 + 2 * p) * 512].rearrange("p (h c) -> p h c", c=XD),
                                      bcast(rn[:, p, :], XD), ALU.mult).then_inc(qn_ready, 1)

                for t in range(T + 2):
                    if t < T:
                        scale_q(t)
                    if 1 <= t <= T:
                        dve.wait_ge(qt_psum, 2 * (T * b + t - 1) + 3)
                        if t >= 2:
                            dve.wait_ge(o_psum, T * b + t)
                        dve.tensor_copy(qnT[:, 4:8, :].rearrange("p a b -> p (a b)"), bank(7)).then_inc(qt_dve, 1)
                    if t >= 2:
                        dve.wait_ge(o_psum, T * b + t)
                        dve.wait_ge(y_res, T * b + t)
                        dve.tensor_tensor(y[:, t - 2, :], yr[:, t - 2, :], bank(t % 2, 0, E), ALU.add).then_inc(y_ready, 1)
                dve.wait_ge(y_ready, T * (b + 1) + 1)
                layernorm(dve, st, [y[:, t, :] for t in tiles], [yn[:, t, :] for t in tiles], yz_ready,
                          t_var, t_rstd, 4 * b + 3)
                dve.wait_ge(ynT_psum, 2 * b + 3)
                dve.tensor_copy(ynT[:, 1, :], bank(3)).then_inc(ynT_ready, 1)
                for t in tiles:
                    dve.wait_ge(m2_psum, T * b + t + 2)
                    dve.wait_ge(y2_res, T * b + t + 2)
                    dve.tensor_tensor(x2[:, t, :], yr[:, t, :], bank(t % 2, 0, E), ALU.add).then_inc(x2_ready, 1)
                dve.wait_ge(x2_ready, T * (b + 1) + 1)
                layernorm(dve, st, [x2[:, t, :] for t in tiles], [zf[:, t, :] for t in tiles], zf_ready,
                          t_var, t_rstd, 4 * b + 4)
                dve.wait_ge(zf_ready, T * (b + 1) + 1)
                for t in range(T + 1):
                    if t < T:
                        quant_scale(dve, st, zf[:, t, :], t % 2, 128, E, NQ0 + b * QPB + t)
                    if t:
                        quant_count(dve, st, (t - 1) % 2, 128, E, NQ0 + b * QPB + t - 1)
                dve.wait_ge(xqT_psum, 2 * b + 3)
                dve.tensor_copy(xqT[:, 1, :], bank(3)).then_inc(xqT_ready, 1)
                for t in range(T + 2):
                    if t < T:
                        g0 = (t % 2) * 3 * 512
                        dve.wait_ge(silu_ready, T * b + t + 2)
                        dve.tensor_tensor(gs[:, t % 2, :], gs[:, t % 2, :], PS[:, g0 + FF:g0 + 2 * FF], ALU.mult).then_inc(hh_ready, 1)
                        dve.wait_ge(hh_ready, T * b + t + 2)
                        quant_scale(dve, st, gs[:, t % 2, :], t % 2, 128, FF, NQ0 + b * QPB + T + t)
                    if 1 <= t <= T:
                        quant_count(dve, st, (t - 1) % 2, 128, FF, NQ0 + b * QPB + T + t - 1)
                    if t >= 2:
                        dve.wait_ge(ht_psum, T * b + t)
                        if t >= 4:
                            dve.wait_ge(dn_psum, T * b + t - 3 + 1)
                        dve.tensor_copy(hqT[:, t % 2, 4, :], bank(7, 0, 128)).then_inc(ht_dve, 1)
                        dve.tensor_copy(hqT[0:FLAST, t % 2, 5, :], bank(7, 128, 256, FLAST)).then_inc(ht_dve, 1)
                        dve.wait_ge(dn_psum, T * b + t)
                        dve.tensor_tensor(yout[:, t - 2, :], x2[:, t - 2, :], bank(7, 256, 512), ALU.add).then_inc(out_ready, 1)
                st.close()

        @block.tensor
        def _(pe):
            def mm(o, l, r, start, stop, **kw):
                return pe.matmul(o, l, r, start=start, stop=stop, **kw)

            def tr(o, i):
                return pe.transpose(o, i, ident[0:i.shape[0], 0:i.shape[0]])

            pe.wait_ge(consts_loaded, 16 * 10 + 1)
            pe.sem_inc(waits_alone, 1)
            for k, (kind, parts, n, i) in enumerate(wjobs):
                pe.wait_ge(quant_out, 2 + k + 2)
                if k:
                    pe.wait_ge(qwT_ready, 2 * k + 1)
                if kind == "d":
                    for c in range(NFF):
                        w = min(128, FF - c * 128)
                        last = tr(PS[0:w, c * 128:c * 128 + 128], qw[:, k % 2, c * 128:c * 128 + w])
                else:
                    for a in range(2):
                        for c in range(2):
                            last = tr(bank(a, c * 128, c * 128 + GR), qw[0:GR, k % 2, (2 * a + c) * 128:(2 * a + c + 1) * 128])
                last.then_inc(qwT_psum, 1)
            pe.wait_ge(qwT_ready, 2 * NQ0 + 1)
            pe.wait_ge(attn_w_loaded, 16 * 4 + 1)
            pe.wait_ge(ctx_w_loaded, 16 * 6 + 1)
            pe.wait_ge(tables_ready, 7)
            pe.wait_ge(setup_pool, START_MEMSETS + 1)
            pe.wait_ge(zeros_stored, 16 * T + 1)
            with pe.Fori(0, NB) as b:
                pe.wait_ge(out_ready, T * b + 1)
                pe.sem_inc(waits_alone, 1)
                for t in range(T):
                    pe.wait_ge(xn_ready, T * b + t + 2)
                    for c in range(2):
                        i = tr(bank(c, t * 128, t * 128 + 128), xn[:, t, c * 128:(c + 1) * 128])
                        if t == T - 1:
                            i.then_inc(xnT_psum, 1)
                pe.wait_ge(xnT_ready, 2 * (b + 1) + 1)
                for q in range(4):
                    for c in range(2):
                        i = mm(bank(2 + q), wk_s[:, c, q * 128:(q + 1) * 128], xnT[:, c, :], c == 0, c == 1)
                    i.then_inc(k_psum, 1)
                for q in range(4):
                    for c in range(2):
                        i = mm(bank((6 + q) % 8), wq_s[:, c, q * 128:(q + 1) * 128], xnT[:, c, :], c == 0, c == 1)
                    i.then_inc(q_psum, 1)
                for t in range(T):
                    if t % 2 == 0:
                        pe.wait_ge(kT_ready, 4 * b + t // 2 + 2)
                    for c in range(2):
                        i = mm(bank(2 + t // 2, (t % 2) * E, (t % 2 + 1) * E), xnT[:, c, t * 128:(t + 1) * 128], wv_s[:, c, :],
                               c == 0, c == 1)
                    if t % 2:
                        i.then_inc(v_psum, 1)
                pe.wait_ge(kT_ready, 4 * (b + 1) + 1)
                pe.wait_ge(qT_ready, 4 * (b + 1) + 1)
                for t in range(T):
                    if t >= 2:
                        pe.wait_ge(r_act, T * b + t)
                        pe.wait_ge(r_dve, T * b + t)
                    for q in range(4):
                        i = mm(bank(4 + 2 * (t % 2) + q // 2, (q % 2) * HG * NREL, (q % 2 + 1) * HG * NREL),
                               QT[:, q, t * 128:(t + 1) * 128], bdk[:], True, True)
                        if q % 2:
                            i.then_inc(r_psum, 1)

                def t_ctx(i, q):
                    n, p = crows(i), q % 2
                    pe.wait_ge(caff_ready, cdone(b, i) + 1)
                    pe.wait_ge(ct_ready, cdone(b, i - 2) + 1)
                    for c in range(2):
                        ins = tr(bank(6 + p, c * 128, c * 128 + n), Kn[0:n, q, c * 128:(c + 1) * 128])
                    ins.then_inc(ct_psum, cinc(i))

                def k_ctx(i, q):
                    n, p = crows(i), q % 2
                    pe.wait_ge(ct_ready, cdone(b, i) + 1)
                    pe.wait_ge(kc_ready, cdone(b, i - 1) + 1)
                    for j in range(2):
                        for c in range(2):
                            ins = mm(bank(4 + j, parts=n), cnT[:, p, c, 0:n], cwk[:, c, j * 512:(j + 1) * 512], c == 0, c == 1)
                    ins.then_inc(ck_psum, cinc(i))

                def g_ctx(i, q):
                    n, p = crows(i), q % 2
                    pe.wait_ge(cs_ready, cdone(b, i) + 1)
                    for m in range(NM):
                        ins = mm(bank(m // 2, (m % 2) * E, (m % 2 + 1) * E), kns[0:n, q, m * 128:(m + 1) * 128], Kn[0:n, q, :],
                                 False, True, skip_group_check=True)
                    ins.then_inc(cg_done, cinc(i))

                pe.wait_ge(v_ready, 2 * (b + 1) + 1)
                pe.wait_ge(r_act, T * (b + 1) + 1)
                pe.wait_ge(r_dve, T * (b + 1) + 1)
                for j in range(4):
                    mm(bank(j), zeros[:, 0:128], zeros[:, :], True, True, skip_group_check=True)
                t_ctx(0, 0)
                t_ctx(1, 1)
                k_ctx(0, 0)
                t_ctx(2, 2)
                k_ctx(1, 1)

                def ctx_pe(i, q):
                    if exists(i + 2):
                        k_ctx(i + 2, (q + 2) % 4)
                    if exists(i + 3):
                        t_ctx(i + 3, (q + 3) % 4)
                    g_ctx(i, q)
                ctx_tiles(pe, ctx_pe)
                pe.wait_ge(g_act, 2 * (b + 1) + 1)
                pe.wait_ge(g_dve, 2 * (b + 1) + 1)
                for c in range(2):
                    for m in range(NM):
                        i = tr(bank(4 + 2 * c + m // 4, (m % 4) * 128, (m % 4 + 1) * 128), Gs[:, m, c * 128:(c + 1) * 128])
                        if m % 4 == 3:
                            i.then_inc(gt_psum, 1)
                pe.wait_ge(gt_act, 2 * (b + 1) + 1)
                pe.wait_ge(gt_dve, 2 * (b + 1) + 1)
                for m in range(NM):
                    for c in range(2):
                        i = mm(bank(m // 4, (m % 4) * 128, (m % 4 + 1) * 128), cwv[:, c, m * 128:(m + 1) * 128], GT[:, c, m, :],
                               c == 0, c == 1)
                    if m % 4 == 3:
                        i.then_inc(kvt_psum, 1)
                for m in range(NM):
                    pe.wait_ge(kvt_ready, 2 * b + m // 4 + 2)
                    i = mm(bank(2 + m // 2, (m % 2) * E, (m % 2 + 1) * E), KVT[:, m, :], cwo[:, m, :], True, True)
                    if m % 2:
                        i.then_inc(m_psum, 1)
                pe.wait_ge(m_act, 4 * (b + 1) + 1)
                pe.wait_ge(m_dve, 4 * (b + 1) + 1)
                pe.wait_ge(vsel_ready, 2 * (T - 1) * (b + 1) + 1)
                pe.sem_inc(waits_alone, 1)
                with pe.Fori(0, T) as t:
                    tile = b * T + t
                    pe.wait_ge(qs_ready, tile + 2)

                    def scores(g):
                        for j in range(HG):
                            u = tile * H + g * HG + j
                            pe.wait_ge(scores_biased, u + 2)
                            mm(bank(j), QS[32 * j:32 * j + HD, g, :], KT[32 * j:32 * j + HD, g, :], True, True)\
                                .then_inc(scores_ready, 1)

                    def transpose_probs(h):
                        u = tile * H + h
                        pe.wait_ge(probs_ready, 4 + u + 2)
                        pe.wait_ge(pt_copied[h % 2], tile * (H // 2) + h // 2 + 1)
                        for k in range(T):
                            i = tr(bank(4 + h % 2, k * 128, (k + 1) * 128),
                                   P[:, (h // HG % 2) * HG + h % HG, PAD + k * 128:PAD + (k + 1) * 128])
                        i.then_inc(transposed, 1)

                    def weigh(h):
                        pe.wait_ge(pt_copied[h % 2], tile * (H // 2) + h // 2 + 2)
                        if h == 0:
                            pe.wait_ge(o_evac, tile + 1)
                        for k in range(T):
                            i = mm(bank(6, h * HD, (h + 1) * HD), PTs[:, h % 2, k * 128:(k + 1) * 128],
                                   Vsel[:, ds(t, 1), k, h * HD:(h + 1) * HD].rearrange("p o e -> p (o e)"),
                                   h == 0 and k == 0, True, skip_group_check=True)
                        i.then_inc(pv_done, 1)

                    for g in range(NG + 1):
                        if g < NG:
                            scores(g)
                        if g:
                            for h in range((g - 1) * HG, g * HG):
                                transpose_probs(h)
                                if h:
                                    weigh(h - 1)
                    weigh(H - 1)
                pe.wait_ge(band_loaded, 16 * T * NG * (b + 1) + 1)
                pe.wait_ge(mass_red, T * NG * (b + 1) + 1)
                pe.wait_ge(scores_biased, 4 + T * H * (b + 1) + 1)

                def transpose_band(t):
                    if t >= 2:
                        pe.wait_ge(fa_act, T * b + t)
                        pe.wait_ge(fa_dve, 2 * (T * b + t - 1) + 1)
                    band = Pband[:, t, :, :].rearrange("p h r -> p (h r)")
                    for c in range(4):
                        i = tr(bank(2 * (t % 2), c * 128, (c + 1) * 128), band[:, c * 128:(c + 1) * 128])
                    i.then_inc(fa_psum, 1)
                    tr(bank(2 * (t % 2) + 1, 0, 128), band[:, 512:640])
                    tr(bank(2 * (t % 2) + 1, 128, 256, H), mass[:, t, :]).then_inc(fa_psum, 1)

                def weigh_band(t):
                    pe.wait_ge(fa_act, T * b + t + 2)
                    pe.wait_ge(fa_dve, 2 * (T * b + t + 1) + 1)
                    if t >= 2:
                        pe.wait_ge(attn_ready, T * b + t)
                    mm(bank(4 + t % 2, 0, E), massT[0:H, t % 2, :], bdr[:], True, True, skip_group_check=True)
                    for c in range(5):
                        i = mm(bank(4 + t % 2, 48 * c, 48 * c + 64), AT[:, t % 2, c, :], bdv[:, c, :], False, True,
                               skip_group_check=True)
                    i.then_inc(f_psum, 1)

                transpose_band(0)
                for t in range(T):
                    if t + 1 < T:
                        transpose_band(t + 1)
                    weigh_band(t)
                pe.wait_ge(o_evac, T * (b + 1) + 1)

                def project(t):
                    pe.wait_ge(aT_ready, T * b + t + 2)
                    if t >= 2:
                        pe.wait_ge(x1_ready, T * b + t)
                    for c in range(2):
                        i = mm(bank(4 + t % 2, 0, E), aT[:, t % 2, c, :], wo_s[:, c, :], c == 0, c == 1)
                    i.then_inc(wo_psum, 1)

                for t in range(T):
                    pe.wait_ge(attn_ready, T * b + t + 2)
                    if t >= 2:
                        pe.wait_ge(aT_ready, T * b + t)
                    for c in range(2):
                        i = tr(bank(6 + t % 2, c * 128, (c + 1) * 128), Oraw[:, t, c * 128:(c + 1) * 128])
                    i.then_inc(at_psum, 1)
                pe.wait_ge(attn_ready, T * (b + 1) + 1)
                for t in range(T):
                    project(t)
                for t in range(T):
                    pe.wait_ge(qaff_ready, T * b + t + 2)
                    for c in range(2):
                        i = tr(bank(c, t * 128, (t + 1) * 128), Qn[:, t, c * 128:(c + 1) * 128])
                        if t == T - 1:
                            i.then_inc(qnT_psum, 1)
                pe.wait_ge(qnT_ready, 2 * (b + 1) + 1)

                def project_q(t):
                    if t >= 2:
                        pe.wait_ge(qn_ready, T * b + t)
                    for j in range(2):
                        for c in range(2):
                            i = mm(bank(2 + 2 * (t % 2) + j), QnT[:, c, t * 128:(t + 1) * 128], cwq[:, c, j * 512:(j + 1) * 512],
                                   c == 0, c == 1)
                    i.then_inc(xq_psum, 1)

                def cross(t):
                    pe.wait_ge(qn_ready, T * b + t + 2)
                    if t:
                        pe.wait_ge(qt_act, T * b + t + 1)
                        pe.wait_ge(qt_dve, T * b + t + 1)
                    for m in range(NM):
                        i = tr(bank(6 + m // 4, (m % 4) * 128, (m % 4 + 1) * 128), qn[:, t % 2, m * 128:(m + 1) * 128])
                        if m % 4 == 3:
                            i.then_inc(qt_psum, 1)
                    pe.wait_ge(qt_act, T * b + t + 2)
                    pe.wait_ge(qt_dve, T * b + t + 2)
                    if t >= 2:
                        pe.wait_ge(y_ready, T * b + t)
                    for m in range(NM):
                        i = mm(bank(t % 2, 0, E), qnT[:, m, :], M[:, m, :], m == 0, m == NM - 1)
                    i.then_inc(o_psum, 1)

                project_q(0)
                project_q(1)
                for t in range(T):
                    if t + 2 < T:
                        project_q(t + 2)
                    cross(t)
                for t in range(T):
                    pe.wait_ge(yaff_ready, T * b + t + 2)
                    for c in range(2):
                        i = tr(bank(2 + c, t * 128, (t + 1) * 128), yn[:, t, c * 128:(c + 1) * 128])
                        if t == T - 1:
                            i.then_inc(ynT_psum, 1)
                pe.wait_ge(ynT_ready, 2 * (b + 1) + 1)
                for f in range(NF):
                    if f >= 4:
                        pe.wait_ge(h_ready, NF * b + f - 3 + 1)
                    for c in range(2):
                        i = mm(bank(4 + f % 4), w1[:, c, f * 128:(f + 1) * 128], ynT[:, c, :], c == 0, c == 1)
                    i.then_inc(h_psum, 1)
                pe.wait_ge(h_ready, NF * (b + 1) + 1)
                for t in range(T):
                    if t >= 2:
                        pe.wait_ge(x2_ready, T * b + t)
                    for f in range(NF):
                        i = mm(bank(t % 2, 0, E), hT[:, f, t * 128:(t + 1) * 128], w2[:, f, :], f == 0, f == NF - 1)
                    i.then_inc(m2_psum, 1)
                for t in range(T):
                    pe.wait_ge(quant_out, 2 + NQ0 + b * QPB + t + 2)
                    for c in range(2):
                        i = tr(bank(2 + c, t * 128, (t + 1) * 128), xq[:, t, c * 128:(c + 1) * 128])
                        if t == T - 1:
                            i.then_inc(xqT_psum, 1)
                pe.wait_ge(xqT_ready, 2 * (b + 1) + 1)

                def gate_up(t):
                    if t >= 2:
                        pe.wait_ge(hh_ready, T * b + t)
                    g0 = (t % 2) * 3 * 512
                    for w, o, lo, hi in ((wgT, 0, 0, 512), (wgT, 0, 512, FF), (wuT, FF, 0, 1024 - FF), (wuT, FF, 1024 - FF, FF)):
                        for c in range(2):
                            i = mm(PS[:, g0 + o + lo:g0 + o + hi], xqT[:, c, t * 128:(t + 1) * 128], w[:, c, lo:hi], c == 0, c == 1)
                    i.then_inc(gu_psum, 1)

                def down(t):
                    pe.wait_ge(quant_out, 2 + NQ0 + b * QPB + T + t + 2)
                    if t:
                        pe.wait_ge(ht_act, T * b + t + 1)
                        pe.wait_ge(out_ready, T * b + t + 1)
                    for c in range(NFF):
                        w = min(128, FF - c * 128)
                        i = tr(bank(6 + c // 4, (c % 4) * 128, (c % 4 + 1) * 128, w), hq[:, t % 2, c * 128:c * 128 + w])
                    i.then_inc(ht_psum, 1)
                    pe.wait_ge(ht_act, T * b + t + 2)
                    pe.wait_ge(ht_dve, 2 * (T * b + t + 1) + 1)
                    for c in range(NFF):
                        w = min(128, FF - c * 128)
                        i = mm(bank(7, 256, 512), hqT[0:w, t % 2, c, :], wdT[0:w, c, :], c == 0, c == NFF - 1)
                    i.then_inc(dn_psum, 1)

                gate_up(0)
                gate_up(1)
                gate_up(2)
                for t in range(T):
                    down(t)
                    if t == 0:
                        gate_up(3)


def _arrange(inputs):
    a = {k: np.asarray(v) for k, v in inputs.items()}
    f = np.float32

    def halves(w):
        return np.ascontiguousarray(w.reshape(-1, 128, w.shape[1]).transpose(1, 0, 2))

    def padded(w):
        o = np.zeros((w.shape[0], H, 32), f)
        o[:, :, 0:HD] = w.reshape(-1, H, HD)
        return o.reshape(w.shape[0], H * 32)

    d = {"x": a["x"], "ctx": a["ctx_1024"]}
    d["wq"], d["wk"] = halves(padded(a["L0_attn_Wq"].T)), halves(padded(a["L0_attn_Wk"].T))
    d["wv"], d["wo"] = halves(a["L0_attn_Wv"].T), halves(a["L0_attn_Wo"].T)
    d["cwq"], d["cwk"], d["cwv"] = (halves(a["L0_xattn_" + n]) for n in ("wq", "wk", "wv"))
    d["cwo"], d["w1"], d["w2"] = (halves(a["L0_xattn_" + n]) for n in ("wo", "w1", "w2"))
    for n, w in (("w_gate", a["L0_ffn_w_gate"]), ("w_up", a["L0_ffn_w_up"])):
        d[n] = np.ascontiguousarray(w.reshape(NGR, GR, E).transpose(1, 0, 2))
    d["w_down"] = halves(a["L0_ffn_w_down"])
    rk, rv = a["L0_attn_rel_k"], a["L0_attn_rel_v"]
    vecs = [a["L0_attn_bv"], a["L0_attn_bo"], a["L0_xattn_ln1_g"], a["L0_xattn_ln1_b"], a["L0_xattn_bo"],
            a["L0_xattn_ln2_g"], a["L0_xattn_ln2_b"], a["L0_xattn_b2"], np.tile(rv[BAND], H)]
    d["rows"] = np.ascontiguousarray(np.broadcast_to(np.stack(vecs)[None], (128, 9, E)))
    d["cols"] = np.concatenate([padded(a["L0_attn_bq"][None]).reshape(4, 128).T, padded(a["L0_attn_bk"][None]).reshape(4, 128).T,
                                a["L0_xattn_b1"].reshape(8, 128).T], axis=1)

    def tables(kt, vt):
        bk = np.zeros((128, HG, NREL), f)
        for j in range(HG):
            bk[32 * j:32 * j + HD, j, :] = kt.T
        bv = np.zeros((H, BAND, H, HD), f)
        br = np.zeros((H, H, HD), f)
        for h in range(H):
            bv[h, :, h, :] = vt[0:BAND]
            br[h, h, :] = vt[BAND]
        bv = bv.reshape(5, 128, E)
        bv = np.stack([bv[c][:, 48 * c:48 * c + 64] for c in range(5)], axis=1)
        return bk.reshape(128, HG * NREL), bv, br.reshape(H, E)

    d["bdk"], d["bdv"], d["bdr"] = tables(rk, rv)
    k0, v0, r0 = tables(np.broadcast_to(rk[0:1], rk.shape), np.broadcast_to(rv[0:1], rv.shape))
    rel0 = np.zeros((128, TAB0), f)
    o = HG * NREL
    rel0[:, 0:o] = k0
    rel0[:, o:o + 320] = v0.reshape(128, 320)
    rel0[0:H, o + 320:o + 320 + E] = r0
    rel0[:, o + 320 + E:o + 320 + 2 * E] = np.tile(rv[0], H)
    d["rel0"] = rel0
    p = np.arange(128)[:, None]
    d["ident"] = np.eye(128, dtype=f)
    d["right_mask"] = (np.arange(384 + S)[None] - 384 >= p + MAX_REL).astype(f)
    c = np.arange(128)[None] + MAX_REL
    right = (c >= p + MAX_REL).astype(f)
    d["mass_mask"] = np.where(c < 128, right, right - 1).astype(f)
    d["pair_mask"] = (np.arange(128)[None] // XD == p // XD).astype(f)
    return {k: np.ascontiguousarray(v) for k, v in d.items()}


def kernel(**inputs):
    import concourse.bacc as bacc
    import concourse.bass as bass
    from concourse import mybir
    from concourse.bass_utils import run_bass_kernel_spmd

    nc = bacc.Bacc("TRN2", target_bir_lowering=False, num_devices=1)
    arrays = _arrange(inputs)
    d = {k: nc.dram_tensor("in_" + k, v.shape, mybir.dt.from_np(v.dtype), kind="ExternalInput").ap() for k, v in arrays.items()}
    for k in ("bias_scr", "prob_scr"):
        d[k] = nc.dram_tensor(k, [T, H, REGION], mybir.dt.float32, kind="Internal").ap()
    out = nc.dram_tensor("out", [NB, S, E], mybir.dt.float32, kind="ExternalOutput").ap()
    build(nc, bass, mybir, d, out)
    r = run_bass_kernel_spmd(nc, [{"in_" + k: v for k, v in arrays.items()}], core_ids=[0])
    return r.results[0]["out"]
```

```python
import numpy as np

NB, S, E, H, HD = 8, 512, 256, 16, 16
T = S // 128
MAX_REL = 20
BAND = 2 * MAX_REL
NREL = BAND + 1
PAD = MAX_REL
ROW = PAD + S + PAD
WIN = 128 + BAND
SKEW = WIN + 1
REGION = 128 * SKEW
CTX = 1601
CT = (CTX + 127) // 128
CLAST = CTX - (CT - 1) * 128
XH, XD = 16, 64
INNER = XH * XD
NM = INNER // 128
MLP = 1024
NF = MLP // 128
FF = 704
NFF = (FF + 127) // 128
FLAST = FF - (NFF - 1) * 128
QB = 16
EPS = 1e-5
HG = 4
NG = H // HG
GR = 88
NGR = FF // GR
BIG = 3.0e38
ARENA = 25952
HC = H // 2
TAB0 = HC * NREL + 5 * 64 + 3 * E
START_MEMSETS = 3
PARTS = 3
SLOTS_Q = (0, 0, 0, 1, 1, 1, 2, 2)
SLOTS_K = (0, 1, 2, 0, 1, 2, 0, 1)
OWN = {"dve_start": 110, "dve_prep": 8, "dve_norm": 2, "dve_scale": 1, "dve_attn": 9, "dve_tail": 124,
       "pool_start": 10, "pool_affine": 1, "pool_fill": 1, "pool_tail": 20}


def build(nc, bass, mybir, d, out):
    from contextlib import ExitStack
    f32, bf16 = mybir.dt.float32, mybir.dt.bfloat16
    ALU, ACT, AX = mybir.AluOpType, mybir.ActivationFunctionType, mybir.AxisListType
    ds = bass.ds
    ctx = ExitStack()
    with ctx:
        def sb(name, shape, dt=f32):
            return ctx.enter_context(nc.sbuf_tensor(name, shape, dt))

        starts = []

        def sem(name, start=1):
            made = ctx.enter_context(nc.semaphore(name))
            starts.append((made, start))
            return made

        wq_s, wk_s = sb("wq_s", [128, 2, E]), sb("wk_s", [128, 2, E])
        wv_s, wo_s = sb("wv_s", [128, 2, E]), sb("wo_s", [128, 2, E])
        cwq, cwk, cwv = sb("cwq", [128, 2, INNER]), sb("cwk", [128, 2, INNER]), sb("cwv", [128, 2, INNER])
        cwo, w1, w2 = sb("cwo", [128, NM, E]), sb("w1", [128, 2, MLP]), sb("w2", [128, NF, E])
        rows = sb("rows", [128, 9, E])
        V_BV, V_BO, V_G1, V_B1, V_XBO, V_G2, V_B2, V_XB2, V_EDGE = range(9)
        cols = sb("cols", [128, 16])
        ident = sb("ident", [128, 128])
        right_mask = sb("right_mask", [128, 384 + S], bf16)
        mass_mask = sb("mass_mask", [128, 128])
        pair_mask = sb("pair_mask", [128, 128])
        bdk, bdv, bdr = sb("bdk", [128, HC * NREL]), sb("bdv", [128, 5, 64]), sb("bdr", [16, E])
        wgT, wuT, wdT = sb("wgT", [128, 2, FF]), sb("wuT", [128, 2, FF]), sb("wdT", [128, NFF, E])
        zeros = sb("zeros", [128, 512], bf16)
        xin = sb("xin", [128, T, E])
        M = sb("M", [128, NM, E])
        edge = sb("edge", [128, T, H])
        lsum, rl, mass = sb("lsum", [128, T, H]), sb("rl", [128, T, H]), sb("mass", [128, T, H])
        bnst, mv, rstd = sb("bnst", [128, T, 6]), sb("mv", [128, T, 2]), sb("rstd", [128, T])
        mhalf = sb("mhalf", [128, 16])
        ss, rn = sb("ss", [128, 2, 16]), sb("rn", [128, 2, 16])
        am, qsc, qrc, qhs = (sb(n, [128, 2, FF // QB]) for n in ("am", "qsc", "qrc", "qhs"))
        nmax = sb("nmax", [128, HG])
        arena = sb("arena", [128, ARENA])
        used = [0]

        def carve(n, shape, at=None):
            lo = used[0] if at is None else at
            used[0] = lo + n
            assert used[0] <= ARENA, used[0]
            v = arena[:, lo:lo + n]
            if len(shape) == 2:
                return v.rearrange("p (a b) -> p a b", a=shape[0])
            if len(shape) == 3:
                return v.rearrange("p (a b c) -> p a b c", a=shape[0], b=shape[1])
            return v

        Kp = carve(H * S // 2, (H * S // 2,), 0).bitcast(bf16).rearrange("p (h s) -> p h s", h=H)
        Qp = carve(H * 64, (H * 64,)).bitcast(bf16).rearrange("p (h s) -> p h s", h=H)
        Vsel = carve(4096, (T, T, E))
        Rb = carve(T * H * NREL, (T, H, NREL), used[0])
        Pband = carve(T * H * BAND, (T, H, BAND), used[0] - T * H * NREL)
        used[0] += T * H
        xn = carve(1024, (T, E))
        Oraw = xn
        only_attn = used[0]
        Bt = carve(2 * HG * ROW, (2 * HG, ROW))
        Wn = carve(2 * HG * WIN, (2 * HG, WIN))
        P = carve(2 * HG * ROW, (2 * HG, ROW))
        Sb = carve(2 * S, (2, S))
        PTs = carve(2 * 512, (2, 512))
        prod = carve(HG * 128, (HG, 128))
        AT = carve(2 * 640, (2, 5, 128), only_attn)
        massT = carve(2 * 128, (2, 128))
        aT = carve(2 * 256, (2, 2, 128))
        xnT = carve(1024, (2, 512), only_attn)
        cin, Kn = carve(512, (2, E)), carve(1024, (4, E))
        cnT = carve(512, (2, 2, 128))
        csq = carve(1024, (1024,))
        kns_at = used[0]
        kns = carve(4096, (4, INNER))
        QT, KT, Qrest, Krest = (carve(1024, (2, S), kns_at + 1024 * i) for i in range(4))
        qparts, kparts = (carve(PARTS * 512, (PARTS * 512,)).bitcast(bf16).rearrange("p (i c s) -> p i c s", i=PARTS, c=2)
                          for _ in range(2))
        Gs = carve(2048, (NM, E), kns_at + 4096)
        GT = carve(2048, (2, NM, 128), kns_at)
        KVT = carve(1024, (NM, 128))
        Qx, Qn, QnT = carve(1024, (T, E), 0), carve(1024, (T, E)), carve(1024, (2, 512))
        sq = carve(1024, (1024,))
        qn, qnT = carve(2048, (2, INNER)), carve(1024, (NM, 128))
        y, yr = carve(1024, (T, E)), carve(1024, (T, E))
        yn, ynT = Qn, QnT
        hT = carve(4096, (NF, 512))
        x2 = carve(1024, (T, E))
        zf = Qx
        qv, qa, qs, qc, qh = (carve(2 * FF, (2, FF)) for _ in range(5))
        xq, xqT = carve(1024, (T, E)), carve(1024, (2, 512))
        hqT = carve(2 * NFF * 128, (2, NFF, 128), 4096)
        yout = hT[:, 0:2, :].rearrange("p a (b c) -> p (a b) c", b=2)
        gs, hq = carve(2 * FF, (2, FF), 9216 + 1024), carve(2 * FF, (2, FF))

        raw_wg = carve(NGR * E, (NGR, E), H * SKEW)
        raw_wu = carve(NGR * E, (NGR, E))
        raw_wd = carve(2 * FF, (2, FF))
        qw = carve(2 * FF, (2, FF))
        rel0 = carve(TAB0, (TAB0,))
        mask32 = carve(384 + S, (384 + S,))

        PS = ctx.enter_context(nc.psum_tensor("PS", [128, 8 * 512], f32))

        def bank(i, lo=0, hi=512, parts=128):
            return PS[0:parts, i * 512 + lo:i * 512 + hi]

        bias_scr, prob_scr, q_scr, k_scr = d["bias_scr"], d["prob_scr"], d["q_scr"], d["k_scr"]

        waits_alone = sem("waits_alone")
        consts_loaded = sem("consts_loaded")
        attn_w_loaded = sem("attn_w_loaded")
        ctx_w_loaded = sem("ctx_w_loaded")
        ffn_w_loaded = sem("ffn_w_loaded")
        zeros_stored = sem("zeros_stored")
        setup_pool = sem("setup_pool")
        tables_ready = sem("tables_ready")
        dve_start = sem("dve_start")
        dve_prep = sem("dve_prep")
        dve_norm = sem("dve_norm")
        dve_scale = sem("dve_scale")
        dve_attn = sem("dve_attn")
        dve_tail = sem("dve_tail")
        pool_start = sem("pool_start")
        pool_affine = sem("pool_affine")
        pool_fill = sem("pool_fill")
        pool_tail = sem("pool_tail")
        x_var = sem("x_var")
        x_rstd = sem("x_rstd")
        c_var = sem("c_var")
        c_rstd = sem("c_rstd")
        c_norm = sem("c_norm")
        c_rnorm = sem("c_rnorm")
        t_var = sem("t_var")
        t_rstd = sem("t_rstd")
        q_norm = sem("q_norm")
        q_rnorm = sem("q_rnorm")
        x_loaded = sem("x_loaded")
        xn_ready = sem("xn_ready")
        xnT_psum = sem("xnT_psum")
        xnT_ready = sem("xnT_ready")
        k_psum = sem("k_psum")
        kT_ready = sem("kT_ready")
        q_psum = sem("q_psum")
        qT_ready = sem("qT_ready")
        v_psum = sem("v_psum")
        v_ready = sem("v_ready")
        vsel_ready = sem("vsel_ready")
        r_psum = sem("r_psum")
        r_act = sem("r_act")
        r_dve = sem("r_dve")
        e_ready = sem("e_ready")
        xb_ready = sem("xb_ready")
        bias_stored = sem("bias_stored")
        ctx_loaded = [sem("ctx_loaded0"), sem("ctx_loaded1")]
        cz_ready = sem("cz_ready", 5)
        caff_ready = sem("caff_ready", 5)
        ct_psum = sem("ct_psum", 5)
        ct_ready = sem("ct_ready", 5)
        ck_psum = sem("ck_psum", 5)
        kc_ready = sem("kc_ready", 5)
        csq_ready = sem("csq_ready", 5)
        cs_ready = sem("cs_ready", 5)
        cg_done = sem("cg_done", 5)
        g_act = sem("g_act")
        g_dve = sem("g_dve")
        gt_psum = sem("gt_psum")
        gt_act = sem("gt_act")
        gt_dve = sem("gt_dve")
        kvt_psum = sem("kvt_psum")
        kvt_ready = sem("kvt_ready")
        m_psum = sem("m_psum")
        m_act = sem("m_act")
        m_dve = sem("m_dve")
        part0_ready = sem("part0_ready")
        rest_ready = sem("rest_ready")
        part1_ready = sem("part1_ready")
        part2_ready = sem("part2_ready")
        parts_stored = sem("parts_stored")
        k_loaded = sem("k_loaded")
        q_loaded = [sem(f"q_loaded{g}") for g in range(NG)]
        scores_ready = sem("scores_ready")
        scores_biased = sem("scores_biased", 5)
        bias_filled = sem("bias_filled", 3)
        win_loaded = [sem("win_loaded0"), sem("win_loaded1")]
        probs_ready = sem("probs_ready", 5)
        p_stored = [sem("p_stored0"), sem("p_stored1")]
        transposed = sem("transposed", 5)
        pt_copied = [sem("pt_act"), sem("pt_dve")]
        pv_done = sem("pv_done", 3)
        o_evac = sem("o_evac")
        mass_mul = sem("mass_mul", 3)
        mass_red = sem("mass_red")
        band_loaded = sem("band_loaded")
        fa_psum = sem("fa_psum")
        fa_act = sem("fa_act")
        fa_dve = sem("fa_dve")
        f_psum = sem("f_psum")
        attn_ready = sem("attn_ready")
        at_psum = sem("at_psum")
        aT_ready = sem("aT_ready")
        wo_psum = sem("wo_psum")
        x1_ready = sem("x1_ready")
        rl_ready = sem("rl_ready")
        qx_ready = sem("qx_ready")
        qz_ready = sem("qz_ready")
        qaff_ready = sem("qaff_ready")
        qnT_psum = sem("qnT_psum")
        qnT_ready = sem("qnT_ready")
        xq_psum = sem("xq_psum")
        sq_ready = sem("sq_ready")
        qn_ready = sem("qn_ready")
        qt_psum = sem("qt_psum")
        qt_act = sem("qt_act")
        qt_dve = sem("qt_dve")
        o_psum = sem("o_psum")
        y_res = sem("y_res")
        y_ready = sem("y_ready")
        yz_ready = sem("yz_ready")
        yaff_ready = sem("yaff_ready")
        ynT_psum = sem("ynT_psum")
        ynT_ready = sem("ynT_ready")
        h_psum = sem("h_psum")
        h_ready = sem("h_ready")
        y2_res = sem("y2_res")
        m2_psum = sem("m2_psum")
        x2_ready = sem("x2_ready")
        zf_ready = sem("zf_ready")
        quant_scaled = sem("quant_scaled")
        quant_v = sem("quant_v")
        quant_a = sem("quant_a")
        quant_c = sem("quant_c")
        quant_out = sem("quant_out", 3)
        qwT_psum = sem("qwT_psum")
        qwT_ready = sem("qwT_ready")
        xqT_psum = sem("xqT_psum")
        xqT_ready = sem("xqT_ready")
        gu_psum = sem("gu_psum")
        silu_ready = sem("silu_ready")
        hh_ready = sem("hh_ready")
        ht_psum = sem("ht_psum")
        ht_act = sem("ht_act")
        ht_dve = sem("ht_dve")
        dn_psum = sem("dn_psum")
        out_ready = sem("out_ready")
        out_stored = sem("out_stored")

        class Steps:
            def __init__(self, which, name, turn=0):
                self.sem, self.name, self.n, self.base = which, name, 0, turn * OWN[name]

            def __call__(self, ins):
                self.n += 1
                return ins.then_inc(self.sem, 1)

            def all(self):
                return self.base + self.n + 1

            def close(self):
                assert self.n == OWN[self.name], (self.name, self.n)

        def bcast(v, n):
            return v.unsqueeze(2).broadcast_to([v.shape[0], v.shape[1], n])

        def root(pool, x, start, done, n):
            pool.wait_ge(start, n + 1)
            pool.sem_inc(waits_alone, 1)
            pool.tensor_tensor(x, x, mhalf[0:x.shape[0], 0:x.shape[1]], ALU.pow).then_inc(done, 1)

        def layernorm(eng, st, srcs, outs, done, var, inv, turn, parts=128):
            n = len(srcs)
            for i, x in enumerate(srcs):
                st(eng.bn_stats(bnst[0:parts, i, :], x))
            eng.wait_ge(st.sem, st.all())
            eng.sem_inc(waits_alone, 1)
            for i in range(n):
                st(eng.bn_aggr(mv[0:parts, i, :], bnst[0:parts, i, :]))
            eng.wait_ge(st.sem, st.all())
            eng.tensor_scalar(rstd[0:parts, 0:n], mv[0:parts, 0:n, 1], EPS, None, ALU.add).then_inc(var, 1)
            eng.wait_ge(inv, turn + 1)
            for i, x in enumerate(srcs):
                eng.tensor_scalar(outs[i], x, mv[0:parts, i, 0:1], rstd[0:parts, i:i + 1],
                                  ALU.subtract, ALU.mult).then_inc(done, 1)

        def quant_scale(eng, st, X, p, parts, n, k):
            nb = n // QB
            eng.wait_ge(quant_out, k + 2)
            st(eng.tensor_reduce(am[0:parts, p, 0:nb], X.rearrange("p (b c) -> p b c", c=QB), AX.X, ALU.max,
                                 apply_absolute_value=True))
            eng.wait_ge(st.sem, st.all())
            st(eng.tensor_scalar(qsc[0:parts, p, 0:nb], am[0:parts, p, 0:nb], 1.0 / 6.0, 1e-12, ALU.mult, ALU.max))
            eng.wait_ge(st.sem, st.all())
            st(eng.tensor_scalar(qhs[0:parts, p, 0:nb], qsc[0:parts, p, 0:nb], 0.5, None, ALU.mult))
            st(eng.reciprocal(qrc[0:parts, p, 0:nb], qsc[0:parts, p, 0:nb]))
            eng.wait_ge(st.sem, st.all())
            eng.tensor_tensor(qv[0:parts, p, 0:n].rearrange("p (b c) -> p b c", c=QB),
                              X.rearrange("p (b c) -> p b c", c=QB), bcast(qrc[0:parts, p, 0:nb], QB),
                              ALU.mult).then_inc(quant_v, 1)

        def quant_abs(eng, p, parts, n, k):
            eng.wait_ge(quant_v, k + 2)
            eng.activation(qa[0:parts, p, 0:n], qv[0:parts, p, 0:n], ACT.Abs).then_inc(quant_a, 1)
            eng.activation(qs[0:parts, p, 0:n], qv[0:parts, p, 0:n], ACT.Sign).then_inc(quant_a, 1)

        def quant_count(eng, st, p, parts, n, k):
            a, c, t = qa[0:parts, p, 0:n], qc[0:parts, p, 0:n], qv[0:parts, p, 0:n]
            eng.wait_ge(quant_a, 2 * k + 3)
            st(eng.tensor_scalar(c, a, 5.0, 2.0, ALU.is_gt, ALU.mult))
            st(eng.tensor_scalar(t, a, 0.25, None, ALU.is_gt))
            eng.wait_ge(st.sem, st.all())
            for m in (3.5, 2.5):
                st(eng.scalar_tensor_tensor(c, a, m, c, ALU.is_gt, ALU.add))
                eng.wait_ge(st.sem, st.all())
            st(eng.scalar_tensor_tensor(c, c, 2.0, t, ALU.mult, ALU.add))
            eng.wait_ge(st.sem, st.all())
            for m in (1.75, 1.25):
                st(eng.scalar_tensor_tensor(c, a, m, c, ALU.is_gt, ALU.add))
                eng.wait_ge(st.sem, st.all())
            eng.scalar_tensor_tensor(c, a, 0.75, c, ALU.is_gt, ALU.add).then_inc(quant_c, 1)

        def quant_finish(eng, st, X, p, parts, n, k):
            nb = n // QB
            eng.wait_ge(quant_a, 2 * k + 3)
            st(eng.tensor_tensor(qh[0:parts, p, 0:n].rearrange("p (b c) -> p b c", c=QB),
                                 qs[0:parts, p, 0:n].rearrange("p (b c) -> p b c", c=QB),
                                 bcast(qhs[0:parts, p, 0:nb], QB), ALU.mult))
            eng.wait_ge(quant_c, k + 2)
            eng.wait_ge(st.sem, st.all())
            eng.tensor_tensor(X, qc[0:parts, p, 0:n], qh[0:parts, p, 0:n], ALU.mult).then_inc(quant_out, 1)

        wjobs = [("g", GR, 2 * E, i) for i in range(NGR // 2)] + [("u", GR, 2 * E, i) for i in range(NGR // 2)] \
            + [("d", 128, FF, i) for i in range(2)]
        NQ0 = len(wjobs)
        QPB = 2 * T

        def wsrc(kind, i):
            if kind == "d":
                return raw_wd[:, i, :]
            return (raw_wg if kind == "g" else raw_wu)[0:GR, 2 * i:2 * i + 2, :].rearrange("p a b -> p (a b)")

        def ctx_tiles(eng, body):
            with eng.Fori(0, CMAIN // 4) as it:
                for q in range(4):
                    body(4 * it + q, q)
            for i in range(CMAIN, CT):
                body(i, i % 4)

        CMAIN = (CT - 2) // 4 * 4
        AHEAD = HG

        CSTEP = CT + 3

        def cdone(b, i):
            return b * CSTEP + i + 5

        def is_last(i):
            return isinstance(i, int) and i == CT - 1

        def crows(i):
            return CLAST if is_last(i) else 128

        def cinc(i):
            return 4 if is_last(i) else 1

        def exists(i):
            return not isinstance(i, int) or i < CT

        with nc.Block() as first:
            @first.sync
            def _(sp):
                for which, value in starts:
                    sp.sem_inc(which, value)

        block = ctx.enter_context(nc.Block())

        @block.sync
        def _(sp):
            n_attn = 0
            for dst, src in ((ident, "ident"), (mass_mask, "mass_mask"), (pair_mask, "pair_mask"),
                             (rows, "rows"), (cols, "cols"), (bdk, "bdk"), (bdv, "bdv"), (bdr, "bdr")):
                sp.dma_start(dst[:], d[src]).then_inc(consts_loaded, 16)
            sp.dma_start(rel0, d["rel0"]).then_inc(consts_loaded, 16)
            sp.dma_start(mask32, d["right_mask"]).then_inc(consts_loaded, 16)
            for dst, src in ((raw_wg[0:GR], "w_gate"), (raw_wu[0:GR], "w_up"), (raw_wd[:], "w_down")):
                sp.dma_start(dst, d[src]).then_inc(ffn_w_loaded, 16)
            for dst, src in ((wq_s, "wq"), (wk_s, "wk"), (wv_s, "wv"), (wo_s, "wo")):
                sp.dma_start(dst[:], d[src]).then_inc(attn_w_loaded, 16)
            for dst, src in ((cwk, "cwk"), (cwv, "cwv"), (cwo, "cwo"), (cwq, "cwq"), (w1, "w1"), (w2, "w2")):
                sp.dma_start(dst[:], d[src]).then_inc(ctx_w_loaded, 16)
            sp.wait_ge(setup_pool, START_MEMSETS + 1)
            for t in range(T):
                sp.dma_start(bias_scr[t].rearrange("h (p r) -> p h r", r=SKEW),
                             arena[:, 0:H * SKEW].rearrange("p (h r) -> p h r", r=SKEW)).then_inc(zeros_stored, 16)
            sp.wait_ge(zeros_stored, 16 * T + 1)
            with sp.Fori(0, NB) as b:
                sp.wait_ge(y2_res, T * b + 1)
                sp.sem_inc(waits_alone, 1)
                sp.dma_start(xin[:], d["x"][ds(b, 1)].rearrange("o (t p) e -> p (o t) e", p=128)).then_inc(x_loaded, 16)
                def load_ctx(i, q):
                    n, p = crows(i), q % 2
                    sp.wait_ge(caff_ready, cdone(b, i - 2) + 1)
                    sp.sem_inc(waits_alone, 1)
                    sp.dma_start(cin[0:n, p, :], d["ctx"][ds(b, 1), ds(i * 128, n), :].rearrange("o p e -> (o p) e"))\
                        .then_inc(ctx_loaded[p], 16)

                sp.wait_ge(xnT_ready, 2 * (b + 1) + 1)
                sp.sem_inc(waits_alone, 1)
                load_ctx(0, 0)
                load_ctx(1, 1)
                for t in range(T):
                    sp.wait_ge(r_act, T * b + t + 2)
                    sp.sem_inc(waits_alone, 1)
                    sp.wait_ge(r_dve, T * b + t + 2)
                    sp.sem_inc(waits_alone, 1)
                    sp.dma_start(bias_scr[t].rearrange("h (p r) -> p h r", r=SKEW)[:, :, 0:BAND],
                                 Rb[:, t, :, 0:BAND]).then_inc(bias_stored, 16)
                sp.wait_ge(part1_ready, 2 * (b + 1) + 1)
                sp.sem_inc(waits_alone, 1)
                sp.wait_ge(part2_ready, 2 * (b + 1) + 1)
                sp.sem_inc(waits_alone, 1)
                for parts, scr in ((qparts, q_scr), (kparts, k_scr)):
                    for i in range(PARTS):
                        sp.dma_start(scr[i].rearrange("(c r) s -> r c s", c=2), parts[:, i, :, :]).then_inc(parts_stored, 16)

                def more_ctx(i, q):
                    if exists(i + 2):
                        load_ctx(i + 2, q)
                ctx_tiles(sp, more_ctx)
                sp.wait_ge(parts_stored, 16 * 2 * PARTS * (b + 1) + 1)
                sp.sem_inc(waits_alone, 1)

                def load_q(t, g):
                    for slot, part in enumerate(SLOTS_Q):
                        sp.dma_start(Qp[slot * HD:(slot + 1) * HD, g * HG:(g + 1) * HG, :],
                                     q_scr[part, g * HG * HD:(g + 1) * HG * HD, ds(t * 128, 128)]
                                     .rearrange("(h d) s -> d h s", d=HD)).then_inc(q_loaded[g], 16)

                for slot, part in enumerate(SLOTS_K):
                    sp.dma_start(Kp[slot * HD:(slot + 1) * HD, :, :], k_scr[part].rearrange("(h d) s -> d h s", d=HD))\
                        .then_inc(k_loaded, 16)
                for g in range(NG):
                    load_q(0, g)
                sp.wait_ge(bias_stored, 16 * T * (b + 1) + 1)
                sp.sem_inc(waits_alone, 1)
                sp.wait_ge(e_ready, b + 2)
                sp.sem_inc(waits_alone, 1)
                sp.wait_ge(m_dve, 4 * (b + 1) + 1)
                sp.sem_inc(waits_alone, 1)
                sp.wait_ge(m_act, 4 * (b + 1) + 1)
                sp.sem_inc(waits_alone, 1)

                def load_window(t, g):
                    m = (b * T + t) * NG + g
                    sp.wait_ge(bias_filled, m + 2)
                    sp.sem_inc(waits_alone, 1)
                    sp.dma_start(Wn[:, (g % 2) * HG:(g % 2 + 1) * HG, :],
                                 bias_scr[ds(t, 1), g * HG:(g + 1) * HG, 0:128 * WIN]
                                 .rearrange("o h (p r) -> p (o h) r", r=WIN)).then_inc(win_loaded[g % 2], 16)

                def store_probs(t, g):
                    sp.wait_ge(probs_ready, 4 + (b * T + t) * H + (g + 1) * HG + 1)
                    sp.sem_inc(waits_alone, 1)
                    sp.dma_start(prob_scr[ds(t, 1), g * HG:(g + 1) * HG, 0:128 * WIN]
                                 .rearrange("o h (p r) -> p (o h) r", r=WIN),
                                 P[:, (g % 2) * HG:(g % 2 + 1) * HG, ds(t * 128, WIN)]).then_inc(p_stored[g % 2], 16)

                def load_band(t, g):
                    sp.wait_ge(p_stored[g % 2], 16 * ((b * T + t) * 2 + g // 2 + 1) + 1)
                    sp.sem_inc(waits_alone, 1)
                    sp.dma_start(Pband[:, ds(t, 1), g * HG:(g + 1) * HG, :].rearrange("p o h r -> p (o h) r"),
                                 prob_scr[ds(t, 1), g * HG:(g + 1) * HG, :]
                                 .rearrange("o h (p r) -> p (o h) r", r=SKEW)[:, :, 0:BAND]).then_inc(band_loaded, 16)

                def attn_tile(t, last):
                    for g in range(NG):
                        if g + 2 < NG:
                            load_window(t, g + 2)
                        elif not last:
                            load_window(t + 1, g + 2 - NG)
                        if not last:
                            sp.wait_ge(scores_ready, (b * T + t) * H + (g + 1) * HG + 1)
                            sp.sem_inc(waits_alone, 1)
                            load_q(t + 1, g)
                        store_probs(t, g)
                        if g:
                            load_band(t, g - 1)
                    load_band(t, NG - 1)

                load_window(0, 0)
                load_window(0, 1)
                with sp.Fori(0, T - 1) as t:
                    attn_tile(t, False)
                attn_tile(T - 1, True)
                sp.wait_ge(band_loaded, 16 * T * NG * (b + 1) + 1)
                sp.sem_inc(waits_alone, 1)
                for t in range(T):
                    sp.wait_ge(out_ready, T * b + t + 2)
                    sp.sem_inc(waits_alone, 1)
                    sp.dma_start(out[ds(b, 1), t * 128:(t + 1) * 128, :].rearrange("o p e -> (o p) e"),
                                 yout[:, t, :]).then_inc(out_stored, 16)
                sp.wait_ge(out_stored, 16 * T * (b + 1) + 1)
                sp.sem_inc(waits_alone, 1)

        @block.gpsimd
        def _(pool):
            st = Steps(pool_start, "pool_start")
            pool.memset(mhalf[:], -0.5).then_inc(setup_pool, 1)
            pool.memset(zeros[:], 0.0).then_inc(setup_pool, 1)
            pool.memset(arena[:, 0:H * SKEW], 0.0).then_inc(setup_pool, 1)
            pool.wait_ge(consts_loaded, 16 * 10 + 1)
            for k, (kind, parts, n, i) in enumerate(wjobs):
                if k >= 2:
                    pool.wait_ge(qwT_psum, k)
                    pool.sem_inc(waits_alone, 1)
                quant_finish(pool, st, qw[0:parts, k % 2, 0:n], k % 2, parts, n, k)
            st.close()
            pool.wait_ge(tables_ready, 7)
            with pool.Fori(0, NB) as b:
                root(pool, rstd[:, 0:T], x_var, x_rstd, b + 1)
                pool.wait_ge(xn_ready, T * (b + 1) + 1)
                pool.sem_inc(waits_alone, 1)
                pool.tensor_tensor(xin[:], xin[:], rows[:, V_BO:V_BO + 1, :].broadcast_to([128, T, E]), ALU.add)\
                    .then_inc(xb_ready, 1)
                pool.wait_ge(v_ready, 2 * (b + 1) + 1)
                pool.sem_inc(waits_alone, 1)
                for t in range(T - 1):
                    pool.tensor_copy(Vsel[:, t, 0:t + 1, :], Vsel[:, T - 1, 0:t + 1, :]).then_inc(vsel_ready, 1)
                    pool.tensor_tensor(Vsel[:, t, t + 1:T, :], Vsel[:, T - 1, t + 1:T, :],
                                       rows[:, V_EDGE:V_EDGE + 1, :].broadcast_to([128, T - 1 - t, E]), ALU.add)\
                        .then_inc(vsel_ready, 1)
                pool.wait_ge(r_act, T * (b + 1) + 1)
                pool.sem_inc(waits_alone, 1)
                pool.wait_ge(r_dve, T * (b + 1) + 1)
                pool.sem_inc(waits_alone, 1)
                pool.tensor_copy(edge[:], Rb[:, :, :, BAND]).then_inc(e_ready, 1)
                def affine(i, q):
                    n, p = crows(i), q % 2
                    st = Steps(pool_affine, "pool_affine", b * CT + i)
                    root(pool, rstd[0:n, p:p + 1], c_var, c_rstd, b * CT + i + 1)
                    pool.wait_ge(cz_ready, cdone(b, i) + 1)
                    pool.sem_inc(waits_alone, 1)
                    pool.wait_ge(cg_done, cdone(b, i - 4) + 1)
                    pool.sem_inc(waits_alone, 1)
                    st(pool.tensor_tensor(Kn[0:n, q, :], cin[0:n, p, :], rows[0:n, V_G1, :], ALU.mult))
                    pool.wait_ge(st.sem, st.all())
                    pool.sem_inc(waits_alone, 1)
                    pool.tensor_tensor(Kn[0:n, q, :], Kn[0:n, q, :], rows[0:n, V_B1, :], ALU.add)\
                        .then_inc(caff_ready, cinc(i))
                    st.close()

                def norm_root(i, q):
                    root(pool, rn[0:crows(i), q % 2, :], c_norm, c_rnorm, b * CT + i + 1)

                affine(0, 0)
                affine(1, 1)
                affine(2, 2)
                norm_root(0, 0)

                def ctx_pool(i, q):
                    if exists(i + 3):
                        affine(i + 3, (q + 3) % 4)
                    if exists(i + 1):
                        norm_root(i + 1, q + 1)
                ctx_tiles(pool, ctx_pool)

                pool.wait_ge(m_dve, 4 * (b + 1) + 1)
                pool.sem_inc(waits_alone, 1)
                pool.wait_ge(m_act, 4 * (b + 1) + 1)
                pool.sem_inc(waits_alone, 1)
                pool.memset(P[:, :, 0:PAD], 0.0).then_inc(setup_pool, 1)
                pool.memset(P[:, :, PAD + S:ROW], 0.0).then_inc(setup_pool, 1)
                pool.memset(Bt[:, :, 0:PAD], 0.0).then_inc(setup_pool, 1)
                pool.memset(Bt[:, :, PAD + S:ROW], 0.0).then_inc(setup_pool, 1)
                pool.wait_ge(setup_pool, START_MEMSETS + 4 * (b + 1) + 1)
                pool.sem_inc(waits_alone, 1)
                def fill(t, g):
                    m = (b * T + t) * NG + g
                    lo = (g % 2) * HG
                    stt = Steps(pool_fill, "pool_fill", m)
                    pool.wait_ge(scores_biased, m * HG + 1)
                    pool.sem_inc(waits_alone, 1)
                    stt(pool.tensor_tensor(
                        Bt[:, lo:lo + HG, PAD:PAD + S],
                        right_mask[:, ds(384 - t * 128, S)].unsqueeze(1).broadcast_to([128, HG, S]),
                        bcast(edge[:, ds(t, 1), g * HG:(g + 1) * HG].rearrange("p o h -> p (o h)"), S), ALU.mult))
                    pool.wait_ge(stt.sem, stt.all())
                    pool.sem_inc(waits_alone, 1)
                    pool.wait_ge(win_loaded[g % 2], 16 * ((b * T + t) * 2 + g // 2 + 1) + 1)
                    pool.sem_inc(waits_alone, 1)
                    pool.tensor_tensor(Bt[:, lo:lo + HG, ds(t * 128, WIN)], Bt[:, lo:lo + HG, ds(t * 128, WIN)],
                                       Wn[:, lo:lo + HG, :], ALU.add).then_inc(bias_filled, 1)

                def edge_mass(t, g):
                    m = (b * T + t) * NG + g
                    pool.wait_ge(probs_ready, 4 + (m + 1) * HG + 1)
                    pool.sem_inc(waits_alone, 1)
                    pool.wait_ge(mass_red, m + 1)
                    pool.sem_inc(waits_alone, 1)
                    pool.tensor_tensor(prod[:], P[:, (g % 2) * HG:(g % 2 + 1) * HG, ds(t * 128 + BAND, 128)],
                                       mass_mask[:].unsqueeze(1).broadcast_to([128, HG, 128]), ALU.mult)\
                        .then_inc(mass_mul, 1)

                def attn_pool(t, last):
                    for g in range(NG):
                        if g + 2 < NG:
                            fill(t, g + 2)
                        elif not last:
                            fill(t + 1, g + 2 - NG)
                        edge_mass(t, g)

                fill(0, 0)
                fill(0, 1)
                with pool.Fori(0, T - 1) as t:
                    attn_pool(t, False)
                attn_pool(T - 1, True)
                st = Steps(pool_tail, "pool_tail", b)
                root(pool, rstd[:, 0:T], t_var, t_rstd, 4 * b + 1)
                root(pool, rstd[:, 0:T], t_var, t_rstd, 4 * b + 2)
                for t in range(T):
                    pool.wait_ge(qz_ready, T * b + t + 2)
                    pool.sem_inc(waits_alone, 1)
                    st(pool.tensor_tensor(Qn[:, t, :], Qn[:, t, :], rows[:, V_G1, :], ALU.mult))
                    pool.wait_ge(st.sem, st.all())
                    pool.sem_inc(waits_alone, 1)
                    pool.tensor_tensor(Qn[:, t, :], Qn[:, t, :], rows[:, V_B1, :], ALU.add).then_inc(qaff_ready, 1)
                for t in range(T):
                    pool.tensor_tensor(yr[:, t, :], Qx[:, t, :], rows[:, V_XBO, :], ALU.add).then_inc(y_res, 1)
                for t in range(T):
                    root(pool, rn[:, t % 2, :], q_norm, q_rnorm, T * b + t + 1)
                root(pool, rstd[:, 0:T], t_var, t_rstd, 4 * b + 3)
                for t in range(T):
                    pool.wait_ge(yz_ready, T * b + t + 2)
                    pool.sem_inc(waits_alone, 1)
                    st(pool.tensor_tensor(yn[:, t, :], yn[:, t, :], rows[:, V_G2, :], ALU.mult))
                    pool.wait_ge(st.sem, st.all())
                    pool.sem_inc(waits_alone, 1)
                    pool.tensor_tensor(yn[:, t, :], yn[:, t, :], rows[:, V_B2, :], ALU.add).then_inc(yaff_ready, 1)
                for t in range(T):
                    st(pool.tensor_tensor(yr[:, t, :], y[:, t, :], rows[:, V_XB2, :], ALU.add))
                    pool.wait_ge(st.sem, st.all())
                    pool.sem_inc(waits_alone, 1)
                    pool.tensor_tensor(yr[:, t, :], yr[:, t, :], xin[:, t, :], ALU.add).then_inc(y2_res, 1)
                root(pool, rstd[:, 0:T], t_var, t_rstd, 4 * b + 4)
                for t in range(T):
                    k = NQ0 + b * QPB + t
                    quant_finish(pool, st, xq[:, t, :], t % 2, 128, E, k)
                for t in range(T):
                    k = NQ0 + b * QPB + T + t
                    if t >= 2:
                        pool.wait_ge(ht_psum, T * b + t)
                        pool.sem_inc(waits_alone, 1)
                    quant_finish(pool, st, hq[:, t % 2, :], t % 2, 128, FF, k)
                st.close()

        @block.scalar
        def _(act):
            for k, (kind, parts, n, i) in enumerate(wjobs):
                quant_abs(act, k % 2, parts, n, k)
            with act.Fori(0, NB) as b:
                act.wait_ge(xnT_psum, 2 * b + 2)
                act.sem_inc(waits_alone, 1)
                act.activation(xnT[:, 0, :], bank(0), ACT.Copy).then_inc(xnT_ready, 1)
                for c in range(2):
                    act.wait_ge(k_psum, 2 * b + c + 2)
                    act.activation(KT[:, c, :], bank(2 + c), ACT.Identity, bias=cols[:, 2 + c:3 + c]).then_inc(kT_ready, 1)
                for j in range(2):
                    act.wait_ge(v_psum, 2 * b + j + 2)
                    act.activation(Vsel[:, T - 1, 2 * j:2 * j + 2, :].rearrange("p a b -> p (a b)"), bank(6 + j), ACT.Copy)\
                        .then_inc(v_ready, 1)
                act.wait_ge(kT_ready, 2 * (b + 1) + 1)
                act.activation(kparts[:, 0], KT[:], ACT.Copy).then_inc(part0_ready, 1)
                act.wait_ge(qT_ready, 2 * (b + 1) + 1)
                act.activation(qparts[:, 0], QT[:], ACT.Copy).then_inc(part0_ready, 1)
                act.wait_ge(out_stored, 16 * T * b + 1)
                for t in range(T):
                    act.wait_ge(r_psum, 8 * b + 2 * t + 2)
                    act.activation(Rb[:, t, 0:8, :].rearrange("p h r -> p (h r)"), bank(4 + 2 * t % 4, 0, 8 * NREL), ACT.Copy)\
                        .then_inc(r_act, 1)

                for i, (parts, rest) in enumerate(((kparts, Krest), (qparts, Qrest))):
                    act.wait_ge(rest_ready, 2 * b + i + 2)
                    act.activation(parts[:, 1], rest[:], ACT.Copy).then_inc(part1_ready, 1)
                act.wait_ge(part2_ready, 2 * (b + 1) + 1)

                def copy_ct(i, p):
                    n = crows(i)
                    act.wait_ge(ct_psum, cdone(b, i) + 1)
                    act.wait_ge(ck_psum, cdone(b, i - 2) + 1)
                    act.activation(cnT[:, p, :, 0:n],
                                   bank(6 + p, 0, 256).rearrange("p (c t) -> p c t", c=2)[:, :, 0:n], ACT.Copy)\
                        .then_inc(ct_ready, cinc(i))

                def copy_k(i, q):
                    n = crows(i)
                    act.wait_ge(ck_psum, cdone(b, i) + 1)
                    act.wait_ge(cg_done, cdone(b, i - 4) + 1)
                    act.activation(kns[0:n, q, :], PS[0:n, 4 * 512:6 * 512], ACT.Copy).then_inc(kc_ready, cinc(i))

                def square(i, q):
                    n = crows(i)
                    act.wait_ge(kc_ready, cdone(b, i) + 1)
                    act.wait_ge(c_norm, b * CT + i + 1)
                    act.activation(csq[0:n], kns[0:n, q, :], ACT.Square).then_inc(csq_ready, cinc(i))

                copy_ct(0, 0)
                copy_ct(1, 1)
                copy_k(0, 0)
                square(0, 0)
                copy_ct(2, 0)
                copy_k(1, 1)
                square(1, 1)

                def ctx_act(i, q):
                    if exists(i + 2):
                        copy_k(i + 2, (q + 2) % 4)
                    if exists(i + 3):
                        copy_ct(i + 3, (q + 3) % 2)
                    if exists(i + 2):
                        square(i + 2, (q + 2) % 4)
                ctx_tiles(act, ctx_act)
                act.wait_ge(cg_done, cdone(b, CT - 1) + 1)
                act.wait_ge(parts_stored, 16 * 2 * PARTS * (b + 1) + 1)
                for j in (0, 2):
                    act.activation(Gs[:, 2 * j:2 * j + 2, :].rearrange("p a b -> p (a b)"), bank(j), ACT.Copy).then_inc(g_act, 1)
                for c in range(2):
                    act.wait_ge(gt_psum, 4 * b + 2 * c + 2)
                    act.activation(GT[:, c, 0:4, :].rearrange("p a b -> p (a b)"), bank(4 + 2 * c), ACT.Copy).then_inc(gt_act, 1)
                for j in (0, 2):
                    act.wait_ge(m_psum, 4 * b + j + 2)
                    act.activation(M[:, 2 * j:2 * j + 2, :].rearrange("p a b -> p (a b)"), bank(2 + j), ACT.Copy)\
                        .then_inc(m_act, 2)
                act.wait_ge(m_dve, 4 * (b + 1) + 1)
                act.wait_ge(setup_pool, START_MEMSETS + 4 * (b + 1) + 1)
                def exps(t, h):
                    g, j = divmod(h, HG)
                    tile = b * T + t
                    u, m = tile * H + h, tile * NG + g
                    if j == 0:
                        act.wait_ge(transposed, m * HG + 1)
                        act.wait_ge(mass_mul, m + 2)
                        act.wait_ge(p_stored[g % 2], 16 * (tile * 2 + g // 2) + 1)
                    act.wait_ge(scores_biased, 4 + u + 2)
                    act.activation(P[:, (g % 2) * HG + j, PAD:PAD + S], Sb[:, h % 2, :], ACT.Exp, bias=nmax[:, j:j + 1],
                                   scale=-1.0, accum_out=lsum[:, ds(t, 1), h]).then_inc(probs_ready, 1)

                def evac(t, h):
                    act.wait_ge(transposed, 4 + (b * T + t) * H + h + 2)
                    act.wait_ge(pv_done, (b * T + t) * H + h + 2)
                    act.activation(PTs[:, 0, :], bank(4), ACT.Copy).then_inc(pt_copied[0], 1)

                def attn_act(t, last):
                    for h in range(H):
                        if h + AHEAD < H:
                            exps(t, h + AHEAD)
                        elif not last:
                            exps(t + 1, h + AHEAD - H)
                        if h % 2 == 0:
                            evac(t, h)
                    act.wait_ge(pv_done, 2 + (b * T + t + 1) * H + 1)
                    act.activation(Oraw[:, ds(t, 1), :].rearrange("p o e -> p (o e)"), bank(6, 0, E), ACT.Copy).then_inc(o_evac, 1)

                for h in range(AHEAD):
                    exps(0, h)
                with act.Fori(0, T - 1) as t:
                    attn_act(t, False)
                attn_act(T - 1, True)
                for t in range(T):
                    act.wait_ge(fa_psum, 2 * (T * b + t) + 2)
                    if t >= 2:
                        act.wait_ge(f_psum, T * b + t)
                    act.activation(AT[:, t % 2, 0:4, :].rearrange("p a b -> p (a b)"), bank(2 * (t % 2)), ACT.Copy)\
                        .then_inc(fa_act, 1)
                for t in range(T):
                    act.wait_ge(at_psum, T * b + t + 2)
                    if t >= 2:
                        act.wait_ge(wo_psum, T * b + t)
                    act.activation(aT[:, t % 2, :, :].rearrange("p a b -> p (a b)"), bank(6 + t % 2, 0, 256), ACT.Copy)\
                        .then_inc(aT_ready, 1)
                act.wait_ge(qnT_psum, 2 * b + 2)
                act.activation(QnT[:, 0, :], bank(0), ACT.Copy).then_inc(qnT_ready, 1)
                for t in range(T + 1):
                    if t < T:
                        act.wait_ge(xq_psum, T * b + t + 2)
                        if t:
                            act.wait_ge(qn_ready, T * b + t + 1)
                        act.activation(sq, PS[:, (2 + 2 * (t % 2)) * 512:(4 + 2 * (t % 2)) * 512], ACT.Square).then_inc(sq_ready, 1)
                    if t:
                        act.wait_ge(qt_psum, 2 * (T * b + t - 1) + 2)
                        if t >= 2:
                            act.wait_ge(o_psum, T * b + t)
                        act.activation(qnT[:, 0:4, :].rearrange("p a b -> p (a b)"), bank(6), ACT.Copy).then_inc(qt_act, 1)
                act.wait_ge(ynT_psum, 2 * b + 2)
                act.activation(ynT[:, 0, :], bank(2), ACT.Copy).then_inc(ynT_ready, 1)
                for f in range(NF):
                    act.wait_ge(h_psum, NF * b + f + 2)
                    act.activation(hT[:, f, :], bank(4 + f % 4), ACT.Gelu, bias=cols[:, 4 + f:5 + f]).then_inc(h_ready, 1)
                for t in range(T):
                    quant_abs(act, t % 2, 128, E, NQ0 + b * QPB + t)
                act.wait_ge(xqT_psum, 2 * b + 2)
                act.activation(xqT[:, 0, :], bank(2), ACT.Copy).then_inc(xqT_ready, 1)
                for t in range(T + 2):
                    if t < T:
                        act.wait_ge(gu_psum, T * b + t + 2)
                        if t >= 2:
                            act.wait_ge(quant_v, NQ0 + b * QPB + T + t)
                        g0 = (t % 2) * 3 * 512
                        act.activation(gs[:, t % 2, :], PS[:, g0:g0 + FF], ACT.Silu).then_inc(silu_ready, 1)
                    if 1 <= t <= T:
                        quant_abs(act, (t - 1) % 2, 128, FF, NQ0 + b * QPB + T + t - 1)
                    if t >= 2:
                        act.wait_ge(ht_psum, T * b + t)
                        if t >= 4:
                            act.wait_ge(dn_psum, T * b + t - 3 + 1)
                        act.activation(hqT[:, t % 2, 0:4, :].rearrange("p a b -> p (a b)"), bank(6), ACT.Copy)\
                            .then_inc(ht_act, 1)

        @block.vector
        def _(dve):
            st = Steps(dve_start, "dve_start")
            dve.wait_ge(consts_loaded, 16 * 10 + 1)
            dve.sem_inc(waits_alone, 1)
            dve.tensor_copy(right_mask[:], mask32).then_inc(tables_ready, 1)
            o = HC * NREL
            dve.tensor_tensor(bdk[:], bdk[:], rel0[:, 0:o], ALU.subtract).then_inc(tables_ready, 1)
            dve.tensor_tensor(bdv[:].rearrange("p a b -> p (a b)"), bdv[:].rearrange("p a b -> p (a b)"),
                              rel0[:, o:o + 320], ALU.subtract).then_inc(tables_ready, 1)
            o += 320
            dve.tensor_tensor(bdr[:], bdr[:], rel0[0:16, o:o + E], ALU.subtract).then_inc(tables_ready, 1)
            dve.tensor_tensor(rows[:, V_EDGE, :], rows[:, V_EDGE, :], rel0[:, o + E:o + 2 * E], ALU.subtract)\
                .then_inc(tables_ready, 1)
            dve.tensor_tensor(rows[:, V_BV, :], rows[:, V_BV, :], rel0[:, o + E:o + 2 * E], ALU.add).then_inc(tables_ready, 1)
            dve.wait_ge(ffn_w_loaded, 16 * 3 + 1)
            def wcopy(k):
                kind, parts, n, i = wjobs[k]
                dve.wait_ge(qwT_psum, k + 2)
                if kind == "d":
                    src = PS[:, 0:1024].rearrange("p (c r) -> p c r", r=128)
                    dve.tensor_copy(wdT[:, 0:5, i * 128:(i + 1) * 128], src[:, 0:5, :]).then_inc(qwT_ready, 1)
                    dve.tensor_copy(wdT[0:FLAST, 5, i * 128:(i + 1) * 128], src[0:FLAST, 5, :]).then_inc(qwT_ready, 1)
                else:
                    dst = wgT if kind == "g" else wuT
                    src = PS[:, 0:1024].rearrange("p (a c r) -> p a c r", a=2, c=4)
                    for a in range(2):
                        dve.tensor_copy(dst[:, :, (2 * i + a) * GR:(2 * i + a + 1) * GR], src[:, a, 0:2, 0:GR]).then_inc(qwT_ready, 1)
            for k, (kind, parts, n, i) in enumerate(wjobs):
                quant_scale(dve, st, wsrc(kind, i), k % 2, parts, n, k)
                if k:
                    _, pp, nn, _ = wjobs[k - 1]
                    quant_count(dve, st, (k - 1) % 2, pp, nn, k - 1)
                if k >= 2:
                    wcopy(k - 2)
            k = len(wjobs)
            quant_count(dve, st, (k - 1) % 2, wjobs[-1][1], wjobs[-1][2], k - 1)
            wcopy(k - 2)
            wcopy(k - 1)
            st.close()
            dve.wait_ge(tables_ready, 7)
            dve.wait_ge(zeros_stored, 16 * T + 1)
            with dve.Fori(0, NB) as b:
                st = Steps(dve_prep, "dve_prep", b)
                dve.wait_ge(x_loaded, 16 * (b + 1) + 1)
                dve.sem_inc(waits_alone, 1)
                layernorm(dve, st, [xin[:, t, :] for t in range(T)], [xn[:, t, :] for t in range(T)], xn_ready,
                          x_var, x_rstd, b + 1)
                dve.wait_ge(xnT_psum, 2 * b + 3)
                dve.tensor_copy(xnT[:, 1, :], bank(1)).then_inc(xnT_ready, 1)
                for c in range(2):
                    dve.wait_ge(q_psum, 2 * b + c + 2)
                    dve.tensor_scalar(QT[:, c, :], bank(4 + c), cols[:, c:c + 1], None, ALU.add).then_inc(qT_ready, 1)
                dve.wait_ge(out_stored, 16 * T * b + 1)
                for t in range(T):
                    dve.wait_ge(r_psum, 8 * b + 2 * t + 3)
                    dve.tensor_copy(Rb[:, t, 8:16, :].rearrange("p h r -> p (h r)"), bank(5 + 2 * t % 4, 0, 8 * NREL))\
                        .then_inc(r_dve, 1)
                for i, (parts, whole, rest) in enumerate(((kparts, KT, Krest), (qparts, QT, Qrest))):
                    dve.wait_ge(part0_ready, 2 * b + i + 2)
                    dve.tensor_tensor(rest[:], whole[:], parts[:, 0], ALU.subtract).then_inc(rest_ready, 1)
                for i, (parts, rest) in enumerate(((kparts, Krest), (qparts, Qrest))):
                    dve.wait_ge(part1_ready, 2 * b + i + 2)
                    dve.tensor_tensor(parts[:, 2], rest[:], parts[:, 1], ALU.subtract).then_inc(part2_ready, 1)
                st.close()

                def norm_stats(i, p):
                    n = crows(i)
                    st = Steps(dve_norm, "dve_norm", b * CT + i)
                    per = (CT + 1) // 2 if p == 0 else CT // 2
                    dve.wait_ge(ctx_loaded[p], 16 * per * b + 8 * (i - p) + 17)
                    st(dve.bn_stats(bnst[0:n, p, :], cin[0:n, p, :]))
                    dve.wait_ge(st.sem, st.all())
                    dve.sem_inc(waits_alone, 1)
                    st(dve.bn_aggr(mv[0:n, p, :], bnst[0:n, p, :]))
                    dve.wait_ge(st.sem, st.all())
                    dve.tensor_scalar(rstd[0:n, p:p + 1], mv[0:n, p, 1:2], EPS, None, ALU.add).then_inc(c_var, 1)
                    st.close()

                def norm_apply(i, p):
                    n = crows(i)
                    x = cin[0:n, p, :]
                    dve.wait_ge(c_rstd, b * CT + i + 2)
                    dve.tensor_scalar(x, x, mv[0:n, p, 0:1], rstd[0:n, p:p + 1], ALU.subtract, ALU.mult)\
                        .then_inc(cz_ready, cinc(i))

                def sum_squares(i, p):
                    n = crows(i)
                    st = Steps(dve_scale, "dve_scale", b * CT + i)
                    dve.wait_ge(csq_ready, cdone(b, i) + 1)
                    st(dve.tensor_reduce(ss[0:n, p, :], csq[0:n].rearrange("p (h c) -> p h c", c=XD), AX.X, ALU.add))
                    dve.wait_ge(st.sem, st.all())
                    dve.tensor_scalar(rn[0:n, p, :], ss[0:n, p, :], 1e-24, None, ALU.max).then_inc(c_norm, 1)
                    st.close()

                def scale_k(i, q):
                    n = crows(i)
                    dve.wait_ge(c_rnorm, b * CT + i + 2)
                    k = kns[0:n, q, :].rearrange("p (h c) -> p h c", c=XD)
                    dve.tensor_tensor(k, k, bcast(rn[0:n, q % 2, :], XD), ALU.mult).then_inc(cs_ready, cinc(i))

                for i in range(3):
                    norm_stats(i, i % 2)
                    norm_apply(i, i % 2)
                sum_squares(0, 0)

                def ctx_dve(i, q):
                    if exists(i + 3):
                        norm_stats(i + 3, (q + 3) % 2)
                    if exists(i + 1):
                        sum_squares(i + 1, (q + 1) % 2)
                    if exists(i + 3):
                        norm_apply(i + 3, (q + 3) % 2)
                    scale_k(i, q)
                ctx_tiles(dve, ctx_dve)
                dve.wait_ge(cg_done, cdone(b, CT - 1) + 1)
                dve.wait_ge(parts_stored, 16 * 2 * PARTS * (b + 1) + 1)
                for j in (1, 3):
                    dve.tensor_copy(Gs[:, 2 * j:2 * j + 2, :].rearrange("p a b -> p (a b)"), bank(j)).then_inc(g_dve, 1)
                for c in range(2):
                    dve.wait_ge(gt_psum, 4 * b + 2 * c + 3)
                    dve.tensor_copy(GT[:, c, 4:8, :].rearrange("p a b -> p (a b)"), bank(5 + 2 * c)).then_inc(gt_dve, 1)
                for j in range(2):
                    dve.wait_ge(kvt_psum, 2 * b + j + 2)
                    dve.tensor_tensor(KVT[:, 4 * j:4 * j + 4, :], bank(j).rearrange("p (a b) -> p a b", a=4),
                                      pair_mask[:].unsqueeze(1).broadcast_to([128, 4, 128]), ALU.mult).then_inc(kvt_ready, 1)
                for j in (1, 3):
                    dve.wait_ge(m_psum, 4 * b + j + 2)
                    dve.tensor_copy(M[:, 2 * j:2 * j + 2, :].rearrange("p a b -> p (a b)"), bank(2 + j)).then_inc(m_dve, 2)
                dve.wait_ge(m_act, 4 * (b + 1) + 1)
                dve.sem_inc(waits_alone, 1)
                def bias(t, h):
                    g, j = divmod(h, HG)
                    tile = b * T + t
                    u = tile * H + h
                    if j == 0:
                        dve.wait_ge(bias_filled, 2 + tile * NG + g + 2)
                    dve.wait_ge(scores_ready, u + 2)
                    dve.wait_ge(probs_ready, u + 4)
                    dve.sem_inc(waits_alone, 1)
                    dve.tensor_tensor_reduce(out=Sb[:, h % 2, :], in0=bank(j), in1=Bt[:, (g % 2) * HG + j, PAD:PAD + S],
                                             scale=-0.25, scalar=BIG, op0=ALU.add, op1=ALU.min,
                                             accum_out=nmax[:, j:j + 1]).then_inc(scores_biased, 1)

                def evac(t, h):
                    dve.wait_ge(transposed, 4 + (b * T + t) * H + h + 2)
                    dve.wait_ge(pv_done, (b * T + t) * H + h + 2)
                    dve.tensor_copy(PTs[:, 1, :], bank(5)).then_inc(pt_copied[1], 1)

                def sum_mass(t, g):
                    dve.wait_ge(mass_mul, 2 + (b * T + t) * NG + g + 2)
                    dve.tensor_reduce(mass[:, ds(t, 1), g * HG:(g + 1) * HG].rearrange("p o h -> p (o h)"), prod, AX.X, ALU.add)\
                        .then_inc(mass_red, 1)

                def attn_dve(t, last):
                    for h in range(H):
                        if h + AHEAD < H:
                            bias(t, h + AHEAD)
                        elif not last:
                            bias(t + 1, h + AHEAD - H)
                        if h % 2 == 1:
                            evac(t, h)
                        if h % HG == HG - 1:
                            sum_mass(t, h // HG)

                for h in range(AHEAD):
                    bias(0, h)
                with dve.Fori(0, T - 1) as t:
                    attn_dve(t, False)
                attn_dve(T - 1, True)
                st = Steps(dve_attn, "dve_attn", b)
                dve.wait_ge(probs_ready, 4 + T * H * (b + 1) + 1)
                st(dve.reciprocal(rl[:], lsum[:]))

                def copy_band(t):
                    dve.wait_ge(fa_psum, 2 * (T * b + t) + 3)
                    if t >= 2:
                        dve.wait_ge(f_psum, T * b + t)
                    dve.tensor_copy(AT[:, t % 2, 4, :], bank(2 * (t % 2) + 1, 0, 128)).then_inc(fa_dve, 1)
                    dve.tensor_copy(massT[0:H, t % 2, :], bank(2 * (t % 2) + 1, 128, 256, H)).then_inc(fa_dve, 1)

                def combine(t):
                    dve.wait_ge(f_psum, T * b + t + 2)
                    dve.wait_ge(o_evac, T * b + t + 2)
                    st(dve.tensor_tensor(Oraw[:, t, :], Oraw[:, t, :], bank(4 + t % 2, 0, E), ALU.add))
                    dve.wait_ge(st.sem, st.all())
                    o = Oraw[:, t, :].rearrange("p (h c) -> p h c", c=HD)
                    st(dve.tensor_tensor(o, o, bcast(rl[:, t, :], HD), ALU.mult))
                    dve.wait_ge(st.sem, st.all())
                    dve.tensor_tensor(Oraw[:, t, :], Oraw[:, t, :], rows[:, V_BV, :], ALU.add).then_inc(attn_ready, 1)

                copy_band(0)
                for t in range(T):
                    if t + 1 < T:
                        copy_band(t + 1)
                    combine(t)
                for t in range(T):
                    dve.wait_ge(wo_psum, T * b + t + 2)
                    dve.wait_ge(xb_ready, b + 2)
                    dve.tensor_tensor(xin[:, t, :], xin[:, t, :], bank(4 + t % 2, 0, E), ALU.add).then_inc(x1_ready, 1)
                st.close()
                st = Steps(dve_tail, "dve_tail", b)
                dve.wait_ge(x1_ready, T * (b + 1) + 1)
                tiles = range(T)
                layernorm(dve, st, [xin[:, t, :] for t in tiles], [Qx[:, t, :] for t in tiles], qx_ready,
                          t_var, t_rstd, 4 * b + 1)
                dve.wait_ge(qx_ready, T * (b + 1) + 1)
                layernorm(dve, st, [Qx[:, t, :] for t in tiles], [Qn[:, t, :] for t in tiles], qz_ready,
                          t_var, t_rstd, 4 * b + 2)
                dve.wait_ge(qnT_psum, 2 * b + 3)
                dve.tensor_copy(QnT[:, 1, :], bank(1)).then_inc(qnT_ready, 1)

                def scale_q(t):
                    p = t % 2
                    dve.wait_ge(sq_ready, T * b + t + 2)
                    st(dve.tensor_reduce(ss[:, p, :], sq.rearrange("p (h c) -> p h c", c=XD), AX.X, ALU.add))
                    dve.wait_ge(st.sem, st.all())
                    dve.tensor_scalar(rn[:, p, :], ss[:, p, :], 1e-24, None, ALU.max).then_inc(q_norm, 1)
                    dve.wait_ge(q_rnorm, T * b + t + 2)
                    if t >= 2:
                        dve.wait_ge(qt_psum, 2 * (T * b + t - 1) + 1)
                    dve.tensor_tensor(qn[:, p, :].rearrange("p (h c) -> p h c", c=XD),
                                      PS[:, (2 + 2 * p) * 512:(4 + 2 * p) * 512].rearrange("p (h c) -> p h c", c=XD),
                                      bcast(rn[:, p, :], XD), ALU.mult).then_inc(qn_ready, 1)

                for t in range(T + 2):
                    if t < T:
                        scale_q(t)
                    if 1 <= t <= T:
                        dve.wait_ge(qt_psum, 2 * (T * b + t - 1) + 3)
                        if t >= 2:
                            dve.wait_ge(o_psum, T * b + t)
                        dve.tensor_copy(qnT[:, 4:8, :].rearrange("p a b -> p (a b)"), bank(7)).then_inc(qt_dve, 1)
                    if t >= 2:
                        dve.wait_ge(o_psum, T * b + t)
                        dve.wait_ge(y_res, T * b + t)
                        dve.tensor_tensor(y[:, t - 2, :], yr[:, t - 2, :], bank(t % 2, 0, E), ALU.add).then_inc(y_ready, 1)
                dve.wait_ge(y_ready, T * (b + 1) + 1)
                layernorm(dve, st, [y[:, t, :] for t in tiles], [yn[:, t, :] for t in tiles], yz_ready,
                          t_var, t_rstd, 4 * b + 3)
                dve.wait_ge(ynT_psum, 2 * b + 3)
                dve.tensor_copy(ynT[:, 1, :], bank(3)).then_inc(ynT_ready, 1)
                for t in tiles:
                    dve.wait_ge(m2_psum, T * b + t + 2)
                    dve.wait_ge(y2_res, T * b + t + 2)
                    dve.tensor_tensor(x2[:, t, :], yr[:, t, :], bank(t % 2, 0, E), ALU.add).then_inc(x2_ready, 1)
                dve.wait_ge(x2_ready, T * (b + 1) + 1)
                layernorm(dve, st, [x2[:, t, :] for t in tiles], [zf[:, t, :] for t in tiles], zf_ready,
                          t_var, t_rstd, 4 * b + 4)
                dve.wait_ge(zf_ready, T * (b + 1) + 1)
                for t in range(T + 1):
                    if t < T:
                        quant_scale(dve, st, zf[:, t, :], t % 2, 128, E, NQ0 + b * QPB + t)
                    if t:
                        quant_count(dve, st, (t - 1) % 2, 128, E, NQ0 + b * QPB + t - 1)
                dve.wait_ge(xqT_psum, 2 * b + 3)
                dve.tensor_copy(xqT[:, 1, :], bank(3)).then_inc(xqT_ready, 1)
                for t in range(T + 2):
                    if t < T:
                        g0 = (t % 2) * 3 * 512
                        dve.wait_ge(silu_ready, T * b + t + 2)
                        dve.tensor_tensor(gs[:, t % 2, :], gs[:, t % 2, :], PS[:, g0 + FF:g0 + 2 * FF], ALU.mult).then_inc(hh_ready, 1)
                        dve.wait_ge(hh_ready, T * b + t + 2)
                        quant_scale(dve, st, gs[:, t % 2, :], t % 2, 128, FF, NQ0 + b * QPB + T + t)
                    if 1 <= t <= T:
                        quant_count(dve, st, (t - 1) % 2, 128, FF, NQ0 + b * QPB + T + t - 1)
                    if t >= 2:
                        dve.wait_ge(ht_psum, T * b + t)
                        if t >= 4:
                            dve.wait_ge(dn_psum, T * b + t - 3 + 1)
                        dve.tensor_copy(hqT[:, t % 2, 4, :], bank(7, 0, 128)).then_inc(ht_dve, 1)
                        dve.tensor_copy(hqT[0:FLAST, t % 2, 5, :], bank(7, 128, 256, FLAST)).then_inc(ht_dve, 1)
                        dve.wait_ge(dn_psum, T * b + t)
                        dve.tensor_tensor(yout[:, t - 2, :], x2[:, t - 2, :], bank(7, 256, 512), ALU.add).then_inc(out_ready, 1)
                st.close()

        @block.tensor
        def _(pe):
            def mm(o, l, r, start, stop, **kw):
                return pe.matmul(o, l, r, start=start, stop=stop, **kw)

            def tr(o, i):
                return pe.transpose(o, i, ident[0:i.shape[0], 0:i.shape[0]])

            pe.wait_ge(consts_loaded, 16 * 10 + 1)
            pe.sem_inc(waits_alone, 1)
            for k, (kind, parts, n, i) in enumerate(wjobs):
                pe.wait_ge(quant_out, 2 + k + 2)
                if k:
                    pe.wait_ge(qwT_ready, 2 * k + 1)
                if kind == "d":
                    for c in range(NFF):
                        w = min(128, FF - c * 128)
                        last = tr(PS[0:w, c * 128:c * 128 + 128], qw[:, k % 2, c * 128:c * 128 + w])
                else:
                    for a in range(2):
                        for c in range(2):
                            last = tr(bank(a, c * 128, c * 128 + GR), qw[0:GR, k % 2, (2 * a + c) * 128:(2 * a + c + 1) * 128])
                last.then_inc(qwT_psum, 1)
            pe.wait_ge(qwT_ready, 2 * NQ0 + 1)
            pe.wait_ge(attn_w_loaded, 16 * 4 + 1)
            pe.wait_ge(ctx_w_loaded, 16 * 6 + 1)
            pe.wait_ge(tables_ready, 7)
            pe.wait_ge(setup_pool, START_MEMSETS + 1)
            pe.wait_ge(zeros_stored, 16 * T + 1)
            with pe.Fori(0, NB) as b:
                pe.wait_ge(out_ready, T * b + 1)
                pe.sem_inc(waits_alone, 1)
                for t in range(T):
                    pe.wait_ge(xn_ready, T * b + t + 2)
                    for c in range(2):
                        i = tr(bank(c, t * 128, t * 128 + 128), xn[:, t, c * 128:(c + 1) * 128])
                        if t == T - 1:
                            i.then_inc(xnT_psum, 1)
                pe.wait_ge(xnT_ready, 2 * (b + 1) + 1)
                for q in range(2):
                    for c in range(2):
                        i = mm(bank(2 + q), wk_s[:, c, q * 128:(q + 1) * 128], xnT[:, c, :], c == 0, c == 1)
                    i.then_inc(k_psum, 1)
                for q in range(2):
                    for c in range(2):
                        i = mm(bank(4 + q), wq_s[:, c, q * 128:(q + 1) * 128], xnT[:, c, :], c == 0, c == 1)
                    i.then_inc(q_psum, 1)
                for t in range(T):
                    for c in range(2):
                        i = mm(bank(6 + t // 2, (t % 2) * E, (t % 2 + 1) * E), xnT[:, c, t * 128:(t + 1) * 128], wv_s[:, c, :],
                               c == 0, c == 1)
                    if t % 2:
                        i.then_inc(v_psum, 1)
                pe.wait_ge(qT_ready, 2 * (b + 1) + 1)
                for t in range(T):
                    if t == 1:
                        pe.wait_ge(v_ready, 2 * (b + 1) + 1)
                    if t >= 2:
                        pe.wait_ge(r_act, T * b + t)
                        pe.wait_ge(r_dve, T * b + t)
                    for c in range(2):
                        mm(bank(4 + 2 * (t % 2) + c, 0, HC * NREL), QT[:, c, t * 128:(t + 1) * 128], bdk[:], True, True)\
                            .then_inc(r_psum, 1)

                def t_ctx(i, q):
                    n, p = crows(i), q % 2
                    pe.wait_ge(caff_ready, cdone(b, i) + 1)
                    pe.wait_ge(ct_ready, cdone(b, i - 2) + 1)
                    for c in range(2):
                        ins = tr(bank(6 + p, c * 128, c * 128 + n), Kn[0:n, q, c * 128:(c + 1) * 128])
                    ins.then_inc(ct_psum, cinc(i))

                def k_ctx(i, q):
                    n, p = crows(i), q % 2
                    pe.wait_ge(ct_ready, cdone(b, i) + 1)
                    pe.wait_ge(kc_ready, cdone(b, i - 1) + 1)
                    for j in range(2):
                        for c in range(2):
                            ins = mm(bank(4 + j, parts=n), cnT[:, p, c, 0:n], cwk[:, c, j * 512:(j + 1) * 512], c == 0, c == 1)
                    ins.then_inc(ck_psum, cinc(i))

                def g_ctx(i, q):
                    n, p = crows(i), q % 2
                    pe.wait_ge(cs_ready, cdone(b, i) + 1)
                    for m in range(NM):
                        ins = mm(bank(m // 2, (m % 2) * E, (m % 2 + 1) * E), kns[0:n, q, m * 128:(m + 1) * 128], Kn[0:n, q, :],
                                 False, True, skip_group_check=True)
                    ins.then_inc(cg_done, cinc(i))

                pe.wait_ge(kT_ready, 2 * (b + 1) + 1)
                pe.wait_ge(r_act, T * (b + 1) + 1)
                pe.wait_ge(r_dve, T * (b + 1) + 1)
                for j in range(4):
                    mm(bank(j), zeros[:, 0:128], zeros[:, :], True, True, skip_group_check=True)
                t_ctx(0, 0)
                t_ctx(1, 1)
                k_ctx(0, 0)
                t_ctx(2, 2)
                k_ctx(1, 1)

                def ctx_pe(i, q):
                    if exists(i + 2):
                        k_ctx(i + 2, (q + 2) % 4)
                    if exists(i + 3):
                        t_ctx(i + 3, (q + 3) % 4)
                    g_ctx(i, q)
                ctx_tiles(pe, ctx_pe)
                pe.wait_ge(g_act, 2 * (b + 1) + 1)
                pe.wait_ge(g_dve, 2 * (b + 1) + 1)
                for c in range(2):
                    for m in range(NM):
                        i = tr(bank(4 + 2 * c + m // 4, (m % 4) * 128, (m % 4 + 1) * 128), Gs[:, m, c * 128:(c + 1) * 128])
                        if m % 4 == 3:
                            i.then_inc(gt_psum, 1)
                pe.wait_ge(gt_act, 2 * (b + 1) + 1)
                pe.wait_ge(gt_dve, 2 * (b + 1) + 1)
                for m in range(NM):
                    for c in range(2):
                        i = mm(bank(m // 4, (m % 4) * 128, (m % 4 + 1) * 128), cwv[:, c, m * 128:(m + 1) * 128], GT[:, c, m, :],
                               c == 0, c == 1)
                    if m % 4 == 3:
                        i.then_inc(kvt_psum, 1)
                for m in range(NM):
                    pe.wait_ge(kvt_ready, 2 * b + m // 4 + 2)
                    i = mm(bank(2 + m // 2, (m % 2) * E, (m % 2 + 1) * E), KVT[:, m, :], cwo[:, m, :], True, True)
                    if m % 2:
                        i.then_inc(m_psum, 1)
                pe.wait_ge(m_act, 4 * (b + 1) + 1)
                pe.wait_ge(m_dve, 4 * (b + 1) + 1)
                pe.wait_ge(vsel_ready, 2 * (T - 1) * (b + 1) + 1)
                pe.sem_inc(waits_alone, 1)
                pe.wait_ge(k_loaded, 16 * len(SLOTS_K) * (b + 1) + 1)

                def scores(t, g):
                    pe.wait_ge(q_loaded[g], 16 * len(SLOTS_Q) * (b * T + t + 1) + 1)
                    for j in range(HG):
                        h = g * HG + j
                        u = (b * T + t) * H + h
                        pe.wait_ge(scores_biased, u + 2)
                        mm(bank(j), Qp[:, h, :], Kp[:, h, :], True, True).then_inc(scores_ready, 1)

                def transpose_probs(t, h):
                    tile = b * T + t
                    pe.wait_ge(probs_ready, 4 + tile * H + h + 2)
                    pe.wait_ge(pt_copied[h % 2], tile * (H // 2) + h // 2 + 1)
                    for k in range(T):
                        i = tr(bank(4 + h % 2, k * 128, (k + 1) * 128),
                               P[:, (h // HG % 2) * HG + h % HG, PAD + k * 128:PAD + (k + 1) * 128])
                    i.then_inc(transposed, 1)

                def weigh(t, h):
                    tile = b * T + t
                    pe.wait_ge(pt_copied[h % 2], tile * (H // 2) + h // 2 + 2)
                    if h == 0:
                        pe.wait_ge(o_evac, tile + 1)
                    for k in range(T):
                        i = mm(bank(6, h * HD, (h + 1) * HD), PTs[:, h % 2, k * 128:(k + 1) * 128],
                               Vsel[:, ds(t, 1), k, h * HD:(h + 1) * HD].rearrange("p o e -> p (o e)"),
                               h == 0 and k == 0, True, skip_group_check=True)
                    i.then_inc(pv_done, 1)

                def attn_pe(t, last):
                    for g in range(NG):
                        if g + 1 < NG:
                            scores(t, g + 1)
                        elif not last:
                            scores(t + 1, 0)
                        for h in range(g * HG, (g + 1) * HG):
                            transpose_probs(t, h)
                            if h:
                                weigh(t, h - 1)
                    weigh(t, H - 1)

                scores(0, 0)
                with pe.Fori(0, T - 1) as t:
                    attn_pe(t, False)
                attn_pe(T - 1, True)
                pe.wait_ge(band_loaded, 16 * T * NG * (b + 1) + 1)
                pe.wait_ge(mass_red, T * NG * (b + 1) + 1)
                pe.wait_ge(scores_biased, 4 + T * H * (b + 1) + 1)

                def transpose_band(t):
                    if t >= 2:
                        pe.wait_ge(fa_act, T * b + t)
                        pe.wait_ge(fa_dve, 2 * (T * b + t - 1) + 1)
                    band = Pband[:, t, :, :].rearrange("p h r -> p (h r)")
                    for c in range(4):
                        i = tr(bank(2 * (t % 2), c * 128, (c + 1) * 128), band[:, c * 128:(c + 1) * 128])
                    i.then_inc(fa_psum, 1)
                    tr(bank(2 * (t % 2) + 1, 0, 128), band[:, 512:640])
                    tr(bank(2 * (t % 2) + 1, 128, 256, H), mass[:, t, :]).then_inc(fa_psum, 1)

                def weigh_band(t):
                    pe.wait_ge(fa_act, T * b + t + 2)
                    pe.wait_ge(fa_dve, 2 * (T * b + t + 1) + 1)
                    if t >= 2:
                        pe.wait_ge(attn_ready, T * b + t)
                    mm(bank(4 + t % 2, 0, E), massT[0:H, t % 2, :], bdr[:], True, True, skip_group_check=True)
                    for c in range(5):
                        i = mm(bank(4 + t % 2, 48 * c, 48 * c + 64), AT[:, t % 2, c, :], bdv[:, c, :], False, True,
                               skip_group_check=True)
                    i.then_inc(f_psum, 1)

                transpose_band(0)
                for t in range(T):
                    if t + 1 < T:
                        transpose_band(t + 1)
                    weigh_band(t)
                pe.wait_ge(o_evac, T * (b + 1) + 1)

                def project(t):
                    pe.wait_ge(aT_ready, T * b + t + 2)
                    if t >= 2:
                        pe.wait_ge(x1_ready, T * b + t)
                    for c in range(2):
                        i = mm(bank(4 + t % 2, 0, E), aT[:, t % 2, c, :], wo_s[:, c, :], c == 0, c == 1)
                    i.then_inc(wo_psum, 1)

                for t in range(T):
                    pe.wait_ge(attn_ready, T * b + t + 2)
                    if t >= 2:
                        pe.wait_ge(aT_ready, T * b + t)
                    for c in range(2):
                        i = tr(bank(6 + t % 2, c * 128, (c + 1) * 128), Oraw[:, t, c * 128:(c + 1) * 128])
                    i.then_inc(at_psum, 1)
                pe.wait_ge(attn_ready, T * (b + 1) + 1)
                for t in range(T):
                    project(t)
                for t in range(T):
                    pe.wait_ge(qaff_ready, T * b + t + 2)
                    for c in range(2):
                        i = tr(bank(c, t * 128, (t + 1) * 128), Qn[:, t, c * 128:(c + 1) * 128])
                        if t == T - 1:
                            i.then_inc(qnT_psum, 1)
                pe.wait_ge(qnT_ready, 2 * (b + 1) + 1)

                def project_q(t):
                    if t >= 2:
                        pe.wait_ge(qn_ready, T * b + t)
                    for j in range(2):
                        for c in range(2):
                            i = mm(bank(2 + 2 * (t % 2) + j), QnT[:, c, t * 128:(t + 1) * 128], cwq[:, c, j * 512:(j + 1) * 512],
                                   c == 0, c == 1)
                    i.then_inc(xq_psum, 1)

                def cross(t):
                    pe.wait_ge(qn_ready, T * b + t + 2)
                    if t:
                        pe.wait_ge(qt_act, T * b + t + 1)
                        pe.wait_ge(qt_dve, T * b + t + 1)
                    for m in range(NM):
                        i = tr(bank(6 + m // 4, (m % 4) * 128, (m % 4 + 1) * 128), qn[:, t % 2, m * 128:(m + 1) * 128])
                        if m % 4 == 3:
                            i.then_inc(qt_psum, 1)
                    pe.wait_ge(qt_act, T * b + t + 2)
                    pe.wait_ge(qt_dve, T * b + t + 2)
                    if t >= 2:
                        pe.wait_ge(y_ready, T * b + t)
                    for m in range(NM):
                        i = mm(bank(t % 2, 0, E), qnT[:, m, :], M[:, m, :], m == 0, m == NM - 1)
                    i.then_inc(o_psum, 1)

                project_q(0)
                project_q(1)
                for t in range(T):
                    if t + 2 < T:
                        project_q(t + 2)
                    cross(t)
                for t in range(T):
                    pe.wait_ge(yaff_ready, T * b + t + 2)
                    for c in range(2):
                        i = tr(bank(2 + c, t * 128, (t + 1) * 128), yn[:, t, c * 128:(c + 1) * 128])
                        if t == T - 1:
                            i.then_inc(ynT_psum, 1)
                pe.wait_ge(ynT_ready, 2 * (b + 1) + 1)
                for f in range(NF):
                    if f >= 4:
                        pe.wait_ge(h_ready, NF * b + f - 3 + 1)
                    for c in range(2):
                        i = mm(bank(4 + f % 4), w1[:, c, f * 128:(f + 1) * 128], ynT[:, c, :], c == 0, c == 1)
                    i.then_inc(h_psum, 1)
                pe.wait_ge(h_ready, NF * (b + 1) + 1)
                for t in range(T):
                    if t >= 2:
                        pe.wait_ge(x2_ready, T * b + t)
                    for f in range(NF):
                        i = mm(bank(t % 2, 0, E), hT[:, f, t * 128:(t + 1) * 128], w2[:, f, :], f == 0, f == NF - 1)
                    i.then_inc(m2_psum, 1)
                for t in range(T):
                    pe.wait_ge(quant_out, 2 + NQ0 + b * QPB + t + 2)
                    for c in range(2):
                        i = tr(bank(2 + c, t * 128, (t + 1) * 128), xq[:, t, c * 128:(c + 1) * 128])
                        if t == T - 1:
                            i.then_inc(xqT_psum, 1)
                pe.wait_ge(xqT_ready, 2 * (b + 1) + 1)

                def gate_up(t):
                    if t >= 2:
                        pe.wait_ge(hh_ready, T * b + t)
                    g0 = (t % 2) * 3 * 512
                    for w, o, lo, hi in ((wgT, 0, 0, 512), (wgT, 0, 512, FF), (wuT, FF, 0, 1024 - FF), (wuT, FF, 1024 - FF, FF)):
                        for c in range(2):
                            i = mm(PS[:, g0 + o + lo:g0 + o + hi], xqT[:, c, t * 128:(t + 1) * 128], w[:, c, lo:hi], c == 0, c == 1)
                    i.then_inc(gu_psum, 1)

                def down(t):
                    pe.wait_ge(quant_out, 2 + NQ0 + b * QPB + T + t + 2)
                    if t:
                        pe.wait_ge(ht_act, T * b + t + 1)
                        pe.wait_ge(out_ready, T * b + t + 1)
                    for c in range(NFF):
                        w = min(128, FF - c * 128)
                        i = tr(bank(6 + c // 4, (c % 4) * 128, (c % 4 + 1) * 128, w), hq[:, t % 2, c * 128:c * 128 + w])
                    i.then_inc(ht_psum, 1)
                    pe.wait_ge(ht_act, T * b + t + 2)
                    pe.wait_ge(ht_dve, 2 * (T * b + t + 1) + 1)
                    for c in range(NFF):
                        w = min(128, FF - c * 128)
                        i = mm(bank(7, 256, 512), hqT[0:w, t % 2, c, :], wdT[0:w, c, :], c == 0, c == NFF - 1)
                    i.then_inc(dn_psum, 1)

                gate_up(0)
                gate_up(1)
                gate_up(2)
                for t in range(T):
                    down(t)
                    if t == 0:
                        gate_up(3)


def _arrange(inputs):
    a = {k: np.asarray(v) for k, v in inputs.items()}
    f = np.float32

    def halves(w):
        return np.ascontiguousarray(w.reshape(-1, 128, w.shape[1]).transpose(1, 0, 2))

    d = {"x": a["x"], "ctx": a["ctx_1024"]}
    d["wq"], d["wk"] = halves(a["L0_attn_Wq"].T), halves(a["L0_attn_Wk"].T)
    d["wv"], d["wo"] = halves(a["L0_attn_Wv"].T), halves(a["L0_attn_Wo"].T)
    d["cwq"], d["cwk"], d["cwv"] = (halves(a["L0_xattn_" + n]) for n in ("wq", "wk", "wv"))
    d["cwo"], d["w1"], d["w2"] = (halves(a["L0_xattn_" + n]) for n in ("wo", "w1", "w2"))
    for n, w in (("w_gate", a["L0_ffn_w_gate"]), ("w_up", a["L0_ffn_w_up"])):
        d[n] = np.ascontiguousarray(w.reshape(NGR, GR, E).transpose(1, 0, 2))
    d["w_down"] = halves(a["L0_ffn_w_down"])
    rk, rv = a["L0_attn_rel_k"], a["L0_attn_rel_v"]
    vecs = [a["L0_attn_bv"], a["L0_attn_bo"], a["L0_xattn_ln1_g"], a["L0_xattn_ln1_b"], a["L0_xattn_bo"],
            a["L0_xattn_ln2_g"], a["L0_xattn_ln2_b"], a["L0_xattn_b2"], np.tile(rv[BAND], H)]
    d["rows"] = np.ascontiguousarray(np.broadcast_to(np.stack(vecs)[None], (128, 9, E)))
    d["cols"] = np.concatenate([a["L0_attn_bq"].reshape(2, 128).T, a["L0_attn_bk"].reshape(2, 128).T,
                                a["L0_xattn_b1"].reshape(8, 128).T, np.zeros((128, 4), f)], axis=1)

    def tables(kt, vt):
        bk = np.zeros((128, HC, NREL), f)
        for j in range(HC):
            bk[j * HD:(j + 1) * HD, j, :] = kt.T
        bv = np.zeros((H, BAND, H, HD), f)
        br = np.zeros((H, H, HD), f)
        for h in range(H):
            bv[h, :, h, :] = vt[0:BAND]
            br[h, h, :] = vt[BAND]
        bv = bv.reshape(5, 128, E)
        bv = np.stack([bv[c][:, 48 * c:48 * c + 64] for c in range(5)], axis=1)
        return bk.reshape(128, HC * NREL), bv, br.reshape(H, E)

    d["bdk"], d["bdv"], d["bdr"] = tables(rk, rv)
    k0, v0, r0 = tables(np.broadcast_to(rk[0:1], rk.shape), np.broadcast_to(rv[0:1], rv.shape))
    rel0 = np.zeros((128, TAB0), f)
    o = HC * NREL
    rel0[:, 0:o] = k0
    rel0[:, o:o + 320] = v0.reshape(128, 320)
    rel0[0:H, o + 320:o + 320 + E] = r0
    rel0[:, o + 320 + E:o + 320 + 2 * E] = np.tile(rv[0], H)
    d["rel0"] = rel0
    p = np.arange(128)[:, None]
    d["ident"] = np.eye(128, dtype=f)
    d["right_mask"] = (np.arange(384 + S)[None] - 384 >= p + MAX_REL).astype(f)
    c = np.arange(128)[None] + MAX_REL
    right = (c >= p + MAX_REL).astype(f)
    d["mass_mask"] = np.where(c < 128, right, right - 1).astype(f)
    d["pair_mask"] = (np.arange(128)[None] // XD == p // XD).astype(f)
    return {k: np.ascontiguousarray(v) for k, v in d.items()}


def kernel(**inputs):
    import concourse.bacc as bacc
    import concourse.bass as bass
    from concourse import mybir
    from concourse.bass_utils import run_bass_kernel_spmd

    nc = bacc.Bacc("TRN2", target_bir_lowering=False, num_devices=1)
    arrays = _arrange(inputs)
    d = {k: nc.dram_tensor("in_" + k, v.shape, mybir.dt.from_np(v.dtype), kind="ExternalInput").ap() for k, v in arrays.items()}
    for k in ("bias_scr", "prob_scr"):
        d[k] = nc.dram_tensor(k, [T, H, REGION], mybir.dt.float32, kind="Internal").ap()
    for k in ("q_scr", "k_scr"):
        d[k] = nc.dram_tensor(k, [PARTS, E, S], mybir.dt.bfloat16, kind="Internal").ap()
    out = nc.dram_tensor("out", [NB, S, E], mybir.dt.float32, kind="ExternalOutput").ap()
    build(nc, bass, mybir, d, out)
    r = run_bass_kernel_spmd(nc, [{"in_" + k: v for k, v in arrays.items()}], core_ids=[0])
    return r.results[0]["out"]
```

```python
import numpy as np

NB, S, E, H, HD = 8, 512, 256, 16, 16
T = S // 128
MAX_REL = 20
BAND = 2 * MAX_REL
NREL = BAND + 1
PAD = MAX_REL
ROW = PAD + S + PAD
WIN = 128 + BAND
SKEW = WIN + 1
REGION = 128 * SKEW
CTX = 1601
CT = (CTX + 127) // 128
CLAST = CTX - (CT - 1) * 128
XH, XD = 16, 64
INNER = XH * XD
NM = INNER // 128
MLP = 1024
NF = MLP // 128
FF = 704
NFF = (FF + 127) // 128
FLAST = FF - (NFF - 1) * 128
QB = 16
EPS = 1e-5
HG = 4
NG = H // HG
GR = 88
NGR = FF // GR
BIG = 3.0e38
ARENA = 26976
HC = H // 2
TAB0 = HC * NREL + 5 * 64 + 3 * E
START_MEMSETS = 3
PARTS = 3
SLOTS_Q = (0, 0, 0, 1, 1, 1, 2, 2)
SLOTS_K = (0, 1, 2, 0, 1, 2, 0, 1)
OWN = {"dve_start": 110, "dve_prep": 8, "dve_norm": 2, "dve_scale": 1, "dve_attn": 5, "dve_tail": 89,
       "pool_start": 10, "pool_affine": 1, "pool_fill": 1, "pool_tail": 10}


def build(nc, bass, mybir, d, out):
    from contextlib import ExitStack
    f32, bf16 = mybir.dt.float32, mybir.dt.bfloat16
    ALU, ACT, AX = mybir.AluOpType, mybir.ActivationFunctionType, mybir.AxisListType
    ds = bass.ds
    ctx = ExitStack()
    with ctx:
        def sb(name, shape, dt=f32):
            return ctx.enter_context(nc.sbuf_tensor(name, shape, dt))

        starts = []

        def sem(name, start=1):
            made = ctx.enter_context(nc.semaphore(name))
            starts.append((made, start))
            return made

        wq_s, wk_s = sb("wq_s", [128, 2, E]), sb("wk_s", [128, 2, E])
        wv_s, wo_s = sb("wv_s", [128, 2, E]), sb("wo_s", [128, 2, E])
        cwq, cwk, cwv = sb("cwq", [128, 2, INNER]), sb("cwk", [128, 2, INNER]), sb("cwv", [128, 2, INNER])
        cwo, w1, w2 = sb("cwo", [128, NM, E]), sb("w1", [128, 2, MLP]), sb("w2", [128, NF, E])
        rows = sb("rows", [128, 7, E])
        V_BV, V_BO, V_G1, V_B1, V_XBO, V_XB2, V_EDGE = range(7)
        cols = sb("cols", [128, 20])
        C_G1, C_B1, C_G2, C_B2 = 12, 14, 16, 18
        ident = sb("ident", [128, 128])
        right_mask = sb("right_mask", [128, 384 + S], bf16)
        mass_mask = sb("mass_mask", [128, 128])
        pair_mask = sb("pair_mask", [128, 128])
        pack = sb("pack", [128, HG * HD])
        bdk, bdv, bdr = sb("bdk", [128, HC * NREL]), sb("bdv", [128, 5, 64]), sb("bdr", [16, E])
        wgT, wuT, wdT = sb("wgT", [128, 2, FF]), sb("wuT", [128, 2, FF]), sb("wdT", [128, NFF, E])
        zeros = sb("zeros", [128, 128], bf16)
        xin = sb("xin", [128, T, E])
        M = sb("M", [128, NM, E])
        edge = sb("edge", [128, T, H])
        lsum, rl, mass = sb("lsum", [128, T, H]), sb("rl", [128, T, H]), sb("mass", [128, T, H])
        bnst, mv, rstd = sb("bnst", [128, T, 6]), sb("mv", [128, T, 2]), sb("rstd", [128, T])
        rstd2 = sb("rstd2", [128, T])
        mhalf = sb("mhalf", [128, 16])
        ss, rn = sb("ss", [128, 2, 16]), sb("rn", [128, 2, 16])
        am, qsc, qrc, qhs = (sb(n, [128, 2, FF // QB]) for n in ("am", "qsc", "qrc", "qhs"))
        nmax = sb("nmax", [128, HG])
        arena = sb("arena", [128, ARENA])
        used = [0]

        def carve(n, shape, at=None):
            lo = used[0] if at is None else at
            used[0] = lo + n
            assert used[0] <= ARENA, used[0]
            v = arena[:, lo:lo + n]
            if len(shape) == 2:
                return v.rearrange("p (a b) -> p a b", a=shape[0])
            if len(shape) == 3:
                return v.rearrange("p (a b c) -> p a b c", a=shape[0], b=shape[1])
            return v

        Kp = carve(H * S // 2, (H * S // 2,), 0).bitcast(bf16).rearrange("p (h s) -> p h s", h=H)
        Qp = carve(H * 64, (H * 64,)).bitcast(bf16).rearrange("p (h s) -> p h s", h=H)
        V = carve(T * E, (T, E))
        Vcur = carve(T * E, (T, E))
        OT = carve(T * 512, (T, 512))
        Rb = carve(T * H * NREL, (T, H, NREL), used[0])
        Pband = carve(T * H * BAND, (T, H, BAND), used[0] - T * H * NREL)
        used[0] += T * H
        only_attn = used[0]
        Bt = carve(2 * HG * ROW, (2 * HG, ROW))
        Wn = carve(2 * HG * WIN, (2 * HG, WIN))
        P = carve(2 * HG * ROW, (2 * HG, ROW))
        Sb = carve(4 * S, (4, S))
        PTs = carve(2 * 512, (2, 512))
        prod = carve(HG * 128, (HG, 128))
        AT = carve(2 * 640, (2, 5, 128), only_attn)
        massT = carve(2 * 128, (2, 128))
        aT = carve(2 * 256, (2, 2, 128))
        Oraw = carve(1024, (T, E))
        xnT = carve(1024, (2, 512), only_attn)
        cin, Kn = carve(512, (2, E)), carve(1024, (4, E))
        cnT = carve(512, (2, 2, 128))
        csq = carve(1024, (1024,))
        kns_at = used[0]
        kns = carve(4096, (4, INNER))
        QT, KT, Qrest, Krest = (carve(1024, (2, S), kns_at + 1024 * i) for i in range(4))
        qparts, kparts = (carve(PARTS * 512, (PARTS * 512,)).bitcast(bf16).rearrange("p (i c s) -> p i c s", i=PARTS, c=2)
                          for _ in range(2))
        Gs = carve(2048, (NM, E), kns_at + 4096)
        GT = carve(2048, (2, NM, 128), kns_at + 2048)
        assert kns_at + 2048 >= only_attn + 2 * HG * (ROW + WIN)
        KVT = carve(1024, (NM, 128))
        Qx, Qn, QnT = carve(1024, (T, E), 0), carve(1024, (T, E)), carve(1024, (2, 512))
        sq = carve(1024, (1024,))
        qn, qnT = carve(2048, (2, INNER)), carve(1024, (NM, 128))
        y, yr = carve(1024, (T, E)), carve(1024, (T, E))
        yn, ynT = Qn, QnT
        hT = carve(4096, (NF, 512))
        x2 = carve(1024, (T, E))
        zf = Qx
        qv, qa, qs, qc, qh = (carve(2 * FF, (2, FF)) for _ in range(5))
        xq, xqT = carve(1024, (T, E)), carve(1024, (2, 512))
        hqT = carve(2 * NFF * 128, (2, NFF, 128), 4096)
        yout = hT[:, 0:2, :].rearrange("p a (b c) -> p (a b) c", b=2)
        gs = carve(T * FF, (T, FF), 9216 + 1024)
        hq = carve(2 * FF, (2, FF), 7168)

        xn = carve(1024, (T, E), ARENA - 1024)
        raw_wg = carve(NGR * E, (NGR, E), H * SKEW)
        raw_wu = carve(NGR * E, (NGR, E))
        raw_wd = carve(2 * FF, (2, FF))
        qw = carve(2 * FF, (2, FF))
        rel0 = carve(TAB0, (TAB0,))
        mask32 = carve(384 + S, (384 + S,))

        PS = ctx.enter_context(nc.psum_tensor("PS", [128, 8 * 512], f32))

        def bank(i, lo=0, hi=512, parts=128):
            return PS[0:parts, i * 512 + lo:i * 512 + hi]

        bias_scr, prob_scr, q_scr, k_scr = d["bias_scr"], d["prob_scr"], d["q_scr"], d["k_scr"]

        waits_alone = sem("waits_alone")
        consts_loaded = sem("consts_loaded")
        attn_w_loaded = sem("attn_w_loaded")
        ctx_w_loaded = sem("ctx_w_loaded")
        ffn_w_loaded = sem("ffn_w_loaded")
        zeros_stored = sem("zeros_stored")
        setup_pool = sem("setup_pool")
        tables_ready = sem("tables_ready")
        dve_start = sem("dve_start")
        dve_prep = sem("dve_prep")
        dve_norm = sem("dve_norm")
        dve_scale = sem("dve_scale")
        dve_attn = sem("dve_attn")
        dve_tail = sem("dve_tail")
        pool_start = sem("pool_start")
        pool_affine = sem("pool_affine")
        pool_fill = sem("pool_fill")
        pool_tail = sem("pool_tail")
        x_var = sem("x_var")
        x_rstd = sem("x_rstd")
        c_var = sem("c_var")
        c_rstd = sem("c_rstd")
        c_norm = sem("c_norm")
        c_rnorm = sem("c_rnorm")
        t_var = sem("t_var")
        t_rstd = sem("t_rstd")
        q_norm = sem("q_norm")
        q_rnorm = sem("q_rnorm")
        x_loaded = sem("x_loaded")
        xn_ready = sem("xn_ready")
        xnT_psum = sem("xnT_psum")
        xnT_ready = sem("xnT_ready")
        k_psum = sem("k_psum")
        kT_ready = sem("kT_ready")
        q_psum = sem("q_psum")
        qT_ready = sem("qT_ready")
        v_psum = sem("v_psum")
        v_ready = sem("v_ready")
        vcur_ready = sem("vcur_ready")
        vcur_moved = sem("vcur_moved")
        r_psum = sem("r_psum")
        r_act = sem("r_act")
        r_dve = sem("r_dve")
        e_ready = sem("e_ready")
        xb_ready = sem("xb_ready")
        bias_stored = sem("bias_stored")
        ctx_loaded = [sem("ctx_loaded0"), sem("ctx_loaded1")]
        cz_ready = sem("cz_ready", 5)
        caff_ready = sem("caff_ready", 5)
        ct_psum = sem("ct_psum", 5)
        ct_ready = sem("ct_ready", 5)
        ck_psum = sem("ck_psum", 5)
        kc_ready = sem("kc_ready", 5)
        csq_ready = sem("csq_ready", 5)
        cs_ready = sem("cs_ready", 5)
        cg_done = sem("cg_done", 5)
        g_act = sem("g_act")
        g_dve = sem("g_dve")
        gt_psum = sem("gt_psum")
        gt_act = sem("gt_act")
        gt_dve = sem("gt_dve")
        kvt_psum = sem("kvt_psum")
        kvt_ready = sem("kvt_ready")
        m_psum = sem("m_psum")
        m_act = sem("m_act")
        m_dve = sem("m_dve")
        part0_ready = sem("part0_ready")
        rest_ready = sem("rest_ready")
        part1_ready = sem("part1_ready")
        part2_ready = sem("part2_ready")
        parts_stored = sem("parts_stored")
        k_loaded = sem("k_loaded")
        q_loaded = [sem(f"q_loaded{g}") for g in range(NG)]
        scores_ready = sem("scores_ready")
        scores_biased = sem("scores_biased", 5)
        edge_filled = sem("edge_filled")
        bias_filled = sem("bias_filled", 3)
        win_loaded = [sem("win_loaded0"), sem("win_loaded1")]
        probs_ready = sem("probs_ready", 5)
        p_stored = [sem("p_stored0"), sem("p_stored1")]
        transposed = sem("transposed", 5)
        pt_copied = [sem("pt_act"), sem("pt_dve")]
        pv_done = sem("pv_done", 3)
        o_evac = sem("o_evac")
        mass_mul = sem("mass_mul")
        mass_ready = sem("mass_ready", 3)
        band_loaded = sem("band_loaded")
        fa_psum = sem("fa_psum")
        fa_act = sem("fa_act")
        fa_dve = sem("fa_dve")
        f_psum = sem("f_psum")
        attn_ready = sem("attn_ready")
        at_psum = sem("at_psum")
        aT_ready = sem("aT_ready")
        wo_psum = sem("wo_psum")
        x1_ready = sem("x1_ready")
        qx_ready = sem("qx_ready")
        qz_ready = sem("qz_ready")
        qnT_psum = sem("qnT_psum")
        qnT_ready = sem("qnT_ready")
        xq_psum = sem("xq_psum")
        sq_ready = sem("sq_ready")
        qn_ready = sem("qn_ready")
        qt_psum = sem("qt_psum")
        qt_act = sem("qt_act")
        qt_dve = sem("qt_dve")
        o_psum = sem("o_psum")
        y_res = sem("y_res")
        y_ready = sem("y_ready")
        yz_ready = sem("yz_ready")
        ynT_psum = sem("ynT_psum")
        ynT_ready = sem("ynT_ready")
        h_psum = sem("h_psum")
        h_ready = sem("h_ready")
        y2_res = sem("y2_res")
        m2_psum = sem("m2_psum")
        x2_ready = sem("x2_ready")
        zf_ready = sem("zf_ready")
        quant_s = sem("quant_s")
        quant_v = sem("quant_v")
        quant_a = sem("quant_a")
        quant_c = sem("quant_c")
        quant_out = sem("quant_out", 3)
        qwT_psum = sem("qwT_psum")
        qwT_ready = sem("qwT_ready")
        xqT_psum = sem("xqT_psum")
        xqT_ready = sem("xqT_ready")
        gu_psum = sem("gu_psum")
        silu_ready = sem("silu_ready")
        hh_ready = sem("hh_ready")
        ht_psum = sem("ht_psum")
        ht_ready = sem("ht_ready")
        dn_psum = sem("dn_psum")
        out_ready = sem("out_ready")
        out_stored = sem("out_stored")

        class Steps:
            def __init__(self, which, name, turn=0):
                self.sem, self.name, self.n, self.base = which, name, 0, turn * OWN[name]

            def __call__(self, ins):
                self.n += 1
                return ins.then_inc(self.sem, 1)

            def all(self):
                return self.base + self.n + 1

            def close(self):
                assert self.n == OWN[self.name], (self.name, self.n)

        def bcast(v, n):
            return v.unsqueeze(2).broadcast_to([v.shape[0], v.shape[1], n])

        def root(pool, x, start, done, n):
            pool.wait_ge(start, n + 1)
            pool.sem_inc(waits_alone, 1)
            pool.tensor_tensor(x, x, mhalf[0:x.shape[0], 0:x.shape[1]], ALU.pow).then_inc(done, 1)

        def layernorm(eng, st, srcs, outs, done, var, inv, turn, lo=0, have_stats=False):
            hi = lo + len(srcs)
            for i, x in zip(range(lo, hi), srcs):
                if not have_stats:
                    st(eng.bn_stats(bnst[:, i, :], x))
            eng.wait_ge(st.sem, st.all())
            eng.sem_inc(waits_alone, 1)
            for i in range(lo, hi):
                st(eng.bn_aggr(mv[:, i, :], bnst[:, i, :]))
            eng.wait_ge(st.sem, st.all())
            eng.tensor_scalar(rstd[:, lo:hi], mv[:, lo:hi, 1], EPS, None, ALU.add).then_inc(var, 1)
            eng.wait_ge(inv, turn + 1)
            for i, x, y in zip(range(lo, hi), srcs, outs):
                eng.tensor_scalar(y, x, mv[:, i, 0:1], rstd[:, i:i + 1], ALU.subtract, ALU.mult).then_inc(done, 1)

        def quant_scale(eng, st, X, p, parts, n, k, divide=True):
            nb = n // QB
            eng.wait_ge(quant_out, k + 2)
            st(eng.tensor_reduce(am[0:parts, p, 0:nb], X.rearrange("p (b c) -> p b c", c=QB), AX.X, ALU.max,
                                 apply_absolute_value=True))
            eng.wait_ge(st.sem, st.all())
            st(eng.tensor_scalar(qsc[0:parts, p, 0:nb], am[0:parts, p, 0:nb], 1.0 / 6.0, 1e-12, ALU.mult, ALU.max))
            eng.wait_ge(st.sem, st.all())
            half = eng.tensor_scalar(qhs[0:parts, p, 0:nb], qsc[0:parts, p, 0:nb], 0.5, None, ALU.mult)
            if not divide:
                half.then_inc(quant_s, 1)
                eng.reciprocal(qrc[0:parts, p, 0:nb], qsc[0:parts, p, 0:nb]).then_inc(quant_s, 1)
                return
            st(half)
            st(eng.reciprocal(qrc[0:parts, p, 0:nb], qsc[0:parts, p, 0:nb]))
            eng.wait_ge(st.sem, st.all())
            quant_divide(eng, X, p, parts, n)

        def quant_divide(eng, X, p, parts, n):
            eng.tensor_tensor(qv[0:parts, p, 0:n].rearrange("p (b c) -> p b c", c=QB),
                              X.rearrange("p (b c) -> p b c", c=QB), bcast(qrc[0:parts, p, 0:n // QB], QB),
                              ALU.mult).then_inc(quant_v, 1)

        def quant_abs(eng, p, parts, n, k):
            eng.wait_ge(quant_v, k + 2)
            eng.activation(qa[0:parts, p, 0:n], qv[0:parts, p, 0:n], ACT.Abs).then_inc(quant_a, 1)
            eng.activation(qs[0:parts, p, 0:n], qv[0:parts, p, 0:n], ACT.Sign).then_inc(quant_a, 1)

        def quant_count(eng, st, p, parts, n, k):
            a, c, t = qa[0:parts, p, 0:n], qc[0:parts, p, 0:n], qv[0:parts, p, 0:n]
            eng.wait_ge(quant_a, 2 * k + 3)
            st(eng.tensor_scalar(c, a, 5.0, 2.0, ALU.is_gt, ALU.mult))
            st(eng.tensor_scalar(t, a, 0.25, None, ALU.is_gt))
            eng.wait_ge(st.sem, st.all())
            for m in (3.5, 2.5):
                st(eng.scalar_tensor_tensor(c, a, m, c, ALU.is_gt, ALU.add))
                eng.wait_ge(st.sem, st.all())
            st(eng.scalar_tensor_tensor(c, c, 2.0, t, ALU.mult, ALU.add))
            eng.wait_ge(st.sem, st.all())
            for m in (1.75, 1.25):
                st(eng.scalar_tensor_tensor(c, a, m, c, ALU.is_gt, ALU.add))
                eng.wait_ge(st.sem, st.all())
            eng.scalar_tensor_tensor(c, a, 0.75, c, ALU.is_gt, ALU.add).then_inc(quant_c, 1)

        def quant_finish(eng, st, X, p, parts, n, k):
            nb = n // QB
            eng.wait_ge(quant_a, 2 * k + 3)
            st(eng.tensor_tensor(qh[0:parts, p, 0:n].rearrange("p (b c) -> p b c", c=QB),
                                 qs[0:parts, p, 0:n].rearrange("p (b c) -> p b c", c=QB),
                                 bcast(qhs[0:parts, p, 0:nb], QB), ALU.mult))
            eng.wait_ge(quant_c, k + 2)
            eng.wait_ge(st.sem, st.all())
            eng.tensor_tensor(X, qc[0:parts, p, 0:n], qh[0:parts, p, 0:n], ALU.mult).then_inc(quant_out, 1)

        wjobs = [("g", GR, 2 * E, i) for i in range(NGR // 2)] + [("u", GR, 2 * E, i) for i in range(NGR // 2)] \
            + [("d", 128, FF, i) for i in range(2)]
        NQ0 = len(wjobs)
        XQ = 2
        NXQ = T // XQ
        TROOTS = 3 + NXQ
        QPB = NXQ + T

        def wsrc(kind, i):
            if kind == "d":
                return raw_wd[:, i, :]
            return (raw_wg if kind == "g" else raw_wu)[0:GR, 2 * i:2 * i + 2, :].rearrange("p a b -> p (a b)")

        def ctx_tiles(eng, body):
            with eng.Fori(0, CMAIN // 4) as it:
                for q in range(4):
                    body(4 * it + q, q)
            for i in range(CMAIN, CT):
                body(i, i % 4)

        CMAIN = (CT - 2) // 4 * 4
        POOL_EDGES = 3
        AHEAD = HG

        CSTEP = CT + 3

        def cdone(b, i):
            return b * CSTEP + i + 5

        def is_last(i):
            return isinstance(i, int) and i == CT - 1

        def crows(i):
            return CLAST if is_last(i) else 128

        def cinc(i):
            return 4 if is_last(i) else 1

        def exists(i):
            return not isinstance(i, int) or i < CT

        with nc.Block() as first:
            @first.sync
            def _(sp):
                for which, value in starts:
                    sp.sem_inc(which, value)

        block = ctx.enter_context(nc.Block())

        @block.sync
        def _(sp):
            n_attn = 0
            for dst, src in ((ident, "ident"), (mass_mask, "mass_mask"), (pair_mask, "pair_mask"), (pack, "pack"),
                             (rows, "rows"), (cols, "cols"), (bdk, "bdk"), (bdv, "bdv"), (bdr, "bdr")):
                sp.dma_start(dst[:], d[src]).then_inc(consts_loaded, 16)
            sp.dma_start(rel0, d["rel0"]).then_inc(consts_loaded, 16)
            sp.dma_start(mask32, d["right_mask"]).then_inc(consts_loaded, 16)
            for dst, src in ((raw_wg[0:GR], "w_gate"), (raw_wu[0:GR], "w_up"), (raw_wd[:], "w_down")):
                sp.dma_start(dst, d[src]).then_inc(ffn_w_loaded, 16)
            for dst, src in ((wq_s, "wq"), (wk_s, "wk"), (wv_s, "wv"), (wo_s, "wo")):
                sp.dma_start(dst[:], d[src]).then_inc(attn_w_loaded, 16)
            for dst, src in ((cwk, "cwk"), (cwv, "cwv"), (cwo, "cwo"), (cwq, "cwq"), (w1, "w1"), (w2, "w2")):
                sp.dma_start(dst[:], d[src]).then_inc(ctx_w_loaded, 16)
            sp.wait_ge(setup_pool, START_MEMSETS + 1)
            for t in range(T):
                sp.dma_start(bias_scr[t].rearrange("h (p r) -> p h r", r=SKEW),
                             arena[:, 0:H * SKEW].rearrange("p (h r) -> p h r", r=SKEW)).then_inc(zeros_stored, 16)
            sp.wait_ge(zeros_stored, 16 * T + 1)
            sp.dma_start(xin[:], d["x"][0].rearrange("(t p) e -> p t e", p=128)).then_inc(x_loaded, 16)
            with sp.Fori(0, NB) as b:
                def load_ctx(i, q):
                    n, p = crows(i), q % 2
                    sp.wait_ge(caff_ready, cdone(b, i - 2) + 1)
                    sp.sem_inc(waits_alone, 1)
                    sp.dma_start(cin[0:n, p, :], d["ctx"][ds(b, 1), ds(i * 128, n), :].rearrange("o p e -> (o p) e"))\
                        .then_inc(ctx_loaded[p], 16)

                sp.wait_ge(xnT_ready, 2 * (b + 1) + 1)
                sp.sem_inc(waits_alone, 1)
                load_ctx(0, 0)
                load_ctx(1, 1)
                load_ctx(2, 2)
                for t in range(T):
                    sp.wait_ge(r_act, T * b + t + 2)
                    sp.sem_inc(waits_alone, 1)
                    sp.wait_ge(r_dve, T * b + t + 2)
                    sp.sem_inc(waits_alone, 1)
                    sp.dma_start(bias_scr[t].rearrange("h (p r) -> p h r", r=SKEW)[:, :, 0:BAND],
                                 Rb[:, t, :, 0:BAND]).then_inc(bias_stored, 16)
                sp.wait_ge(part1_ready, 2 * (b + 1) + 1)
                sp.sem_inc(waits_alone, 1)
                sp.wait_ge(part2_ready, 2 * (b + 1) + 1)
                sp.sem_inc(waits_alone, 1)
                for parts, scr in ((qparts, q_scr), (kparts, k_scr)):
                    for i in range(PARTS):
                        sp.dma_start(scr[i].rearrange("(c r) s -> r c s", c=2), parts[:, i, :, :]).then_inc(parts_stored, 16)

                def more_ctx(i, q):
                    if exists(i + 3):
                        load_ctx(i + 3, q + 3)
                ctx_tiles(sp, more_ctx)
                sp.wait_ge(parts_stored, 16 * 2 * PARTS * (b + 1) + 1)
                sp.sem_inc(waits_alone, 1)

                def load_q(t, g):
                    for slot, part in enumerate(SLOTS_Q):
                        sp.dma_start(Qp[slot * HD:(slot + 1) * HD, g * HG:(g + 1) * HG, :],
                                     q_scr[part, g * HG * HD:(g + 1) * HG * HD, ds(t * 128, 128)]
                                     .rearrange("(h d) s -> d h s", d=HD)).then_inc(q_loaded[g], 16)

                for slot, part in enumerate(SLOTS_K):
                    sp.dma_start(Kp[slot * HD:(slot + 1) * HD, :, :], k_scr[part].rearrange("(h d) s -> d h s", d=HD))\
                        .then_inc(k_loaded, 16)
                for g in range(NG):
                    load_q(0, g)
                sp.wait_ge(bias_stored, 16 * T * (b + 1) + 1)
                sp.sem_inc(waits_alone, 1)
                sp.wait_ge(e_ready, b + 2)
                sp.sem_inc(waits_alone, 1)
                sp.wait_ge(cg_done, cdone(b, CT - 1) + 1)
                sp.sem_inc(waits_alone, 1)

                def load_window(t, g):
                    m = (b * T + t) * NG + g
                    sp.wait_ge(bias_filled, m + 2)
                    sp.sem_inc(waits_alone, 1)
                    sp.dma_start(Wn[:, (g % 2) * HG:(g % 2 + 1) * HG, :],
                                 bias_scr[ds(t, 1), g * HG:(g + 1) * HG, 0:128 * WIN]
                                 .rearrange("o h (p r) -> p (o h) r", r=WIN)).then_inc(win_loaded[g % 2], 16)

                def store_probs(t, g):
                    sp.wait_ge(probs_ready, 4 + (b * T + t) * H + (g + 1) * HG + 1)
                    sp.sem_inc(waits_alone, 1)
                    sp.dma_start(prob_scr[ds(t, 1), g * HG:(g + 1) * HG, 0:128 * WIN]
                                 .rearrange("o h (p r) -> p (o h) r", r=WIN),
                                 P[:, (g % 2) * HG:(g % 2 + 1) * HG, ds(t * 128, WIN)]).then_inc(p_stored[g % 2], 16)

                def load_band(t, g):
                    sp.wait_ge(p_stored[g % 2], 16 * ((b * T + t) * 2 + g // 2 + 1) + 1)
                    sp.sem_inc(waits_alone, 1)
                    sp.dma_start(Pband[:, ds(t, 1), g * HG:(g + 1) * HG, :].rearrange("p o h r -> p (o h) r"),
                                 prob_scr[ds(t, 1), g * HG:(g + 1) * HG, :]
                                 .rearrange("o h (p r) -> p (o h) r", r=SKEW)[:, :, 0:BAND]).then_inc(band_loaded, 16)

                def attn_tile(t, last):
                    for g in range(NG):
                        if g + 2 < NG:
                            load_window(t, g + 2)
                        elif not last:
                            load_window(t + 1, g + 2 - NG)
                        if not last:
                            sp.wait_ge(scores_ready, (b * T + t) * H + (g + 1) * HG + 1)
                            sp.sem_inc(waits_alone, 1)
                            load_q(t + 1, g)
                        store_probs(t, g)
                        if g:
                            load_band(t, g - 1)
                    load_band(t, NG - 1)

                load_window(0, 0)
                load_window(0, 1)
                with sp.Fori(0, T - 1) as t:
                    attn_tile(t, False)
                attn_tile(T - 1, True)
                sp.wait_ge(band_loaded, 16 * T * NG * (b + 1) + 1)
                sp.sem_inc(waits_alone, 1)
                sp.wait_ge(y2_res, T * (b + 1) + 1)
                sp.sem_inc(waits_alone, 1)
                sp.dma_start(xin[:], d["x"][ds(b + 1, 1)].rearrange("o (t p) e -> p (o t) e", p=128)).then_inc(x_loaded, 16)
                for t in range(T):
                    sp.wait_ge(out_ready, T * b + t + 2)
                    sp.sem_inc(waits_alone, 1)
                    sp.dma_start(out[ds(b, 1), t * 128:(t + 1) * 128, :].rearrange("o p e -> (o p) e"),
                                 yout[:, t, :]).then_inc(out_stored, 16)
                sp.wait_ge(out_stored, 16 * T * (b + 1) + 1)
                sp.sem_inc(waits_alone, 1)

        @block.gpsimd
        def _(pool):
            st = Steps(pool_start, "pool_start")
            pool.memset(mhalf[:], -0.5).then_inc(setup_pool, 1)
            pool.memset(zeros[:], 0.0).then_inc(setup_pool, 1)
            pool.memset(arena[:, 0:H * SKEW], 0.0).then_inc(setup_pool, 1)
            pool.wait_ge(consts_loaded, 16 * 11 + 1)
            for k, (kind, parts, n, i) in enumerate(wjobs):
                if k >= 2:
                    pool.wait_ge(qwT_psum, k)
                    pool.sem_inc(waits_alone, 1)
                quant_finish(pool, st, qw[0:parts, k % 2, 0:n], k % 2, parts, n, k)
            st.close()
            pool.wait_ge(tables_ready, 7)
            root(pool, rstd[:, 0:T], x_var, x_rstd, 1)
            with pool.Fori(0, NB) as b:
                pool.wait_ge(xn_ready, T * (b + 1) + 1)
                pool.sem_inc(waits_alone, 1)
                pool.tensor_tensor(xin[:], xin[:], rows[:, V_BO:V_BO + 1, :].broadcast_to([128, T, E]), ALU.add)\
                    .then_inc(xb_ready, 1)
                def affine(i, q):
                    n, p = crows(i), q % 2
                    st = Steps(pool_affine, "pool_affine", b * CT + i)
                    root(pool, rstd[0:n, p:p + 1], c_var, c_rstd, b * CT + i + 1)
                    pool.wait_ge(cz_ready, cdone(b, i) + 1)
                    pool.sem_inc(waits_alone, 1)
                    pool.wait_ge(cg_done, cdone(b, i - 4) + 1)
                    pool.sem_inc(waits_alone, 1)
                    st(pool.tensor_tensor(Kn[0:n, q, :], cin[0:n, p, :], rows[0:n, V_G1, :], ALU.mult))
                    pool.wait_ge(st.sem, st.all())
                    pool.sem_inc(waits_alone, 1)
                    pool.tensor_tensor(Kn[0:n, q, :], Kn[0:n, q, :], rows[0:n, V_B1, :], ALU.add)\
                        .then_inc(caff_ready, cinc(i))
                    st.close()

                affine(0, 0)
                affine(1, 1)
                pool.wait_ge(v_ready, 2 * (b + 1) + 1)
                pool.sem_inc(waits_alone, 1)
                pool.tensor_copy(Vcur[:, 0, :], V[:, 0, :]).then_inc(vcur_ready, 1)
                pool.tensor_tensor(Vcur[:, 1:T, :], V[:, 1:T, :],
                                   rows[:, V_EDGE:V_EDGE + 1, :].broadcast_to([128, T - 1, E]), ALU.add).then_inc(vcur_ready, 1)
                pool.wait_ge(r_act, T * (b + 1) + 1)
                pool.sem_inc(waits_alone, 1)
                pool.wait_ge(r_dve, T * (b + 1) + 1)
                pool.sem_inc(waits_alone, 1)
                pool.tensor_copy(edge[:], Rb[:, :, :, BAND]).then_inc(e_ready, 1)
                def norm_root(i, q):
                    root(pool, rn[0:crows(i), q % 2, :], c_norm, c_rnorm, b * CT + i + 1)

                affine(2, 2)
                norm_root(0, 0)

                def ctx_pool(i, q):
                    if exists(i + 3):
                        affine(i + 3, (q + 3) % 4)
                    if exists(i + 1):
                        norm_root(i + 1, q + 1)
                ctx_tiles(pool, ctx_pool)

                pool.wait_ge(cg_done, cdone(b, CT - 1) + 1)
                pool.sem_inc(waits_alone, 1)
                pool.memset(Bt[:, :, 0:PAD], 0.0).then_inc(setup_pool, 1)
                pool.memset(Bt[:, :, PAD + S:ROW], 0.0).then_inc(setup_pool, 1)
                pool.wait_ge(setup_pool, START_MEMSETS + 4 * b + 2 + 1)
                pool.sem_inc(waits_alone, 1)
                def fill(t, g):
                    m = (b * T + t) * NG + g
                    lo = (g % 2) * HG
                    stt = Steps(pool_fill, "pool_fill", m)
                    pool.wait_ge(scores_biased, m * HG + 1)
                    pool.sem_inc(waits_alone, 1)
                    stt(pool.tensor_tensor(
                        Bt[:, lo:lo + POOL_EDGES, PAD:PAD + S],
                        right_mask[:, ds(384 - t * 128, S)].unsqueeze(1).broadcast_to([128, POOL_EDGES, S]),
                        bcast(edge[:, ds(t, 1), g * HG:g * HG + POOL_EDGES].rearrange("p o h -> p (o h)"), S), ALU.mult))
                    pool.wait_ge(stt.sem, stt.all())
                    pool.sem_inc(waits_alone, 1)
                    pool.wait_ge(win_loaded[g % 2], 16 * ((b * T + t) * 2 + g // 2 + 1) + 1)
                    pool.sem_inc(waits_alone, 1)
                    pool.wait_ge(edge_filled, (HG - POOL_EDGES) * (m + 1) + 1)
                    pool.sem_inc(waits_alone, 1)
                    pool.tensor_tensor(Bt[:, lo:lo + HG, ds(t * 128, WIN)], Bt[:, lo:lo + HG, ds(t * 128, WIN)],
                                       Wn[:, lo:lo + HG, :], ALU.add).then_inc(bias_filled, 1)

                def attn_pool(t, last):
                    for g in range(NG):
                        if g + 2 < NG:
                            fill(t, g + 2)
                        elif not last:
                            fill(t + 1, g + 2 - NG)

                fill(0, 0)
                fill(0, 1)
                pool.wait_ge(m_dve, 4 * (b + 1) + 1)
                pool.sem_inc(waits_alone, 1)
                pool.wait_ge(m_act, 4 * (b + 1) + 1)
                pool.sem_inc(waits_alone, 1)
                pool.memset(P[:, :, 0:PAD], 0.0).then_inc(setup_pool, 1)
                pool.memset(P[:, :, PAD + S:ROW], 0.0).then_inc(setup_pool, 1)
                with pool.Fori(0, T - 1) as t:
                    attn_pool(t, False)
                attn_pool(T - 1, True)
                st = Steps(pool_tail, "pool_tail", b)
                root(pool, rstd[:, 0:T], t_var, t_rstd, TROOTS * b + 1)
                root(pool, rstd2[:], t_var, t_rstd, TROOTS * b + 2)
                for t in range(T):
                    pool.wait_ge(qx_ready, T * b + t + 2)
                    pool.sem_inc(waits_alone, 1)
                    pool.tensor_tensor(yr[:, t, :], Qx[:, t, :], rows[:, V_XBO, :], ALU.add).then_inc(y_res, 1)
                for t in range(T):
                    root(pool, rn[:, t % 2, :], q_norm, q_rnorm, T * b + t + 1)
                root(pool, rstd[:, 0:T], t_var, t_rstd, TROOTS * b + 3)
                for t in range(T):
                    pool.wait_ge(y_ready, T * b + t + 2)
                    pool.sem_inc(waits_alone, 1)
                    st(pool.tensor_tensor(yr[:, t, :], y[:, t, :], rows[:, V_XB2, :], ALU.add))
                    pool.wait_ge(st.sem, st.all())
                    pool.sem_inc(waits_alone, 1)
                    pool.tensor_tensor(yr[:, t, :], yr[:, t, :], xin[:, t, :], ALU.add).then_inc(y2_res, 1)
                for i in range(NXQ):
                    root(pool, rstd[:, XQ * i:XQ * (i + 1)], t_var, t_rstd, TROOTS * b + 4 + i)
                    quant_finish(pool, st, xq[:, XQ * i:XQ * (i + 1), :].rearrange("p a b -> p (a b)"), i % 2, 128, XQ * E,
                                 NQ0 + b * QPB + i)
                for t in range(T + 1):
                    if t < T:
                        pool.wait_ge(quant_s, 2 * (T * b + t + 1) + 1)
                        pool.sem_inc(waits_alone, 1)
                        quant_divide(pool, gs[:, t, :], t % 2, 128, FF)
                    if t:
                        if t >= 3:
                            pool.wait_ge(ht_psum, T * b + t - 1)
                            pool.sem_inc(waits_alone, 1)
                        quant_finish(pool, st, hq[:, (t - 1) % 2, :], (t - 1) % 2, 128, FF, NQ0 + b * QPB + NXQ + t - 1)
                st.close()
                root(pool, rstd[:, 0:T], x_var, x_rstd, b + 2)

        @block.scalar
        def _(act):
            for k, (kind, parts, n, i) in enumerate(wjobs):
                quant_abs(act, k % 2, parts, n, k)
            with act.Fori(0, NB) as b:
                act.wait_ge(xnT_psum, 2 * b + 2)
                act.sem_inc(waits_alone, 1)
                act.activation(xnT[:, 0, :], bank(0), ACT.Copy).then_inc(xnT_ready, 1)
                for c in range(2):
                    act.wait_ge(k_psum, 2 * b + c + 2)
                    act.activation(KT[:, c, :], bank(2 + c), ACT.Identity, bias=cols[:, 2 + c:3 + c]).then_inc(kT_ready, 1)
                act.wait_ge(kT_ready, 2 * (b + 1) + 1)
                act.activation(kparts[:, 0], KT[:], ACT.Copy).then_inc(part0_ready, 1)
                for j in range(2):
                    act.wait_ge(v_psum, 2 * b + j + 2)
                    act.activation(V[:, 2 * j:2 * j + 2, :].rearrange("p a b -> p (a b)"), bank(6 + j), ACT.Copy)\
                        .then_inc(v_ready, 1)
                act.wait_ge(qT_ready, 2 * (b + 1) + 1)
                act.activation(qparts[:, 0], QT[:], ACT.Copy).then_inc(part0_ready, 1)
                act.wait_ge(rest_ready, 2 * b + 2)
                act.activation(kparts[:, 1], Krest[:], ACT.Copy).then_inc(part1_ready, 1)
                act.wait_ge(out_stored, 16 * T * b + 1)
                for t in range(T):
                    act.wait_ge(r_psum, 8 * b + 2 * t + 2)
                    act.activation(Rb[:, t, 0:8, :].rearrange("p h r -> p (h r)"), bank(4 + 2 * t % 4, 0, 8 * NREL), ACT.Copy)\
                        .then_inc(r_act, 1)

                def copy_ct(i, p):
                    n = crows(i)
                    act.wait_ge(ct_psum, cdone(b, i) + 1)
                    act.wait_ge(ck_psum, cdone(b, i - 2) + 1)
                    act.activation(cnT[:, p, :, 0:n],
                                   bank(6 + p, 0, 256).rearrange("p (c t) -> p c t", c=2)[:, :, 0:n], ACT.Copy)\
                        .then_inc(ct_ready, cinc(i))

                def copy_k(i, q):
                    n = crows(i)
                    act.wait_ge(ck_psum, cdone(b, i) + 1)
                    act.wait_ge(cg_done, cdone(b, i - 4) + 1)
                    act.activation(kns[0:n, q, :], PS[0:n, 4 * 512:6 * 512], ACT.Copy).then_inc(kc_ready, cinc(i))

                def square(i, q):
                    n = crows(i)
                    act.wait_ge(kc_ready, cdone(b, i) + 1)
                    act.wait_ge(c_norm, b * CT + i + 1)
                    act.activation(csq[0:n], kns[0:n, q, :], ACT.Square).then_inc(csq_ready, cinc(i))

                copy_ct(0, 0)
                copy_ct(1, 1)
                act.wait_ge(rest_ready, 2 * b + 3)
                act.activation(qparts[:, 1], Qrest[:], ACT.Copy).then_inc(part1_ready, 1)
                act.wait_ge(part2_ready, 2 * (b + 1) + 1)
                copy_k(0, 0)
                square(0, 0)
                copy_ct(2, 0)
                copy_k(1, 1)
                square(1, 1)

                def ctx_act(i, q):
                    if exists(i + 2):
                        copy_k(i + 2, (q + 2) % 4)
                    if exists(i + 3):
                        copy_ct(i + 3, (q + 3) % 2)
                    if exists(i + 2):
                        square(i + 2, (q + 2) % 4)
                ctx_tiles(act, ctx_act)
                act.wait_ge(cg_done, cdone(b, CT - 1) + 1)
                act.wait_ge(parts_stored, 16 * 2 * PARTS * (b + 1) + 1)
                for j in (0, 2):
                    act.activation(Gs[:, 2 * j:2 * j + 2, :].rearrange("p a b -> p (a b)"), bank(j), ACT.Copy).then_inc(g_act, 1)
                for c in range(2):
                    act.wait_ge(gt_psum, 4 * b + 2 * c + 2)
                    act.activation(GT[:, c, 0:4, :].rearrange("p a b -> p (a b)"), bank(4 + 2 * c), ACT.Copy).then_inc(gt_act, 1)
                def edges(t, g):
                    m = (b * T + t) * NG + g
                    act.wait_ge(scores_biased, m * HG + 1)
                    for j in range(POOL_EDGES, HG):
                        act.activation(Bt[:, (g % 2) * HG + j, PAD:PAD + S], right_mask[:, ds(384 - t * 128, S)], ACT.Copy,
                                       scale=edge[:, ds(t, 1), g * HG + j]).then_inc(edge_filled, 1)

                act.wait_ge(e_ready, b + 2)
                act.wait_ge(setup_pool, START_MEMSETS + 4 * b + 2 + 1)
                edges(0, 0)
                edges(0, 1)
                for j in (0, 2):
                    act.wait_ge(m_psum, 4 * b + j + 2)
                    act.activation(M[:, 2 * j:2 * j + 2, :].rearrange("p a b -> p (a b)"), bank(2 + j), ACT.Copy)\
                        .then_inc(m_act, 2)
                act.wait_ge(m_dve, 4 * (b + 1) + 1)
                act.wait_ge(setup_pool, START_MEMSETS + 4 * (b + 1) + 1)
                def exps(t, h):
                    g, j = divmod(h, HG)
                    tile = b * T + t
                    u, m = tile * H + h, tile * NG + g
                    if j == 0:
                        act.wait_ge(transposed, m * HG + 1)
                        act.wait_ge(mass_ready, m + 2)
                        act.wait_ge(p_stored[g % 2], 16 * (tile * 2 + g // 2) + 1)
                    act.wait_ge(scores_biased, 4 + u + 2)
                    act.activation(P[:, (g % 2) * HG + j, PAD:PAD + S], Sb[:, j, :], ACT.Exp, bias=nmax[:, j:j + 1],
                                   scale=-1.0, accum_out=lsum[:, ds(t, 1), h]).then_inc(probs_ready, 1)

                def evac(t, h):
                    act.wait_ge(transposed, 4 + (b * T + t) * H + h + 2)
                    act.wait_ge(pv_done, (b * T + t) * H + h + 2)
                    act.activation(PTs[:, 0, :], bank(4), ACT.Copy).then_inc(pt_copied[0], 1)

                def attn_act(t, last):
                    for h in range(H):
                        if h + AHEAD < H:
                            exps(t, h + AHEAD)
                        elif not last:
                            exps(t + 1, h + AHEAD - H)
                        if h % HG == HG - 1:
                            g = h // HG + 3
                            if g < NG:
                                edges(t, g)
                            elif not last:
                                edges(t + 1, g - NG)
                        if h % 2 == 0:
                            evac(t, h)
                    act.wait_ge(pv_done, 2 + (b * T + t + 1) * H + 1)
                    if not last:
                        act.activation(Vcur[:, ds(t + 1, 1), :], V[:, ds(t + 1, 1), :], ACT.Copy).then_inc(vcur_moved, 1)
                    act.activation(OT[:, ds(t, 1), :].rearrange("p o e -> p (o e)"), bank(6), ACT.Copy).then_inc(o_evac, 1)

                for h in range(AHEAD):
                    exps(0, h)
                edges(0, 2)
                with act.Fori(0, T - 1) as t:
                    attn_act(t, False)
                attn_act(T - 1, True)
                for t in range(T):
                    act.wait_ge(fa_psum, 2 * (T * b + t) + 2)
                    if t >= 2:
                        act.wait_ge(f_psum, T * b + t)
                    act.activation(AT[:, t % 2, 0:4, :].rearrange("p a b -> p (a b)"), bank(2 * (t % 2)), ACT.Copy)\
                        .then_inc(fa_act, 1)
                for t in range(T):
                    act.wait_ge(at_psum, T * b + t + 2)
                    if t >= 2:
                        act.wait_ge(wo_psum, T * b + t)
                    act.activation(aT[:, t % 2, :, :].rearrange("p a b -> p (a b)"), bank(6 + t % 2, 0, 256), ACT.Copy)\
                        .then_inc(aT_ready, 1)
                act.wait_ge(qnT_psum, 2 * b + 2)
                act.activation(QnT[:, 0, :], bank(0), ACT.Identity, bias=cols[:, C_B1:C_B1 + 1], scale=cols[:, C_G1:C_G1 + 1]).then_inc(qnT_ready, 1)
                for t in range(T + 1):
                    if t < T:
                        act.wait_ge(xq_psum, T * b + t + 2)
                        if t:
                            act.wait_ge(qn_ready, T * b + t + 1)
                        act.activation(sq, PS[:, (2 + 2 * (t % 2)) * 512:(4 + 2 * (t % 2)) * 512], ACT.Square).then_inc(sq_ready, 1)
                    if t:
                        act.wait_ge(qt_psum, 2 * (T * b + t - 1) + 2)
                        if t >= 2:
                            act.wait_ge(o_psum, T * b + t)
                        act.activation(qnT[:, 0:4, :].rearrange("p a b -> p (a b)"), bank(6), ACT.Copy).then_inc(qt_act, 1)
                act.wait_ge(ynT_psum, 2 * b + 2)
                act.activation(ynT[:, 0, :], bank(2), ACT.Identity, bias=cols[:, C_B2:C_B2 + 1], scale=cols[:, C_G2:C_G2 + 1]).then_inc(ynT_ready, 1)
                for f in range(NF):
                    act.wait_ge(h_psum, NF * b + f + 2)
                    act.activation(hT[:, f, :], bank(4 + f % 4), ACT.Gelu, bias=cols[:, 4 + f:5 + f]).then_inc(h_ready, 1)
                def copy_xq(i):
                    act.wait_ge(xqT_psum, NXQ * b + i + 2)
                    act.activation(xqT[:, :, XQ * i * 128:XQ * (i + 1) * 128],
                                   PS[:, (6 + i) * 512:(7 + i) * 512].rearrange("p (c t) -> p c t", c=2), ACT.Copy).then_inc(xqT_ready, 1)

                quant_abs(act, 0, 128, XQ * E, NQ0 + b * QPB)
                copy_xq(0)
                quant_abs(act, 1, 128, XQ * E, NQ0 + b * QPB + 1)
                for t in range(T + 2):
                    if t == 1:
                        copy_xq(1)
                    if t < T:
                        act.wait_ge(gu_psum, T * b + t + 2)
                        g0 = (t % 2) * 3 * 512
                        act.activation(gs[:, t, :], PS[:, g0:g0 + FF], ACT.Silu).then_inc(silu_ready, 1)
                    if 1 <= t <= T:
                        quant_abs(act, (t - 1) % 2, 128, FF, NQ0 + b * QPB + NXQ + t - 1)
                    if t >= 2:
                        act.wait_ge(ht_psum, T * b + t)
                        if t >= 4:
                            act.wait_ge(dn_psum, T * b + t - 3 + 1)
                        act.activation(hqT[:, t % 2, 0:4, :].rearrange("p a b -> p (a b)"), bank(6), ACT.Copy).then_inc(ht_ready, 1)
                        act.activation(hqT[:, t % 2, 4, :], bank(7, 0, 128), ACT.Copy).then_inc(ht_ready, 1)
                        act.activation(hqT[0:FLAST, t % 2, 5, :], bank(7, 128, 256, FLAST), ACT.Copy).then_inc(ht_ready, 1)

        @block.vector
        def _(dve):
            st = Steps(dve_start, "dve_start")
            dve.wait_ge(consts_loaded, 16 * 11 + 1)
            dve.sem_inc(waits_alone, 1)
            dve.tensor_copy(right_mask[:], mask32).then_inc(tables_ready, 1)
            o = HC * NREL
            dve.tensor_tensor(bdk[:], bdk[:], rel0[:, 0:o], ALU.subtract).then_inc(tables_ready, 1)
            dve.tensor_tensor(bdv[:].rearrange("p a b -> p (a b)"), bdv[:].rearrange("p a b -> p (a b)"),
                              rel0[:, o:o + 320], ALU.subtract).then_inc(tables_ready, 1)
            o += 320
            dve.tensor_tensor(bdr[:], bdr[:], rel0[0:16, o:o + E], ALU.subtract).then_inc(tables_ready, 1)
            dve.tensor_tensor(rows[:, V_EDGE, :], rows[:, V_EDGE, :], rel0[:, o + E:o + 2 * E], ALU.subtract)\
                .then_inc(tables_ready, 1)
            dve.tensor_tensor(rows[:, V_BV, :], rows[:, V_BV, :], rel0[:, o + E:o + 2 * E], ALU.add).then_inc(tables_ready, 1)
            dve.wait_ge(ffn_w_loaded, 16 * 3 + 1)
            def wcopy(k):
                kind, parts, n, i = wjobs[k]
                dve.wait_ge(qwT_psum, k + 2)
                if kind == "d":
                    src = PS[:, 0:1024].rearrange("p (c r) -> p c r", r=128)
                    dve.tensor_copy(wdT[:, 0:5, i * 128:(i + 1) * 128], src[:, 0:5, :]).then_inc(qwT_ready, 1)
                    dve.tensor_copy(wdT[0:FLAST, 5, i * 128:(i + 1) * 128], src[0:FLAST, 5, :]).then_inc(qwT_ready, 1)
                else:
                    dst = wgT if kind == "g" else wuT
                    src = PS[:, 0:1024].rearrange("p (a c r) -> p a c r", a=2, c=4)
                    for a in range(2):
                        dve.tensor_copy(dst[:, :, (2 * i + a) * GR:(2 * i + a + 1) * GR], src[:, a, 0:2, 0:GR]).then_inc(qwT_ready, 1)
            for k, (kind, parts, n, i) in enumerate(wjobs):
                quant_scale(dve, st, wsrc(kind, i), k % 2, parts, n, k)
                if k:
                    _, pp, nn, _ = wjobs[k - 1]
                    quant_count(dve, st, (k - 1) % 2, pp, nn, k - 1)
                if k >= 2:
                    wcopy(k - 2)
            k = len(wjobs)
            quant_count(dve, st, (k - 1) % 2, wjobs[-1][1], wjobs[-1][2], k - 1)
            wcopy(k - 2)
            wcopy(k - 1)
            st.close()
            dve.wait_ge(tables_ready, 7)
            dve.wait_ge(zeros_stored, 16 * T + 1)

            def norm_x(b):
                st = Steps(dve_prep, "dve_prep", b)
                dve.wait_ge(x_loaded, 16 * (b + 1) + 1)
                dve.sem_inc(waits_alone, 1)
                layernorm(dve, st, [xin[:, t, :] for t in range(T)], [xn[:, t, :] for t in range(T)], xn_ready,
                          x_var, x_rstd, b + 1)
                st.close()

            norm_x(0)
            with dve.Fori(0, NB) as b:
                dve.wait_ge(xnT_psum, 2 * b + 3)
                dve.tensor_copy(xnT[:, 1, :], bank(1)).then_inc(xnT_ready, 1)
                for c in range(2):
                    dve.wait_ge(q_psum, 2 * b + c + 2)
                    dve.tensor_scalar(QT[:, c, :], bank(4 + c), cols[:, c:c + 1], None, ALU.add).then_inc(qT_ready, 1)
                def norm_stats(i, p):
                    n = crows(i)
                    st = Steps(dve_norm, "dve_norm", b * CT + i)
                    per = (CT + 1) // 2 if p == 0 else CT // 2
                    dve.wait_ge(ctx_loaded[p], 16 * per * b + 8 * (i - p) + 17)
                    st(dve.bn_stats(bnst[0:n, p, :], cin[0:n, p, :]))
                    dve.wait_ge(st.sem, st.all())
                    dve.sem_inc(waits_alone, 1)
                    st(dve.bn_aggr(mv[0:n, p, :], bnst[0:n, p, :]))
                    dve.wait_ge(st.sem, st.all())
                    dve.tensor_scalar(rstd[0:n, p:p + 1], mv[0:n, p, 1:2], EPS, None, ALU.add).then_inc(c_var, 1)
                    st.close()

                def norm_apply(i, p):
                    n = crows(i)
                    x = cin[0:n, p, :]
                    dve.wait_ge(c_rstd, b * CT + i + 2)
                    dve.tensor_scalar(x, x, mv[0:n, p, 0:1], rstd[0:n, p:p + 1], ALU.subtract, ALU.mult)\
                        .then_inc(cz_ready, cinc(i))

                dve.wait_ge(part0_ready, 2 * b + 2)
                dve.wait_ge(kT_ready, 2 * (b + 1) + 1)
                dve.tensor_tensor(Krest[:], KT[:], kparts[:, 0], ALU.subtract).then_inc(rest_ready, 1)
                for i in range(2):
                    norm_stats(i, i % 2)
                    norm_apply(i, i % 2)
                dve.wait_ge(out_stored, 16 * T * b + 1)
                for t in range(T):
                    dve.wait_ge(r_psum, 8 * b + 2 * t + 3)
                    dve.tensor_copy(Rb[:, t, 8:16, :].rearrange("p h r -> p (h r)"), bank(5 + 2 * t % 4, 0, 8 * NREL))\
                        .then_inc(r_dve, 1)
                norm_stats(2, 0)
                norm_apply(2, 0)
                dve.wait_ge(part0_ready, 2 * b + 3)
                dve.tensor_tensor(Qrest[:], QT[:], qparts[:, 0], ALU.subtract).then_inc(rest_ready, 1)
                for i, (parts, rest) in enumerate(((kparts, Krest), (qparts, Qrest))):
                    dve.wait_ge(part1_ready, 2 * b + i + 2)
                    dve.tensor_tensor(parts[:, 2], rest[:], parts[:, 1], ALU.subtract).then_inc(part2_ready, 1)

                def sum_squares(i, p):
                    n = crows(i)
                    st = Steps(dve_scale, "dve_scale", b * CT + i)
                    dve.wait_ge(csq_ready, cdone(b, i) + 1)
                    st(dve.tensor_reduce(ss[0:n, p, :], csq[0:n].rearrange("p (h c) -> p h c", c=XD), AX.X, ALU.add))
                    dve.wait_ge(st.sem, st.all())
                    dve.tensor_scalar(rn[0:n, p, :], ss[0:n, p, :], 1e-24, None, ALU.max).then_inc(c_norm, 1)
                    st.close()

                def scale_k(i, q):
                    n = crows(i)
                    dve.wait_ge(c_rnorm, b * CT + i + 2)
                    k = kns[0:n, q, :].rearrange("p (h c) -> p h c", c=XD)
                    dve.tensor_tensor(k, k, bcast(rn[0:n, q % 2, :], XD), ALU.mult).then_inc(cs_ready, cinc(i))

                sum_squares(0, 0)

                def ctx_dve(i, q):
                    if exists(i + 3):
                        norm_stats(i + 3, (q + 3) % 2)
                    if exists(i + 1):
                        sum_squares(i + 1, (q + 1) % 2)
                    if exists(i + 3):
                        norm_apply(i + 3, (q + 3) % 2)
                    scale_k(i, q)
                ctx_tiles(dve, ctx_dve)
                dve.wait_ge(cg_done, cdone(b, CT - 1) + 1)
                dve.wait_ge(parts_stored, 16 * 2 * PARTS * (b + 1) + 1)
                for j in (1, 3):
                    dve.tensor_copy(Gs[:, 2 * j:2 * j + 2, :].rearrange("p a b -> p (a b)"), bank(j)).then_inc(g_dve, 1)
                for c in range(2):
                    dve.wait_ge(gt_psum, 4 * b + 2 * c + 3)
                    dve.tensor_copy(GT[:, c, 4:8, :].rearrange("p a b -> p (a b)"), bank(5 + 2 * c)).then_inc(gt_dve, 1)
                for j in range(2):
                    dve.wait_ge(kvt_psum, 2 * b + j + 2)
                    dve.tensor_tensor(KVT[:, 4 * j:4 * j + 4, :], bank(j).rearrange("p (a b) -> p a b", a=4),
                                      pair_mask[:].unsqueeze(1).broadcast_to([128, 4, 128]), ALU.mult).then_inc(kvt_ready, 1)
                for j in (1, 3):
                    dve.wait_ge(m_psum, 4 * b + j + 2)
                    dve.tensor_copy(M[:, 2 * j:2 * j + 2, :].rearrange("p a b -> p (a b)"), bank(2 + j)).then_inc(m_dve, 2)
                dve.wait_ge(m_act, 4 * (b + 1) + 1)
                dve.sem_inc(waits_alone, 1)
                def bias(t, h):
                    g, j = divmod(h, HG)
                    tile = b * T + t
                    u = tile * H + h
                    if j == 0:
                        dve.wait_ge(bias_filled, 2 + tile * NG + g + 2)
                    dve.wait_ge(scores_ready, u + 2)
                    dve.wait_ge(probs_ready, u + 2)
                    dve.sem_inc(waits_alone, 1)
                    dve.tensor_tensor_reduce(out=Sb[:, j, :], in0=bank(j), in1=Bt[:, (g % 2) * HG + j, PAD:PAD + S],
                                             scale=-0.25, scalar=BIG, op0=ALU.add, op1=ALU.min,
                                             accum_out=nmax[:, j:j + 1]).then_inc(scores_biased, 1)

                def evac(t, h):
                    dve.wait_ge(transposed, 4 + (b * T + t) * H + h + 2)
                    dve.wait_ge(pv_done, (b * T + t) * H + h + 2)
                    dve.tensor_copy(PTs[:, 1, :], bank(5)).then_inc(pt_copied[1], 1)

                def edge_mass(t, g):
                    m = (b * T + t) * NG + g
                    dve.wait_ge(probs_ready, 4 + (m + 1) * HG + 1)
                    dve.wait_ge(mass_ready, m + 3)
                    dve.tensor_tensor(prod[:], P[:, (g % 2) * HG:(g % 2 + 1) * HG, ds(t * 128 + BAND, 128)],
                                      mass_mask[:].unsqueeze(1).broadcast_to([128, HG, 128]), ALU.mult).then_inc(mass_mul, 1)
                    dve.wait_ge(mass_mul, m + 2)
                    dve.tensor_reduce(mass[:, ds(t, 1), g * HG:(g + 1) * HG].rearrange("p o h -> p (o h)"), prod, AX.X, ALU.add)\
                        .then_inc(mass_ready, 1)

                def attn_dve(t, last):
                    for h in range(H):
                        if h + AHEAD < H:
                            bias(t, h + AHEAD)
                        elif not last:
                            bias(t + 1, h + AHEAD - H)
                        if h % HG == HG - 1:
                            edge_mass(t, h // HG)
                        if h % 2 == 1:
                            evac(t, h)

                for h in range(AHEAD):
                    bias(0, h)
                with dve.Fori(0, T - 1) as t:
                    attn_dve(t, False)
                attn_dve(T - 1, True)
                st = Steps(dve_attn, "dve_attn", b)
                dve.wait_ge(probs_ready, 4 + T * H * (b + 1) + 1)
                st(dve.reciprocal(rl[:], lsum[:]))

                def copy_band(t):
                    dve.wait_ge(fa_psum, 2 * (T * b + t) + 3)
                    if t >= 2:
                        dve.wait_ge(f_psum, T * b + t)
                    dve.tensor_copy(AT[:, t % 2, 4, :], bank(2 * (t % 2) + 1, 0, 128)).then_inc(fa_dve, 1)
                    dve.tensor_copy(massT[0:H, t % 2, :], bank(2 * (t % 2) + 1, 128, 256, H)).then_inc(fa_dve, 1)

                def combine(t):
                    dve.wait_ge(f_psum, T * b + t + 2)
                    if t == 0:
                        dve.wait_ge(st.sem, st.all())
                    st(dve.tensor_tensor(Oraw[:, t, :].rearrange("p (h c) -> p h c", c=HD),
                                         bank(4 + t % 2, 0, E).rearrange("p (h c) -> p h c", c=HD), bcast(rl[:, t, :], HD),
                                         ALU.mult))
                    dve.wait_ge(st.sem, st.all())
                    dve.tensor_tensor(Oraw[:, t, :], Oraw[:, t, :], rows[:, V_BV, :], ALU.add).then_inc(attn_ready, 1)

                copy_band(0)
                for t in range(T):
                    if t + 1 < T:
                        copy_band(t + 1)
                    combine(t)
                tail = Steps(dve_tail, "dve_tail", b)
                for t in range(T):
                    dve.wait_ge(wo_psum, T * b + t + 2)
                    dve.wait_ge(xb_ready, b + 2)
                    dve.tensor_tensor(xin[:, t, :], xin[:, t, :], bank(4 + t % 2, 0, E), ALU.add).then_inc(x1_ready, 1)
                    dve.wait_ge(x1_ready, T * b + t + 2)
                    tail(dve.bn_stats(bnst[:, t, :], xin[:, t, :]))
                st.close()
                st = tail
                tiles = range(T)
                dve.wait_ge(st.sem, st.all())
                dve.sem_inc(waits_alone, 1)
                for t in tiles:
                    st(dve.bn_aggr(mv[:, t, :], bnst[:, t, :]))
                dve.wait_ge(st.sem, st.all())
                dve.tensor_scalar(rstd[:, 0:T], mv[:, 0:T, 1], EPS, None, ALU.add).then_inc(t_var, 1)
                dve.wait_ge(t_rstd, TROOTS * b + 2)
                for _ in range(2):
                    st(dve.tensor_tensor(mv[:, 0:T, 1], mv[:, 0:T, 1], rstd[:, 0:T], ALU.mult))
                    dve.wait_ge(st.sem, st.all())
                dve.tensor_scalar(rstd2[:], mv[:, 0:T, 1], EPS, None, ALU.add).then_inc(t_var, 1)
                for t in tiles:
                    dve.tensor_scalar(Qx[:, t, :], xin[:, t, :], mv[:, t, 0:1], rstd[:, t:t + 1], ALU.subtract, ALU.mult)\
                        .then_inc(qx_ready, 1)
                dve.wait_ge(t_rstd, TROOTS * b + 3)
                st(dve.tensor_tensor(rstd2[:], rstd2[:], rstd[:, 0:T], ALU.mult))
                dve.wait_ge(st.sem, st.all())
                for t in tiles:
                    dve.tensor_scalar(Qn[:, t, :], xin[:, t, :], mv[:, t, 0:1], rstd2[:, t:t + 1], ALU.subtract, ALU.mult)\
                        .then_inc(qz_ready, 1)
                dve.wait_ge(qnT_psum, 2 * b + 3)
                dve.tensor_scalar(QnT[:, 1, :], bank(1), cols[:, C_G1 + 1:C_G1 + 2], cols[:, C_B1 + 1:C_B1 + 2], ALU.mult, ALU.add).then_inc(qnT_ready, 1)

                def scale_q(t):
                    p = t % 2
                    dve.wait_ge(sq_ready, T * b + t + 2)
                    st(dve.tensor_reduce(ss[:, p, :], sq.rearrange("p (h c) -> p h c", c=XD), AX.X, ALU.add))
                    dve.wait_ge(st.sem, st.all())
                    dve.tensor_scalar(rn[:, p, :], ss[:, p, :], 1e-24, None, ALU.max).then_inc(q_norm, 1)
                    dve.wait_ge(q_rnorm, T * b + t + 2)
                    if t >= 2:
                        dve.wait_ge(qt_psum, 2 * (T * b + t - 1) + 1)
                    dve.tensor_tensor(qn[:, p, :].rearrange("p (h c) -> p h c", c=XD),
                                      PS[:, (2 + 2 * p) * 512:(4 + 2 * p) * 512].rearrange("p (h c) -> p h c", c=XD),
                                      bcast(rn[:, p, :], XD), ALU.mult).then_inc(qn_ready, 1)

                for t in range(T + 2):
                    if t < T:
                        scale_q(t)
                    if 1 <= t <= T:
                        dve.wait_ge(qt_psum, 2 * (T * b + t - 1) + 3)
                        if t >= 2:
                            dve.wait_ge(o_psum, T * b + t)
                        dve.tensor_copy(qnT[:, 4:8, :].rearrange("p a b -> p (a b)"), bank(7)).then_inc(qt_dve, 1)
                    if t >= 2:
                        dve.wait_ge(o_psum, T * b + t)
                        dve.wait_ge(y_res, T * b + t)
                        dve.tensor_tensor(y[:, t - 2, :], yr[:, t - 2, :], bank(t % 2, 0, E), ALU.add).then_inc(y_ready, 1)
                        dve.wait_ge(y_ready, T * b + t)
                        st(dve.bn_stats(bnst[:, t - 2, :], y[:, t - 2, :]))
                dve.wait_ge(y_ready, T * (b + 1) + 1)
                layernorm(dve, st, [y[:, t, :] for t in tiles], [yn[:, t, :] for t in tiles], yz_ready,
                          t_var, t_rstd, TROOTS * b + 3, have_stats=True)
                dve.wait_ge(ynT_psum, 2 * b + 3)
                dve.tensor_scalar(ynT[:, 1, :], bank(3), cols[:, C_G2 + 1:C_G2 + 2], cols[:, C_B2 + 1:C_B2 + 2], ALU.mult, ALU.add).then_inc(ynT_ready, 1)
                for i in range(NXQ):
                    some = range(XQ * i, XQ * (i + 1))
                    for t in some:
                        dve.wait_ge(m2_psum, T * b + t + 2)
                        dve.wait_ge(y2_res, T * b + t + 2)
                        dve.tensor_tensor(x2[:, t, :], yr[:, t, :], bank(t % 2, 0, E), ALU.add).then_inc(x2_ready, 1)
                    dve.wait_ge(x2_ready, T * b + XQ * (i + 1) + 1)
                    layernorm(dve, st, [x2[:, t, :] for t in some], [zf[:, t, :] for t in some], zf_ready,
                              t_var, t_rstd, TROOTS * b + 4 + i, XQ * i)
                    dve.wait_ge(zf_ready, T * b + XQ * (i + 1) + 1)
                    quant_scale(dve, st, zf[:, XQ * i:XQ * (i + 1), :].rearrange("p a b -> p (a b)"), i % 2, 128, XQ * E,
                                NQ0 + b * QPB + i)
                    quant_count(dve, st, i % 2, 128, XQ * E, NQ0 + b * QPB + i)
                for t in range(T + 3):
                    if t < T:
                        g0 = (t % 2) * 3 * 512
                        dve.wait_ge(silu_ready, T * b + t + 2)
                        dve.tensor_tensor(gs[:, t, :], gs[:, t, :], PS[:, g0 + FF:g0 + 2 * FF], ALU.mult).then_inc(hh_ready, 1)
                        dve.wait_ge(hh_ready, T * b + t + 2)
                        quant_scale(dve, st, gs[:, t, :], t % 2, 128, FF, NQ0 + b * QPB + NXQ + t, divide=False)
                    if 1 <= t <= T:
                        quant_count(dve, st, (t - 1) % 2, 128, FF, NQ0 + b * QPB + NXQ + t - 1)
                    if t >= 3:
                        dve.wait_ge(dn_psum, T * b + t - 1)
                        dve.tensor_tensor(yout[:, t - 3, :], x2[:, t - 3, :], bank((t - 3) % 2, 0, E), ALU.add).then_inc(out_ready, 1)
                    if t == T:
                        norm_x(b + 1)
                st.close()

        @block.tensor
        def _(pe):
            def mm(o, l, r, start, stop, **kw):
                return pe.matmul(o, l, r, start=start, stop=stop, **kw)

            def tr(o, i):
                return pe.transpose(o, i, ident[0:i.shape[0], 0:i.shape[0]])

            pe.wait_ge(consts_loaded, 16 * 11 + 1)
            pe.sem_inc(waits_alone, 1)
            for k, (kind, parts, n, i) in enumerate(wjobs):
                pe.wait_ge(quant_out, 2 + k + 2)
                if k:
                    pe.wait_ge(qwT_ready, 2 * k + 1)
                if kind == "d":
                    for c in range(NFF):
                        w = min(128, FF - c * 128)
                        last = tr(PS[0:w, c * 128:c * 128 + 128], qw[:, k % 2, c * 128:c * 128 + w])
                else:
                    for a in range(2):
                        for c in range(2):
                            last = tr(bank(a, c * 128, c * 128 + GR), qw[0:GR, k % 2, (2 * a + c) * 128:(2 * a + c + 1) * 128])
                last.then_inc(qwT_psum, 1)
            pe.wait_ge(qwT_ready, 2 * NQ0 + 1)
            pe.wait_ge(attn_w_loaded, 16 * 4 + 1)
            pe.wait_ge(ctx_w_loaded, 16 * 6 + 1)
            pe.wait_ge(tables_ready, 7)
            pe.wait_ge(setup_pool, START_MEMSETS + 1)
            pe.wait_ge(zeros_stored, 16 * T + 1)
            with pe.Fori(0, NB) as b:
                pe.wait_ge(out_ready, T * b + 1)
                pe.sem_inc(waits_alone, 1)
                for t in range(T):
                    pe.wait_ge(xn_ready, T * b + t + 2)
                    for c in range(2):
                        i = tr(bank(c, t * 128, t * 128 + 128), xn[:, t, c * 128:(c + 1) * 128])
                        if t == T - 1:
                            i.then_inc(xnT_psum, 1)
                pe.wait_ge(xnT_ready, 2 * (b + 1) + 1)
                for q in range(2):
                    for c in range(2):
                        i = mm(bank(2 + q), wk_s[:, c, q * 128:(q + 1) * 128], xnT[:, c, :], c == 0, c == 1)
                    i.then_inc(k_psum, 1)
                for q in range(2):
                    for c in range(2):
                        i = mm(bank(4 + q), wq_s[:, c, q * 128:(q + 1) * 128], xnT[:, c, :], c == 0, c == 1)
                    i.then_inc(q_psum, 1)
                for t in range(T):
                    for c in range(2):
                        i = mm(bank(6 + t // 2, (t % 2) * E, (t % 2 + 1) * E), xnT[:, c, t * 128:(t + 1) * 128], wv_s[:, c, :],
                               c == 0, c == 1)
                    if t % 2:
                        i.then_inc(v_psum, 1)
                pe.wait_ge(qT_ready, 2 * (b + 1) + 1)
                for t in range(T):
                    if t == 1:
                        pe.wait_ge(v_ready, 2 * (b + 1) + 1)
                    if t >= 2:
                        pe.wait_ge(r_act, T * b + t)
                        pe.wait_ge(r_dve, T * b + t)
                    for c in range(2):
                        mm(bank(4 + 2 * (t % 2) + c, 0, HC * NREL), QT[:, c, t * 128:(t + 1) * 128], bdk[:], True, True)\
                            .then_inc(r_psum, 1)

                def t_ctx(i, q):
                    n, p = crows(i), q % 2
                    pe.wait_ge(caff_ready, cdone(b, i) + 1)
                    pe.wait_ge(ct_ready, cdone(b, i - 2) + 1)
                    for c in range(2):
                        ins = tr(bank(6 + p, c * 128, c * 128 + n), Kn[0:n, q, c * 128:(c + 1) * 128])
                    ins.then_inc(ct_psum, cinc(i))

                def k_ctx(i, q):
                    n, p = crows(i), q % 2
                    pe.wait_ge(ct_ready, cdone(b, i) + 1)
                    pe.wait_ge(kc_ready, cdone(b, i - 1) + 1)
                    for j in range(2):
                        for c in range(2):
                            ins = mm(bank(4 + j, parts=n), cnT[:, p, c, 0:n], cwk[:, c, j * 512:(j + 1) * 512], c == 0, c == 1)
                    ins.then_inc(ck_psum, cinc(i))

                def g_ctx(i, q):
                    n, p = crows(i), q % 2
                    pe.wait_ge(cs_ready, cdone(b, i) + 1)
                    for m in range(NM):
                        ins = mm(bank(m // 2, (m % 2) * E, (m % 2 + 1) * E), kns[0:n, q, m * 128:(m + 1) * 128], Kn[0:n, q, :],
                                 False, True, skip_group_check=True)
                    ins.then_inc(cg_done, cinc(i))

                pe.wait_ge(kT_ready, 2 * (b + 1) + 1)
                pe.wait_ge(r_act, T * (b + 1) + 1)
                pe.wait_ge(r_dve, T * (b + 1) + 1)
                for j in range(4):
                    mm(bank(j), zeros[:], right_mask[:, 0:512], True, True, skip_group_check=True)
                t_ctx(0, 0)
                t_ctx(1, 1)
                k_ctx(0, 0)
                t_ctx(2, 2)
                k_ctx(1, 1)

                def ctx_pe(i, q):
                    if exists(i + 2):
                        k_ctx(i + 2, (q + 2) % 4)
                    if exists(i + 3):
                        t_ctx(i + 3, (q + 3) % 4)
                    g_ctx(i, q)
                ctx_tiles(pe, ctx_pe)
                pe.wait_ge(g_act, 2 * (b + 1) + 1)
                pe.wait_ge(g_dve, 2 * (b + 1) + 1)
                for c in range(2):
                    for m in range(NM):
                        i = tr(bank(4 + 2 * c + m // 4, (m % 4) * 128, (m % 4 + 1) * 128), Gs[:, m, c * 128:(c + 1) * 128])
                        if m % 4 == 3:
                            i.then_inc(gt_psum, 1)
                pe.wait_ge(gt_act, 2 * (b + 1) + 1)
                pe.wait_ge(gt_dve, 2 * (b + 1) + 1)
                for m in range(NM):
                    for c in range(2):
                        i = mm(bank(m // 4, (m % 4) * 128, (m % 4 + 1) * 128), cwv[:, c, m * 128:(m + 1) * 128], GT[:, c, m, :],
                               c == 0, c == 1)
                    if m % 4 == 3:
                        i.then_inc(kvt_psum, 1)
                for m in range(NM):
                    pe.wait_ge(kvt_ready, 2 * b + m // 4 + 2)
                    i = mm(bank(2 + m // 2, (m % 2) * E, (m % 2 + 1) * E), KVT[:, m, :], cwo[:, m, :], True, True)
                    if m % 2:
                        i.then_inc(m_psum, 1)
                pe.wait_ge(m_act, 4 * (b + 1) + 1)
                pe.wait_ge(m_dve, 4 * (b + 1) + 1)
                pe.wait_ge(vcur_ready, 2 * (b + 1) + 1)
                pe.sem_inc(waits_alone, 1)
                pe.wait_ge(k_loaded, 16 * len(SLOTS_K) * (b + 1) + 1)

                def scores(t, g):
                    pe.wait_ge(q_loaded[g], 16 * len(SLOTS_Q) * (b * T + t + 1) + 1)
                    for j in range(HG):
                        h = g * HG + j
                        u = (b * T + t) * H + h
                        pe.wait_ge(scores_biased, u + 2)
                        mm(bank(j), Qp[:, h, :], Kp[:, h, :], True, True).then_inc(scores_ready, 1)

                def transpose_probs(t, h):
                    tile = b * T + t
                    pe.wait_ge(probs_ready, 4 + tile * H + h + 2)
                    pe.wait_ge(pt_copied[h % 2], tile * (H // 2) + h // 2 + 1)
                    for k in range(T):
                        i = tr(bank(4 + h % 2, k * 128, (k + 1) * 128),
                               P[:, (h // HG % 2) * HG + h % HG, PAD + k * 128:PAD + (k + 1) * 128])
                    i.then_inc(transposed, 1)

                def weigh(t, h):
                    tile = b * T + t
                    pe.wait_ge(pt_copied[h % 2], tile * (H // 2) + h // 2 + 2)
                    if h == 0:
                        pe.wait_ge(o_evac, tile + 1)
                        pe.wait_ge(vcur_moved, b * (T - 1) + t + 1)
                    g, j = divmod(h, HG)
                    for k in range(T):
                        i = mm(PS[32 * j:32 * j + HD, 6 * 512 + g * 128:6 * 512 + (g + 1) * 128],
                               Vcur[:, k, h * HD:(h + 1) * HD], PTs[:, h % 2, k * 128:(k + 1) * 128],
                               g == 0 and k == 0, True, skip_group_check=True)
                    i.then_inc(pv_done, 1)

                def attn_pe(t, last):
                    for g in range(NG):
                        if g + 1 < NG:
                            scores(t, g + 1)
                        elif not last:
                            scores(t + 1, 0)
                        for h in range(g * HG, (g + 1) * HG):
                            transpose_probs(t, h)
                            if h:
                                weigh(t, h - 1)
                    weigh(t, H - 1)

                mm(bank(6), zeros[:], right_mask[:, 0:512], True, True, skip_group_check=True)
                scores(0, 0)
                with pe.Fori(0, T - 1) as t:
                    attn_pe(t, False)
                attn_pe(T - 1, True)
                pe.wait_ge(band_loaded, 16 * T * NG * (b + 1) + 1)
                pe.wait_ge(mass_ready, 2 + T * NG * (b + 1) + 1)
                pe.wait_ge(scores_biased, 4 + T * H * (b + 1) + 1)

                def transpose_band(t):
                    if t >= 2:
                        pe.wait_ge(fa_act, T * b + t)
                        pe.wait_ge(fa_dve, 2 * (T * b + t - 1) + 1)
                    band = Pband[:, t, :, :].rearrange("p h r -> p (h r)")
                    for c in range(4):
                        i = tr(bank(2 * (t % 2), c * 128, (c + 1) * 128), band[:, c * 128:(c + 1) * 128])
                    i.then_inc(fa_psum, 1)
                    tr(bank(2 * (t % 2) + 1, 0, 128), band[:, 512:640])
                    tr(bank(2 * (t % 2) + 1, 128, 256, H), mass[:, t, :]).then_inc(fa_psum, 1)

                def weigh_band(t):
                    pe.wait_ge(fa_act, T * b + t + 2)
                    pe.wait_ge(fa_dve, 2 * (T * b + t + 1) + 1)
                    if t >= 2:
                        pe.wait_ge(attn_ready, T * b + t)
                    mm(bank(4 + t % 2, 0, E), massT[0:H, t % 2, :], bdr[:], True, True, skip_group_check=True)
                    for g in range(NG):
                        mm(bank(4 + t % 2, g * HG * HD, (g + 1) * HG * HD), OT[:, t, g * 128:(g + 1) * 128], pack[:], False, True,
                           skip_group_check=True)
                    for c in range(5):
                        i = mm(bank(4 + t % 2, 48 * c, 48 * c + 64), AT[:, t % 2, c, :], bdv[:, c, :], False, True,
                               skip_group_check=True)
                    i.then_inc(f_psum, 1)

                transpose_band(0)
                pe.wait_ge(o_evac, T * (b + 1) + 1)
                for t in range(T):
                    if t + 1 < T:
                        transpose_band(t + 1)
                    weigh_band(t)

                def project(t):
                    pe.wait_ge(aT_ready, T * b + t + 2)
                    if t >= 2:
                        pe.wait_ge(x1_ready, T * b + t)
                    for c in range(2):
                        i = mm(bank(4 + t % 2, 0, E), aT[:, t % 2, c, :], wo_s[:, c, :], c == 0, c == 1)
                    i.then_inc(wo_psum, 1)

                for t in range(T):
                    pe.wait_ge(attn_ready, T * b + t + 2)
                    if t >= 2:
                        pe.wait_ge(aT_ready, T * b + t)
                    for c in range(2):
                        i = tr(bank(6 + t % 2, c * 128, (c + 1) * 128), Oraw[:, t, c * 128:(c + 1) * 128])
                    i.then_inc(at_psum, 1)
                pe.wait_ge(attn_ready, T * (b + 1) + 1)
                for t in range(T):
                    project(t)
                for t in range(T):
                    pe.wait_ge(qz_ready, T * b + t + 2)
                    for c in range(2):
                        i = tr(bank(c, t * 128, (t + 1) * 128), Qn[:, t, c * 128:(c + 1) * 128])
                        if t == T - 1:
                            i.then_inc(qnT_psum, 1)
                pe.wait_ge(qnT_ready, 2 * (b + 1) + 1)

                def project_q(t):
                    if t >= 2:
                        pe.wait_ge(qn_ready, T * b + t)
                    for j in range(2):
                        for c in range(2):
                            i = mm(bank(2 + 2 * (t % 2) + j), QnT[:, c, t * 128:(t + 1) * 128], cwq[:, c, j * 512:(j + 1) * 512],
                                   c == 0, c == 1)
                    i.then_inc(xq_psum, 1)

                def cross(t):
                    pe.wait_ge(qn_ready, T * b + t + 2)
                    if t:
                        pe.wait_ge(qt_act, T * b + t + 1)
                        pe.wait_ge(qt_dve, T * b + t + 1)
                    for m in range(NM):
                        i = tr(bank(6 + m // 4, (m % 4) * 128, (m % 4 + 1) * 128), qn[:, t % 2, m * 128:(m + 1) * 128])
                        if m % 4 == 3:
                            i.then_inc(qt_psum, 1)
                    pe.wait_ge(qt_act, T * b + t + 2)
                    pe.wait_ge(qt_dve, T * b + t + 2)
                    if t >= 2:
                        pe.wait_ge(y_ready, T * b + t)
                    for m in range(NM):
                        i = mm(bank(t % 2, 0, E), qnT[:, m, :], M[:, m, :], m == 0, m == NM - 1)
                    i.then_inc(o_psum, 1)

                project_q(0)
                project_q(1)
                for t in range(T):
                    if t + 2 < T:
                        project_q(t + 2)
                    cross(t)
                for t in range(T):
                    pe.wait_ge(yz_ready, T * b + t + 2)
                    for c in range(2):
                        i = tr(bank(2 + c, t * 128, (t + 1) * 128), yn[:, t, c * 128:(c + 1) * 128])
                        if t == T - 1:
                            i.then_inc(ynT_psum, 1)
                pe.wait_ge(ynT_ready, 2 * (b + 1) + 1)
                for f in range(NF):
                    if f >= 4:
                        pe.wait_ge(h_ready, NF * b + f - 3 + 1)
                    for c in range(2):
                        i = mm(bank(4 + f % 4), w1[:, c, f * 128:(f + 1) * 128], ynT[:, c, :], c == 0, c == 1)
                    i.then_inc(h_psum, 1)
                pe.wait_ge(h_ready, NF * (b + 1) + 1)
                for t in range(T):
                    if t >= 2:
                        pe.wait_ge(x2_ready, T * b + t)
                    for f in range(NF):
                        i = mm(bank(t % 2, 0, E), hT[:, f, t * 128:(t + 1) * 128], w2[:, f, :], f == 0, f == NF - 1)
                    i.then_inc(m2_psum, 1)
                def transpose_xq(i):
                    pe.wait_ge(quant_out, 2 + NQ0 + b * QPB + i + 2)
                    for j in range(XQ):
                        for c in range(2):
                            ins = tr(bank(6 + i, (c * XQ + j) * 128, (c * XQ + j + 1) * 128), xq[:, XQ * i + j, c * 128:(c + 1) * 128])
                    ins.then_inc(xqT_psum, 1)

                def gate_up(t):
                    if t >= 2:
                        pe.wait_ge(hh_ready, T * b + t)
                    g0 = (t % 2) * 3 * 512
                    for w, o, lo, hi in ((wgT, 0, 0, 512), (wgT, 0, 512, FF), (wuT, FF, 0, 1024 - FF), (wuT, FF, 1024 - FF, FF)):
                        for c in range(2):
                            i = mm(PS[:, g0 + o + lo:g0 + o + hi], xqT[:, c, t * 128:(t + 1) * 128], w[:, c, lo:hi], c == 0, c == 1)
                    i.then_inc(gu_psum, 1)

                def down(t):
                    pe.wait_ge(quant_out, 2 + NQ0 + b * QPB + NXQ + t + 2)
                    for c in range(NFF):
                        w = min(128, FF - c * 128)
                        i = tr(bank(6 + c // 4, (c % 4) * 128, (c % 4 + 1) * 128, w), hq[:, t % 2, c * 128:c * 128 + w])
                    i.then_inc(ht_psum, 1)
                    pe.wait_ge(ht_ready, 3 * (T * b + t + 1) + 1)
                    if t == 0:
                        pe.wait_ge(hh_ready, T * b + 4)
                    if t >= 2:
                        pe.wait_ge(out_ready, T * b + t)
                    for c in range(NFF):
                        w = min(128, FF - c * 128)
                        i = mm(bank(t % 2, 0, E), hqT[0:w, t % 2, c, :], wdT[0:w, c, :], c == 0, c == NFF - 1)
                    i.then_inc(dn_psum, 1)

                transpose_xq(0)
                pe.wait_ge(x2_ready, T * (b + 1) + 1)
                for t in range(T):
                    if t == XQ:
                        transpose_xq(1)
                    if t % XQ == 0:
                        pe.wait_ge(xqT_ready, NXQ * b + t // XQ + 2)
                    gate_up(t)
                pe.wait_ge(xqT_ready, NXQ * (b + 1) + 1)
                for t in range(T):
                    down(t)


def _arrange(inputs):
    a = {k: np.asarray(v) for k, v in inputs.items()}
    f = np.float32

    def halves(w):
        return np.ascontiguousarray(w.reshape(-1, 128, w.shape[1]).transpose(1, 0, 2))

    d = {"x": np.concatenate([a["x"], np.zeros((1, S, E), f)]), "ctx": a["ctx_1024"]}
    d["wq"], d["wk"] = halves(a["L0_attn_Wq"].T), halves(a["L0_attn_Wk"].T)
    d["wv"], d["wo"] = halves(a["L0_attn_Wv"].T), halves(a["L0_attn_Wo"].T)
    d["cwq"], d["cwk"], d["cwv"] = (halves(a["L0_xattn_" + n]) for n in ("wq", "wk", "wv"))
    d["cwo"], d["w1"], d["w2"] = (halves(a["L0_xattn_" + n]) for n in ("wo", "w1", "w2"))
    for n, w in (("w_gate", a["L0_ffn_w_gate"]), ("w_up", a["L0_ffn_w_up"])):
        d[n] = np.ascontiguousarray(w.reshape(NGR, GR, E).transpose(1, 0, 2))
    d["w_down"] = halves(a["L0_ffn_w_down"])
    rk, rv = a["L0_attn_rel_k"], a["L0_attn_rel_v"]
    vecs = [a["L0_attn_bv"], a["L0_attn_bo"], a["L0_xattn_ln1_g"], a["L0_xattn_ln1_b"], a["L0_xattn_bo"],
            a["L0_xattn_b2"], np.tile(rv[BAND], H)]
    d["rows"] = np.ascontiguousarray(np.broadcast_to(np.stack(vecs)[None], (128, 7, E)))
    d["cols"] = np.concatenate([a["L0_attn_bq"].reshape(2, 128).T, a["L0_attn_bk"].reshape(2, 128).T,
                                a["L0_xattn_b1"].reshape(8, 128).T]
                               + [a["L0_xattn_" + n].reshape(2, 128).T for n in ("ln1_g", "ln1_b", "ln2_g", "ln2_b")], axis=1)

    def tables(kt, vt):
        bk = np.zeros((128, HC, NREL), f)
        for j in range(HC):
            bk[j * HD:(j + 1) * HD, j, :] = kt.T
        bv = np.zeros((H, BAND, H, HD), f)
        br = np.zeros((H, H, HD), f)
        for h in range(H):
            bv[h, :, h, :] = vt[0:BAND]
            br[h, h, :] = vt[BAND]
        bv = bv.reshape(5, 128, E)
        bv = np.stack([bv[c][:, 48 * c:48 * c + 64] for c in range(5)], axis=1)
        return bk.reshape(128, HC * NREL), bv, br.reshape(H, E)

    d["bdk"], d["bdv"], d["bdr"] = tables(rk, rv)
    k0, v0, r0 = tables(np.broadcast_to(rk[0:1], rk.shape), np.broadcast_to(rv[0:1], rv.shape))
    rel0 = np.zeros((128, TAB0), f)
    o = HC * NREL
    rel0[:, 0:o] = k0
    rel0[:, o:o + 320] = v0.reshape(128, 320)
    rel0[0:H, o + 320:o + 320 + E] = r0
    rel0[:, o + 320 + E:o + 320 + 2 * E] = np.tile(rv[0], H)
    d["rel0"] = rel0
    p = np.arange(128)[:, None]
    d["ident"] = np.eye(128, dtype=f)
    d["right_mask"] = (np.arange(384 + S)[None] - 384 >= p + MAX_REL).astype(f)
    c = np.arange(128)[None] + MAX_REL
    right = (c >= p + MAX_REL).astype(f)
    d["mass_mask"] = np.where(c < 128, right, right - 1).astype(f)
    d["pack"] = ((p // 32 == np.arange(HG * HD)[None] // HD) & (p % 32 == np.arange(HG * HD)[None] % HD)).astype(f)
    d["pair_mask"] = (np.arange(128)[None] // XD == p // XD).astype(f)
    return {k: np.ascontiguousarray(v) for k, v in d.items()}


def kernel(**inputs):
    import concourse.bacc as bacc
    import concourse.bass as bass
    from concourse import mybir
    from concourse.bass_utils import run_bass_kernel_spmd

    nc = bacc.Bacc("TRN2", target_bir_lowering=False, num_devices=1)
    arrays = _arrange(inputs)
    d = {k: nc.dram_tensor("in_" + k, v.shape, mybir.dt.from_np(v.dtype), kind="ExternalInput").ap() for k, v in arrays.items()}
    for k in ("bias_scr", "prob_scr"):
        d[k] = nc.dram_tensor(k, [T, H, REGION], mybir.dt.float32, kind="Internal").ap()
    for k in ("q_scr", "k_scr"):
        d[k] = nc.dram_tensor(k, [PARTS, E, S], mybir.dt.bfloat16, kind="Internal").ap()
    out = nc.dram_tensor("out", [NB, S, E], mybir.dt.float32, kind="ExternalOutput").ap()
    build(nc, bass, mybir, d, out)
    r = run_bass_kernel_spmd(nc, [{"in_" + k: v for k, v in arrays.items()}], core_ids=[0])
    return r.results[0]["out"]
```
